# Optimizing a Trainium2 kernel written in Bass

```python
import numpy as np
import jax
import jax.numpy as jnp

def _softmax(x, axis=-1):
    return jax.nn.softmax(x, axis=axis)

def _gelu(x):
    return jax.nn.gelu(x, approximate=True)

def _silu(x):
    return jax.nn.silu(x)

def _sigmoid(x):
    return jax.nn.sigmoid(x)

def _layernorm(x, axis=-1, eps=1e-05):
    m = jnp.mean(x, axis=axis, keepdims=True)
    v = jnp.var(x, axis=axis, keepdims=True)
    return (x - m) / jnp.sqrt(v + eps)

def _scatter_add(tgt, idx, src, axis=0):
    return tgt.at[idx].add(src)

def _segment_sum(src, seg, n):
    return jax.ops.segment_sum(src, seg, n)
kernel_name = 'mk_early_fusion_embed_d1_tok_img256_r4_47d7b4'

def setup_inputs(seed: int=0):
    np.random.seed(seed)
    _w = jnp.asarray

    def _rec_inputs():
        import jax
        import jax.numpy as jnp
        _rk = jax.random.key(seed)
        x = -7.10856e-05 + 0.999911 * jax.random.normal(jax.random.fold_in(_rk, 1), (8, 64, 128, 64), jnp.float32)
        x_txt = jax.random.randint(jax.random.fold_in(_rk, 51), (8, 77), 0, 2048, jnp.int32)
        return (x, x_txt)
    x, x_txt = _rec_inputs()

    def _L0_tok_setup():
        import jax, jax.numpy as jnp
        import numpy as np
        PATCH_LEN = 16
        STRIDE = 8
        PAD = 8
        key = jax.random.key(seed)
        k1, k2 = jax.random.split(key)
        x = jax.random.normal(k1, (32, 64, 128, 64), dtype=jnp.float32)
        in_feat = 64 * (PATCH_LEN // 2 + 1) * 2
        W = jax.random.normal(k2, (64, in_feat), dtype=jnp.float32) * 0.02
        return {'x': x, 'W': W}
    _L0_tok_all = _L0_tok_setup()
    _L0_tok_in = {k: v for k, v in _L0_tok_all.items() if k in ('W',)}
    del _L0_tok_all

    def _L0_txt_setup():
        import jax, jax.numpy as jnp
        import numpy as np
        D = 64
        NLEAF = 8
        N_INTERNAL = 7
        N_STRUCT = 2048
        COMP_V = 256
        OP_V = 64
        EPS = 1e-05

        def _layer_norm(x, gamma, beta):
            mu = jnp.mean(x, axis=-1, keepdims=True)
            var = jnp.mean(jnp.square(x - mu), axis=-1, keepdims=True)
            return (x - mu) * jax.lax.rsqrt(var + EPS) * gamma + beta
        key = jax.random.key(seed)
        ks = jax.random.split(key, 8)
        struct_indices = jax.random.randint(ks[0], (32, 512), 0, N_STRUCT)
        leaf_ids = jax.random.randint(ks[1], (N_STRUCT, NLEAF), 0, COMP_V).astype(jnp.int32)
        op_ids = jax.random.randint(ks[2], (N_STRUCT, N_INTERNAL), 0, OP_V).astype(jnp.int32)
        comp_emb = jax.random.normal(ks[3], (COMP_V, D), dtype=jnp.float32)
        op_emb = jax.random.normal(ks[4], (OP_V, D), dtype=jnp.float32)
        W_bin = jax.random.normal(ks[5], (3 * D, D), dtype=jnp.float32) / np.sqrt(3 * D)
        b_bin = jnp.zeros((D,), dtype=jnp.float32)
        gamma = jnp.ones((D,), dtype=jnp.float32)
        beta = jnp.zeros((D,), dtype=jnp.float32)
        return {'struct_indices': struct_indices, 'leaf_ids': leaf_ids, 'op_ids': op_ids, 'comp_emb': comp_emb, 'op_emb': op_emb, 'W_bin': W_bin, 'b_bin': b_bin, 'gamma': gamma, 'beta': beta}
    _L0_txt_all = _L0_txt_setup()
    _L0_txt_in = {k: v for k, v in _L0_txt_all.items() if k in ('leaf_ids', 'op_ids', 'comp_emb', 'op_emb', 'W_bin', 'b_bin', 'gamma', 'beta')}
    del _L0_txt_all

    def _L0_attn_setup():
        import jax, jax.numpy as jnp
        import numpy as np
        B_SZ, L_SEQ, H_CH, N_ST = (8, 1024, 64, 64)

        def _dplr_kernel(Lambda_re, Lambda_im, P_re, P_im, Q_re, Q_im, B_re, B_im, C_re, C_im, step, L):
            Lam = (Lambda_re + 1j * Lambda_im).astype(jnp.complex64)
            Pc = (P_re + 1j * P_im).astype(jnp.complex64)
            Qc = (Q_re + 1j * Q_im).astype(jnp.complex64)
            Bc = (B_re + 1j * B_im).astype(jnp.complex64)
            Cc = (C_re + 1j * C_im).astype(jnp.complex64)
            k = jnp.arange(L, dtype=jnp.float32)
            Omega = jnp.exp(-2j * jnp.pi * (k / L)).astype(jnp.complex64)
            c = 2.0 / (1.0 + Omega)
            g = 2.0 / step[0] * (1.0 - Omega) / (1.0 + Omega)
            inv = 1.0 / (g[:, None] - Lam[None, :])
            k00 = jnp.einsum('hn,ln->hl', Cc * Bc[None, :], inv)
            k01 = jnp.einsum('hn,ln->hl', Cc * Pc[None, :], inv)
            k10 = jnp.einsum('n,ln->l', Qc * Bc, inv)
            k11 = jnp.einsum('n,ln->l', Qc * Pc, inv)
            atRoots = c[None, :] * (k00 - k01 * (k10 / (1.0 + k11))[None, :])
            K = jnp.fft.ifft(atRoots, axis=-1).real
            return K.astype(jnp.float32)

        def _reference_tuple_inner(x, Lambda_re, Lambda_im, P_re, P_im, Q_re, Q_im, B_re, B_im, C_re, C_im, step, D, W_fc, b_fc, ln_g, ln_b):
            Bsz, L, H = x.shape
            step = jnp.maximum(step, 1e-06)
            K = _dplr_kernel(Lambda_re, Lambda_im, P_re, P_im, Q_re, Q_im, B_re, B_im, C_re, C_im, step, L)
            n = 2 * L
            Kf = jnp.fft.rfft(K, n=n, axis=-1)
            uf = jnp.fft.rfft(x, n=n, axis=1)
            h1 = jnp.fft.irfft(uf * Kf.T[None], n=n, axis=1)[:, :L, :]
            y1 = jax.nn.gelu(h1 + D * x, approximate=False)
            y2 = jax.nn.gelu(y1 @ W_fc.T + b_fc, approximate=False)
            y2 = y2 + x
            mu = jnp.mean(y2, axis=-1, keepdims=True)
            var = jnp.var(y2, axis=-1, keepdims=True)
            y = (y2 - mu) / jnp.sqrt(var + 1e-05) * ln_g + ln_b
            h_ratio = jnp.max(jnp.abs(y), axis=1) / (jnp.max(jnp.abs(x), axis=1) + 1e-06)
            return (y, h_ratio)
        key = jax.random.key(seed)
        ks = jax.random.split(key, 12)
        rn = lambda k, s, sc=1.0: jax.random.normal(k, s, jnp.float32) * sc
        inp = {'x': rn(ks[0], (B_SZ, L_SEQ, H_CH)), 'Lambda_re': -(jnp.abs(rn(ks[1], (N_ST,))) + 0.1), 'Lambda_im': jnp.pi * jnp.arange(N_ST, dtype=jnp.float32), 'P_re': rn(ks[2], (N_ST,), N_ST ** (-0.5)), 'P_im': rn(ks[3], (N_ST,), N_ST ** (-0.5)), 'Q_re': rn(ks[4], (N_ST,), N_ST ** (-0.5)), 'Q_im': rn(ks[5], (N_ST,), N_ST ** (-0.5)), 'B_re': rn(ks[6], (N_ST,), N_ST ** (-0.5)), 'B_im': rn(ks[7], (N_ST,), N_ST ** (-0.5)), 'C_re': rn(ks[8], (H_CH, N_ST), N_ST ** (-0.5)), 'C_im': rn(ks[9], (H_CH, N_ST), N_ST ** (-0.5)), 'step': jnp.ones((1,), jnp.float32) * 0.001, 'D': jnp.zeros((1,), jnp.float32), 'W_fc': rn(ks[10], (H_CH, H_CH), H_CH ** (-0.5)), 'b_fc': jnp.zeros((H_CH,), jnp.float32), 'ln_g': jnp.ones((H_CH,), jnp.float32), 'ln_b': jnp.zeros((H_CH,), jnp.float32)}
        return inp
    _L0_attn_all = _L0_attn_setup()
    _L0_attn_in = {k: v for k, v in _L0_attn_all.items() if k in ('Lambda_re', 'Lambda_im', 'P_re', 'P_im', 'Q_re', 'Q_im', 'B_re', 'B_im', 'C_re', 'C_im', 'step', 'D', 'W_fc', 'b_fc', 'ln_g', 'ln_b')}
    del _L0_attn_all

    def _L0_ffn_setup():
        import jax, jax.numpy as jnp
        import numpy as np
        B, S, H, NH, NE = (4, 256, 64, 4, 4)
        D = H // NH
        EPS = 1e-08

        def layernorm(x, g, b):
            m = jnp.mean(x, axis=-1, keepdims=True)
            v = jnp.mean((x - m) ** 2, axis=-1, keepdims=True)
            return (x - m) / jnp.sqrt(v + EPS) * g + b
        key = jax.random.key(seed)
        ks = jax.random.split(key, 18)
        sc = 0.05
        return {'x': jax.random.normal(ks[0], (B, S, H), jnp.float32), 'hl_w': jax.random.normal(ks[1], (NH, D, H), jnp.float32) * sc, 'hl_b': jax.random.normal(ks[2], (NH, D), jnp.float32) * sc, 'wq': jax.random.normal(ks[3], (NH, NE, D, D), jnp.float32) * sc, 'wk': jax.random.normal(ks[4], (NH, D, D), jnp.float32) * sc, 'wv': jax.random.normal(ks[5], (NH, D, D), jnp.float32) * sc, 'gate_w': jax.random.normal(ks[6], (NH, NE, NE * D), jnp.float32) * sc, 'gate_b': jax.random.normal(ks[7], (NH, NE), jnp.float32) * sc, 'ln_g': jnp.ones((D,), jnp.float32), 'ln_b': jnp.zeros((D,), jnp.float32), 'fc1_w': jax.random.normal(ks[8], (D, D), jnp.float32) * sc, 'fc1_b': jax.random.normal(ks[9], (D,), jnp.float32) * sc, 'fc2_w': jax.random.normal(ks[10], (D, D), jnp.float32) * sc, 'fc2_b': jax.random.normal(ks[11], (D,), jnp.float32) * sc, 'fnorm_g': jnp.ones((D,), jnp.float32), 'fnorm_b': jnp.zeros((D,), jnp.float32), 'fgate_w': jax.random.normal(ks[12], (NH, H), jnp.float32) * sc}
    _L0_ffn_all = _L0_ffn_setup()
    _L0_ffn_in = {k: v for k, v in _L0_ffn_all.items() if k in ('hl_w', 'hl_b', 'wq', 'wk', 'wv', 'gate_w', 'gate_b', 'ln_g', 'ln_b', 'fc1_w', 'fc1_b', 'fc2_w', 'fc2_b', 'fnorm_g', 'fnorm_b', 'fgate_w')}
    del _L0_ffn_all
    return {'x': x, 'x_txt': x_txt, 'L0_tok_W': _L0_tok_in['W'], 'L0_txt_leaf_ids': _L0_txt_in['leaf_ids'], 'L0_txt_op_ids': _L0_txt_in['op_ids'], 'L0_txt_comp_emb': _L0_txt_in['comp_emb'], 'L0_txt_op_emb': _L0_txt_in['op_emb'], 'L0_txt_W_bin': _L0_txt_in['W_bin'], 'L0_txt_b_bin': _L0_txt_in['b_bin'], 'L0_txt_gamma': _L0_txt_in['gamma'], 'L0_txt_beta': _L0_txt_in['beta'], 'L0_attn_Lambda_re': _L0_attn_in['Lambda_re'], 'L0_attn_Lambda_im': _L0_attn_in['Lambda_im'], 'L0_attn_P_re': _L0_attn_in['P_re'], 'L0_attn_P_im': _L0_attn_in['P_im'], 'L0_attn_Q_re': _L0_attn_in['Q_re'], 'L0_attn_Q_im': _L0_attn_in['Q_im'], 'L0_attn_B_re': _L0_attn_in['B_re'], 'L0_attn_B_im': _L0_attn_in['B_im'], 'L0_attn_C_re': _L0_attn_in['C_re'], 'L0_attn_C_im': _L0_attn_in['C_im'], 'L0_attn_step': _L0_attn_in['step'], 'L0_attn_D': _L0_attn_in['D'], 'L0_attn_W_fc': _L0_attn_in['W_fc'], 'L0_attn_b_fc': _L0_attn_in['b_fc'], 'L0_attn_ln_g': _L0_attn_in['ln_g'], 'L0_attn_ln_b': _L0_attn_in['ln_b'], 'L0_ffn_hl_w': _L0_ffn_in['hl_w'], 'L0_ffn_hl_b': _L0_ffn_in['hl_b'], 'L0_ffn_wq': _L0_ffn_in['wq'], 'L0_ffn_wk': _L0_ffn_in['wk'], 'L0_ffn_wv': _L0_ffn_in['wv'], 'L0_ffn_gate_w': _L0_ffn_in['gate_w'], 'L0_ffn_gate_b': _L0_ffn_in['gate_b'], 'L0_ffn_ln_g': _L0_ffn_in['ln_g'], 'L0_ffn_ln_b': _L0_ffn_in['ln_b'], 'L0_ffn_fc1_w': _L0_ffn_in['fc1_w'], 'L0_ffn_fc1_b': _L0_ffn_in['fc1_b'], 'L0_ffn_fc2_w': _L0_ffn_in['fc2_w'], 'L0_ffn_fc2_b': _L0_ffn_in['fc2_b'], 'L0_ffn_fnorm_g': _L0_ffn_in['fnorm_g'], 'L0_ffn_fnorm_b': _L0_ffn_in['fnorm_b'], 'L0_ffn_fgate_w': _L0_ffn_in['fgate_w']}

def reference(x, x_txt, L0_tok_W, L0_txt_leaf_ids, L0_txt_op_ids, L0_txt_comp_emb, L0_txt_op_emb, L0_txt_W_bin, L0_txt_b_bin, L0_txt_gamma, L0_txt_beta, L0_attn_Lambda_re, L0_attn_Lambda_im, L0_attn_P_re, L0_attn_P_im, L0_attn_Q_re, L0_attn_Q_im, L0_attn_B_re, L0_attn_B_im, L0_attn_C_re, L0_attn_C_im, L0_attn_step, L0_attn_D, L0_attn_W_fc, L0_attn_b_fc, L0_attn_ln_g, L0_attn_ln_b, L0_ffn_hl_w, L0_ffn_hl_b, L0_ffn_wq, L0_ffn_wk, L0_ffn_wv, L0_ffn_gate_w, L0_ffn_gate_b, L0_ffn_ln_g, L0_ffn_ln_b, L0_ffn_fc1_w, L0_ffn_fc1_b, L0_ffn_fc2_w, L0_ffn_fc2_b, L0_ffn_fnorm_g, L0_ffn_fnorm_b, L0_ffn_fgate_w):
    import jax
    import jax.numpy as jnp

    def _L0_tok_ref(x, W):
        import jax, jax.numpy as jnp
        import numpy as np
        PATCH_LEN = 16
        STRIDE = 8
        PAD = 8
        B, C, T, V = x.shape
        xp = jnp.pad(x, ((0, 0), (0, 0), (0, PAD), (0, 0)), mode='edge')
        Tp = T + PAD
        N = (Tp - PATCH_LEN) // STRIDE + 1
        idx = jnp.arange(N)[:, None] * STRIDE + jnp.arange(PATCH_LEN)[None, :]
        patches = xp[:, :, idx, :]
        patches = jnp.transpose(patches, (0, 4, 2, 3, 1))
        xf = jnp.fft.rfft(patches, axis=-2, norm='ortho')
        F = xf.shape[-2]
        x_real = xf.real.reshape(B, V, N, F * C)
        x_imag = xf.imag.reshape(B, V, N, F * C)
        x_emb = jnp.concatenate([x_real, x_imag], axis=-1)
        x_emb = x_emb @ W.T
        return x_emb.reshape(B, V * N, -1)

    def _L0_txt_ref(struct_indices, leaf_ids, op_ids, comp_emb, op_emb, W_bin, b_bin, gamma, beta):
        import jax, jax.numpy as jnp
        import numpy as np
        D = 64
        NLEAF = 8
        N_INTERNAL = 7
        N_STRUCT = 2048
        COMP_V = 256
        OP_V = 64
        EPS = 1e-05

        def _layer_norm(x, gamma, beta):
            mu = jnp.mean(x, axis=-1, keepdims=True)
            var = jnp.mean(jnp.square(x - mu), axis=-1, keepdims=True)
            return (x - mu) * jax.lax.rsqrt(var + EPS) * gamma + beta
        h = _layer_norm(comp_emb[leaf_ids], gamma, beta)
        off = 0
        while h.shape[1] > 1:
            n = h.shape[1] // 2
            ops = op_emb[op_ids[:, off:off + n]]
            cat = jnp.concatenate([ops, h[:, 0::2], h[:, 1::2]], axis=-1)
            h = _layer_norm(jnp.einsum('nkc,cd->nkd', cat, W_bin) + b_bin, gamma, beta)
            off += n
        root = h[:, 0]
        out = root[struct_indices]
        mask = (struct_indices > 1)[..., None]
        return jnp.where(mask, out, jnp.zeros((), dtype=out.dtype))

    def _L0_attn_ref(x, Lambda_re, Lambda_im, P_re, P_im, Q_re, Q_im, B_re, B_im, C_re, C_im, step, D, W_fc, b_fc, ln_g, ln_b):
        import jax, jax.numpy as jnp
        import numpy as np
        B_SZ, L_SEQ, H_CH, N_ST = (8, 1024, 64, 64)

        def _dplr_kernel(Lambda_re, Lambda_im, P_re, P_im, Q_re, Q_im, B_re, B_im, C_re, C_im, step, L):
            Lam = (Lambda_re + 1j * Lambda_im).astype(jnp.complex64)
            Pc = (P_re + 1j * P_im).astype(jnp.complex64)
            Qc = (Q_re + 1j * Q_im).astype(jnp.complex64)
            Bc = (B_re + 1j * B_im).astype(jnp.complex64)
            Cc = (C_re + 1j * C_im).astype(jnp.complex64)
            k = jnp.arange(L, dtype=jnp.float32)
            Omega = jnp.exp(-2j * jnp.pi * (k / L)).astype(jnp.complex64)
            c = 2.0 / (1.0 + Omega)
            g = 2.0 / step[0] * (1.0 - Omega) / (1.0 + Omega)
            inv = 1.0 / (g[:, None] - Lam[None, :])
            k00 = jnp.einsum('hn,ln->hl', Cc * Bc[None, :], inv)
            k01 = jnp.einsum('hn,ln->hl', Cc * Pc[None, :], inv)
            k10 = jnp.einsum('n,ln->l', Qc * Bc, inv)
            k11 = jnp.einsum('n,ln->l', Qc * Pc, inv)
            atRoots = c[None, :] * (k00 - k01 * (k10 / (1.0 + k11))[None, :])
            K = jnp.fft.ifft(atRoots, axis=-1).real
            return K.astype(jnp.float32)

        def _reference_tuple_inner(x, Lambda_re, Lambda_im, P_re, P_im, Q_re, Q_im, B_re, B_im, C_re, C_im, step, D, W_fc, b_fc, ln_g, ln_b):
            Bsz, L, H = x.shape
            step = jnp.maximum(step, 1e-06)
            K = _dplr_kernel(Lambda_re, Lambda_im, P_re, P_im, Q_re, Q_im, B_re, B_im, C_re, C_im, step, L)
            n = 2 * L
            Kf = jnp.fft.rfft(K, n=n, axis=-1)
            uf = jnp.fft.rfft(x, n=n, axis=1)
            h1 = jnp.fft.irfft(uf * Kf.T[None], n=n, axis=1)[:, :L, :]
            y1 = jax.nn.gelu(h1 + D * x, approximate=False)
            y2 = jax.nn.gelu(y1 @ W_fc.T + b_fc, approximate=False)
            y2 = y2 + x
            mu = jnp.mean(y2, axis=-1, keepdims=True)
            var = jnp.var(y2, axis=-1, keepdims=True)
            y = (y2 - mu) / jnp.sqrt(var + 1e-05) * ln_g + ln_b
            h_ratio = jnp.max(jnp.abs(y), axis=1) / (jnp.max(jnp.abs(x), axis=1) + 1e-06)
            return (y, h_ratio)
        return _reference_tuple_inner(x, Lambda_re, Lambda_im, P_re, P_im, Q_re, Q_im, B_re, B_im, C_re, C_im, step, D, W_fc, b_fc, ln_g, ln_b)[0]

    def _L0_ffn_ref(x, hl_w, hl_b, wq, wk, wv, gate_w, gate_b, ln_g, ln_b, fc1_w, fc1_b, fc2_w, fc2_b, fnorm_g, fnorm_b, fgate_w):
        import jax, jax.numpy as jnp
        import numpy as np
        B, S, H, NH, NE = (4, 256, 64, 4, 4)
        D = H // NH
        EPS = 1e-08

        def layernorm(x, g, b):
            m = jnp.mean(x, axis=-1, keepdims=True)
            v = jnp.mean((x - m) ** 2, axis=-1, keepdims=True)
            return (x - m) / jnp.sqrt(v + EPS) * g + b
        b, s, h = x.shape
        nh, d, _ = wk.shape
        ne = wq.shape[1]
        sx = jnp.einsum('bsh,ndh->bnsd', x, hl_w) + hl_b[None, :, None, :]
        pad = sx == 0
        q = jnp.einsum('bnsd,neod->bneso', sx, wq)
        k = jnp.einsum('bnsd,nod->bnso', sx, wk)
        v = jnp.einsum('bnsd,nod->bnso', sx, wv)
        causal = jnp.where(jnp.tril(jnp.ones((s, s), bool)), 0.0, -jnp.inf).astype(x.dtype)
        scores = jnp.einsum('bnesd,bntd->bnest', q, k) * d ** 0.5 + causal
        att = jax.nn.softmax(scores, axis=-1)
        qkv = jnp.einsum('bnest,bntd->bnesd', att, v)
        qkv = jnp.where(pad[:, :, None], 0.0, qkv)
        out = jnp.transpose(qkv, (0, 1, 3, 2, 4)).reshape(b, nh, s, ne * d)
        gs = jax.nn.softmax(jnp.einsum('bnsf,nef->bnse', out, gate_w) + gate_b[None, :, None, :], axis=-1)
        mixed = jnp.einsum('bnsed,bnse->bnsd', out.reshape(b, nh, s, ne, d), gs)
        resid = sx[jnp.arange(nh), jnp.arange(nh)]
        hn = layernorm(mixed + resid, ln_g, ln_b)
        f_n = jnp.transpose(hn, (0, 2, 1, 3)).reshape(b, s, h)
        fx = f_n.reshape(b, s, nh, d)
        pm = fx == 0
        hx = jnp.where(pm, 0.0, fx @ fc1_w.T + fc1_b)
        hx = jax.nn.relu(hx)
        hx = jnp.where(pm, 0.0, hx @ fc2_w.T + fc2_b)
        hx = layernorm(hx + fx, fnorm_g, fnorm_b)
        fout = hx.reshape(b, s, h)
        fg = jax.nn.softmax(fout @ fgate_w.T, axis=-1)
        return (fout.reshape(b, s, nh, d) * fg[..., None]).reshape(b, s, h)
    h = _L0_tok_ref(x, L0_tok_W)
    h = jnp.concatenate([h, _L0_txt_ref(x_txt, L0_txt_leaf_ids, L0_txt_op_ids, L0_txt_comp_emb, L0_txt_op_emb, L0_txt_W_bin, L0_txt_b_bin, L0_txt_gamma, L0_txt_beta)], axis=1)
    h = h + _L0_attn_ref(_layernorm(h, axis=-1), L0_attn_Lambda_re, L0_attn_Lambda_im, L0_attn_P_re, L0_attn_P_im, L0_attn_Q_re, L0_attn_Q_im, L0_attn_B_re, L0_attn_B_im, L0_attn_C_re, L0_attn_C_im, L0_attn_step, L0_attn_D, L0_attn_W_fc, L0_attn_b_fc, L0_attn_ln_g, L0_attn_ln_b)
    h = h + _L0_ffn_ref(_layernorm(h, axis=-1), L0_ffn_hl_w, L0_ffn_hl_b, L0_ffn_wq, L0_ffn_wk, L0_ffn_wv, L0_ffn_gate_w, L0_ffn_gate_b, L0_ffn_ln_g, L0_ffn_ln_b, L0_ffn_fc1_w, L0_ffn_fc1_b, L0_ffn_fc2_w, L0_ffn_fc2_b, L0_ffn_fnorm_g, L0_ffn_fnorm_b, L0_ffn_fgate_w)
    return h

_drawn_inputs = setup_inputs


def setup_inputs(seed=0):
    import zlib

    import numpy as np

    out = dict(_drawn_inputs(seed))
    spreads = {'L0_txt_b_bin': (0.0, 0.1),
     'L0_txt_gamma': (1.0, 0.2),
     'L0_txt_beta': (0.0, 0.1),
     'L0_attn_b_fc': (0.0, 0.1),
     'L0_attn_ln_g': (1.0, 0.2),
     'L0_attn_ln_b': (0.0, 0.1),
     'L0_ffn_ln_g': (1.0, 0.536),
     'L0_ffn_ln_b': (0.0, 0.515),
     'L0_ffn_fnorm_g': (1.0, 0.2),
     'L0_ffn_fnorm_b': (0.0, 0.497)}
    factors = {'L0_attn_Lambda_re': 8.0,
     'L0_attn_Lambda_im': 8.0,
     'L0_attn_P_re': 8.0,
     'L0_attn_P_im': 8.0,
     'L0_attn_Q_re': 8.0,
     'L0_attn_Q_im': 8.0,
     'L0_attn_B_re': 8.0,
     'L0_attn_B_im': 8.0,
     'L0_attn_C_re': 8.0,
     'L0_attn_C_im': 8.0,
     'L0_attn_W_fc': 8.0,
     'L0_ffn_wq': 8.0,
     'L0_ffn_wk': 8.0,
     'L0_ffn_wv': 8.0,
     'L0_ffn_gate_w': 8.0,
     'L0_ffn_gate_b': 8.0,
     'L0_ffn_fc1_w': 8.0,
     'L0_ffn_fc1_b': 8.0,
     'L0_ffn_fc2_w': 8.0,
     'L0_ffn_fc2_b': 4.737}
    for name, (base, spread) in spreads.items():
        noise = np.random.default_rng([zlib.crc32(name.encode()), seed]).standard_normal(out[name].shape)
        drawn = base * np.exp(spread * noise) if base else spread * noise
        out[name] = jnp.asarray(drawn.astype(out[name].dtype))
    for name, factor in factors.items():
        out[name] = (out[name] * factor).astype(out[name].dtype)
    return out
```

```python
from contextlib import ExitStack

import numpy as np
import concourse.bass as bass
from concourse import mybir

F32 = mybir.dt.float32
BF16 = mybir.dt.bfloat16
I32 = mybir.dt.int32
ACT = mybir.ActivationFunctionType
ALU = mybir.AluOpType
AX = mybir.AxisListType
RMAX = bass.bass_isa.ReduceOp.max

P = 128
B, C, T, V = 8, 64, 128, 64
D = 64
PATCH, STRIDE = 16, 8
NP = (T + STRIDE - PATCH) // STRIDE + 1
F = PATCH // 2 + 1
TXT = 77
IMG = V * NP
L = IMG + TXT
NA = -(-L // P)
LP = NA * P
VOCAB, NOPS = 256, 64
NLEAF, NOP = 8, 7
EPS = 1e-5


def bcast(ap, n):
    return bass.AP(ap.tensor, ap.offset, [*[list(x) for x in ap.ap], [0, n]])


def bmid(ap, n):
    a = [list(x) for x in ap.ap]
    return bass.AP(ap.tensor, ap.offset, [*a[:-1], [0, n], a[-1]])


def rows(ap, n):
    return bass.AP(ap.tensor, ap.offset, [[0, n], *[list(x) for x in ap.ap]])


class Chain:

    def __init__(self, eng, sem, base=0):
        self.eng, self.sem, self.base, self.n = eng, sem, base, 0

    def done(self, ins):
        ins.then_inc(self.sem, 1)
        self.n += 1
        return self.n

    def wait(self, n=None):
        self.eng.wait_ge(self.sem, self.base + (self.n if n is None else n))

    def step(self, ins):
        self.done(ins)
        self.wait()


def stage_embed(nc, t, h1d):
    KB = PATCH * C // P // 2
    with ExitStack() as ctx:
        sb = lambda n, s, d=F32: ctx.enter_context(nc.sbuf_tensor(n, s, d))
        ps = lambda n, s: ctx.enter_context(nc.psum_tensor(n, s, F32))
        sem = lambda n: ctx.enter_context(nc.semaphore(n))
        wf = sb("wf", [2 * F, D, 2, C])
        dft = sb("dft", [2 * F, PATCH])
        g = sb("g", [P, KB, 2, D])
        ident = sb("ident", [P, P])
        fold = sb("fold", [P, D])
        x = sb("x", [P, 2, NP, KB * V])
        xe = sb("xe", [P, B, V])
        ye = sb("ye", [P, B, V])
        y = sb("y", [P, 2, V, NP])
        h = sb("h", [P, NA, B, D])
        comp = sb("comp", [P, 2, D])
        compc = sb("compc", [P, 2, D])
        compq = sb("compq", [P, 2, D])
        compt = sb("compt", [D, 2, P])
        opemb = sb("opemb", [NOPS, D])
        opt = sb("opt", [D, NOPS])
        w0 = sb("w0", [D, D])
        wlr = sb("wlr", [D, 2, D])
        w12 = sb("w12", [P, D])
        bb = sb("bb", [P, D])
        gam = sb("gam", [P, D])
        bet = sb("bet", [P, D])
        tlr = sb("tlr", [P, 2, 2, D])
        top = sb("top", [NOPS, D])
        ids = sb("ids", [TXT, B], I32)
        idf = sb("idf", [TXT, B])
        keep = sb("keep", [TXT, B])
        leaf = sb("leaf", [TXT, B, NLEAF], I32)
        opi = sb("opi", [TXT, B, NOP], I32)
        gl = sb("gl", [TXT, B, 4, D])
        gr = sb("gr", [TXT, B, 4, D])
        go = sb("go", [TXT, B, NOP, D])
        tx = sb("tx", [TXT, 32, D])
        tq = sb("tq", [TXT, 32, D])
        tt = sb("tt", [P, 16, TXT])
        st = sb("st", [P, 4, 32])
        mhalf = sb("mhalf", [P, 32])
        tl_d = nc.dram_tensor("tl_d", [VOCAB, D], F32).ap()
        tr_d = nc.dram_tensor("tr_d", [VOCAB, D], F32).ap()
        to_d = nc.dram_tensor("to_d", [NOPS, D], F32).ap()
        psy = ps("psy", [P, 2, 2, 512])
        pst = ps("pst", [P, 2, 512])
        psw = ps("psw", [P, 2, 512])

        s_w, s_txt, s_e, s_id = sem("weights_loaded"), sem("text_loaded"), sem("edges_loaded"), sem("ids_loaded")
        s_x = [sem("x0_loaded"), sem("x1_loaded")]
        g_ready, g_copied = sem("g_ready"), sem("g_copied")
        y_done = [sem("y0_done"), sem("y1_done")]
        lo_out = [sem("y0_low_copied"), sem("y1_low_copied")]
        hi_out = [sem("y0_high_copied"), sem("y1_high_copied")]
        t_done = [sem("t0_done"), sem("t1_done")]
        t_out = [sem("t0_copied"), sem("t1_copied")]
        h_out = sem("h_stored")
        ye_done, ye_out = sem("ye_done"), sem("ye_copied")
        dve = sem("vector_steps")
        pool_ready, pool_var, pool_r = sem("pool_ready"), sem("variance_ready"), sem("rstd_ready")
        tab_t, tab_tc, tab_m, tab_c, tab_s = sem("tab_turned"), sem("tab_turned_copied"), sem("tab_mult"), sem("tab_copied"), sem("tab_stored")
        s_rows = sem("id_rows")
        s_gath = sem("gathered")
        l_src, l_t, l_tc, l_m = sem("level_ready"), sem("level_turned"), sem("level_copied"), sem("level_mult")
        pad_z = sem("pad_zero")
        txt_ok = sem("text_done")
        comp_ready = sem("vocabulary_normed")

        wfv = t["L0_tok_W"].rearrange("d (f c) -> f d c", c=C)
        xv = t["x"].rearrange("b c (j u r) v -> b u c j (r v)", u=2, r=KB)
        lr = t["L0_txt_W_bin"].rearrange("(s k) d -> k s d", k=D)

        with nc.Block() as block:
            @block.sync
            def _(sp):
                for u in range(2):
                    sp.dma_start(wf[:, :, u, :], wfv).then_inc(s_w, 16)
                sp.dma_start(dft[:], t["c_dft"]).then_inc(s_w, 16)
                sp.dma_start(ident[:], t["c_ident"]).then_inc(s_w, 16)
                sp.dma_start(fold[:], t["c_fold"]).then_inc(s_w, 16)
                sp.dma_start(ids[:], t["x_txt"].rearrange("b k -> k b"), allow_slow_non_contiguous=True).then_inc(s_id, 16)
                for u in range(2):
                    sp.dma_start(xe[u * C:(u + 1) * C], t["x"][:, :, T - 1, :].rearrange("b c v -> c b v")).then_inc(s_e, 16)
                sp.dma_start(comp[:], t["L0_txt_comp_emb"].rearrange("(h p) d -> p h d", p=P)).then_inc(s_txt, 16)
                sp.dma_start(opemb[:], t["L0_txt_op_emb"]).then_inc(s_txt, 16)
                sp.dma_start(w0[:], t["L0_txt_W_bin"][0:D, :]).then_inc(s_txt, 16)
                sp.dma_start(wlr[:], lr[:, 1:3, :]).then_inc(s_txt, 16)
                sp.dma_start(w12[:], t["L0_txt_W_bin"][D:3 * D, :]).then_inc(s_txt, 16)
                sp.dma_start(bb[:], rows(t["L0_txt_b_bin"], P)).then_inc(s_txt, 16)
                sp.dma_start(gam[:], rows(t["L0_txt_gamma"], P)).then_inc(s_txt, 16)
                sp.dma_start(bet[:], rows(t["L0_txt_beta"], P)).then_inc(s_txt, 16)
                for k in range(2):
                    for q in (y_done, lo_out, hi_out, t_done, t_out):
                        sp.sem_inc(q[k], 1)
                with sp.Fori(0, B // 2) as it:
                    for k in range(2):
                        for u in range(2):
                            sp.wait_ge(y_done[k], it * 2 + 1)
                            sp.dma_start(x[u * C:(u + 1) * C, k], xv[it * 2 + k, u]).then_inc(s_x[k], 16)

            @block.tensor
            def _(pe):
                pe.wait_ge(s_w, 80)
                for d in range(D):
                    mm = pe.matmul(psw[:, d // 32, (d % 32) * PATCH:(d % 32 + 1) * PATCH], wf[:, d, :, :], dft[:], start=True, stop=True)
                mm.then_inc(g_ready, 1)
                pe.wait_ge(s_txt, 128)
                pe.wait_ge(comp_ready, 1)
                for v in range(2):
                    pe.transpose(pst[0:D, 0, v * P:(v + 1) * P], comp[:, v, :], ident[:])
                pe.transpose(pst[0:D, 0, 2 * P:2 * P + NOPS], opemb[:], ident[0:NOPS, 0:NOPS]).then_inc(tab_t, 1)
                pe.wait_ge(tab_tc, 2)
                for v in range(2):
                    pe.matmul(pst[:, 1, v * P:(v + 1) * P], compt[:, v, :], wlr[:], start=True, stop=True)
                pe.matmul(pst[0:NOPS, 1, 2 * P:2 * P + D], opt[:], w0[:], start=True, stop=True).then_inc(tab_m, 1)
                pe.wait_ge(g_copied, 4)
                pe.wait_ge(s_e, 32)
                for r in range(KB):
                    mm = pe.matmul(psw[:, 0, :], g[:, r], xe[:], start=(r == 0), stop=(r == KB - 1))
                mm.then_inc(ye_done, 1)
                pe.wait_ge(tab_c, 2)
                pe.wait_ge(ye_out, 1)
                with pe.Fori(0, B // 2) as it:
                    for k in range(2):
                        for j in range(2):
                            pe.wait_ge(s_x[k], it * 32 + 32)
                            pe.wait_ge(lo_out[k], it * 2 + 1)
                            pe.wait_ge(hi_out[k], it * 3 + 1)
                            for r in range(KB):
                                mm = pe.matmul(psy[:, k, j, :], g[:, r], x[:, k, 8 * j:8 * j + 8, r * V:(r + 1) * V], start=(r == 0), stop=(r == KB - 1))
                            mm.then_inc(y_done[k], 1)
                    for k in range(2):
                        pe.wait_ge(lo_out[k], it * 2 + 3)
                        pe.wait_ge(hi_out[k], it * 3 + 4)
                        pe.wait_ge(t_out[k], it + 1)
                        for a in range(8):
                            mm = pe.matmul(pst[:, k, a * D:(a + 1) * D], y[:, k, 8 * a:8 * a + 8, :], fold[:], start=True, stop=True)
                        mm.then_inc(t_done[k], 1)
                for lv, n in ((0, 16), (1, 8)):
                    pe.wait_ge(l_src, lv + 1)
                    for i in range(n):
                        mm = pe.transpose(psw[:, i // 4 % 2, (i % 4) * P:(i % 4) * P + TXT], tx[:, 2 * i:2 * i + 2, :], ident[0:TXT, 0:TXT])
                        if i % 4 == 3:
                            mm.then_inc(l_t, 1)
                            if i // 4 % 2 == 1 and i < n - 1:
                                pe.wait_ge(l_tc, 4 * lv + i // 4 + 1)
                    pe.wait_ge(l_tc, 4 * lv + n // 4)
                    for i in range(n):
                        mm = pe.matmul(pst[0:TXT, i // 8, (i % 8) * D:(i % 8 + 1) * D], tt[:, i, :], w12[:], start=True, stop=True)
                    mm.then_inc(l_m, 1)

            @block.scalar
            def _(act):
                act.wait_ge(ye_done, 1)
                act.wait_ge(tab_c, 2)
                act.dma_start(tl_d.rearrange("(h p) d -> p h d", p=P), tlr[:, :, 0, :]).then_inc(tab_s, 16)
                act.dma_start(tr_d.rearrange("(h p) d -> p h d", p=P), tlr[:, :, 1, :]).then_inc(tab_s, 16)
                act.dma_start(to_d, top[:]).then_inc(tab_s, 16)
                nc.scalar.copy(ye[:].rearrange("p b v -> p (b v)"), psw[:, 0, :]).then_inc(ye_out, 1)
                with act.Fori(0, B // 2) as it:
                    for k in range(2):
                        for j in range(2):
                            act.wait_ge(y_done[k], it * 2 + j + 2)
                            act.wait_ge(t_done[k], it + 1)
                            nc.scalar.copy(y[0:D, k, :, 8 * j:8 * j + 8], psy[0:D, k, j, :].rearrange("p (j v) -> p v j", v=V)).then_inc(lo_out[k], 1)
                for lv, n in ((0, 4), (1, 2)):
                    act.wait_ge(l_m, lv)
                    for i in range(n):
                        act.wait_ge(l_t, 4 * lv + i + 1)
                        nc.scalar.copy(tt[:, 4 * i:4 * i + 4, :], psw[:, i % 2, :].rearrange("p (q k) -> p q k", k=P)[:, :, 0:TXT]).then_inc(l_tc, 1)
                for k in range(2):
                    act.wait_ge(t_out[k], B // 2 + 1)
                act.wait_ge(txt_ok, 1)
                act.dma_start(h1d.rearrange("b (a p) d -> p a b d", p=P)[:, NA - 1], h[:, NA - 1]).then_inc(h_out, 16)
                with act.Fori(0, B) as b:
                    act.dma_start(h1d[b].rearrange("(a p) d -> p a d", p=P)[:, 0:8, :], h[:, 0:8, b, :]).then_inc(h_out, 16)
                act.wait_ge(h_out, 16 * (B + 1))

            @block.gpsimd
            def _(pool):
                pool.memset(mhalf[:], -0.5).then_inc(pool_ready, 1)
                pool.wait_ge(pool_ready, 1)
                pool.memset(h[64:128, NA - 1], 0.0).then_inc(pad_z, 1)
                pool.wait_ge(s_id, 16)
                for b in range(B):
                    pool.indirect_dma_start(leaf[:, b, :], None, t["L0_txt_leaf_ids"], bass.IndirectOffsetOnAxis(ap=ids[:, b:b + 1], axis=0)).then_inc(s_rows, 16)
                    pool.indirect_dma_start(opi[:, b, :], None, t["L0_txt_op_ids"], bass.IndirectOffsetOnAxis(ap=ids[:, b:b + 1], axis=0)).then_inc(s_rows, 16)
                pool.wait_ge(pad_z, 1)
                pool.wait_ge(pool_var, 1)
                pool.tensor_tensor(st[:, 3, 0:2], st[:, 2, 0:2], mhalf[:, 0:2], ALU.pow).then_inc(pool_r, 1)
                pool.wait_ge(tab_s, 48)
                pool.wait_ge(s_rows, 32 * B)
                for b in range(B):
                    for j in range(4):
                        pool.indirect_dma_start(gl[:, b, j, :], None, tl_d, bass.IndirectOffsetOnAxis(ap=leaf[:, b, 2 * j:2 * j + 1], axis=0)).then_inc(s_gath, 16)
                        pool.indirect_dma_start(gr[:, b, j, :], None, tr_d, bass.IndirectOffsetOnAxis(ap=leaf[:, b, 2 * j + 1:2 * j + 2], axis=0)).then_inc(s_gath, 16)
                    for j in range(NOP):
                        pool.indirect_dma_start(go[:, b, j, :], None, to_d, bass.IndirectOffsetOnAxis(ap=opi[:, b, j:j + 1], axis=0)).then_inc(s_gath, 16)
                for lv, n in enumerate((32, 16, 8)):
                    pool.wait_ge(pool_var, 2 + lv)
                    pool.tensor_tensor(st[0:TXT, 3, 0:n], st[0:TXT, 2, 0:n], mhalf[0:TXT, 0:n], ALU.pow).then_inc(pool_r, 1)

            @block.vector
            def _(v):
                ch = Chain(v, dve)

                def layer_norm(out, src, tmp, n, p, which, ready):
                    ch.step(nc.vector.tensor_reduce(st[0:p, 0, 0:n], src, AX.X, ALU.add))
                    ch.step(nc.vector.tensor_scalar(st[0:p, 1, 0:n], st[0:p, 0, 0:n], -1.0 / D, None, ALU.mult))
                    ch.step(nc.vector.tensor_tensor(src, src, bcast(st[0:p, 1, 0:n], D), ALU.add))
                    ch.step(nc.vector.tensor_tensor(tmp, src, src, ALU.mult))
                    ch.step(nc.vector.tensor_reduce(st[0:p, 0, 0:n], tmp, AX.X, ALU.add))
                    nc.vector.tensor_scalar(st[0:p, 2, 0:n], st[0:p, 0, 0:n], 1.0 / D, EPS, ALU.mult, ALU.add).then_inc(pool_var, 1)
                    v.wait_ge(pool_r, which)
                    ch.step(nc.vector.tensor_tensor(tmp, src, bcast(st[0:p, 3, 0:n], D), ALU.mult))
                    ch.step(nc.vector.tensor_tensor(tmp, tmp, bmid(gam[0:p], n), ALU.mult))
                    nc.vector.tensor_tensor(out, tmp, bmid(bet[0:p], n), ALU.add).then_inc(ready, 1)

                v.wait_ge(g_ready, 1)
                for u in range(2):
                    for q in range(2):
                        src = psw[u * C:(u + 1) * C, q, :].rearrange("p (d h w r) -> p w r h d", h=2, w=2, r=KB)[:, u]
                        for hf in range(2):
                            ins = nc.vector.tensor_copy(g[u * C:(u + 1) * C, :, hf, 32 * q:32 * q + 32], src[:, :, hf, :])
                        ins.then_inc(g_copied, 1)
                v.wait_ge(s_txt, 128)
                layer_norm(comp[:], comp[:], compq[:], 2, P, 1, comp_ready)
                v.wait_ge(tab_t, 1)
                nc.vector.tensor_copy(compt[:], pst[0:D, 0, 0:2 * P].rearrange("p (h k) -> p h k", k=P)).then_inc(tab_tc, 1)
                nc.vector.tensor_copy(opt[:], pst[0:D, 0, 2 * P:2 * P + NOPS]).then_inc(tab_tc, 1)
                v.wait_ge(tab_m, 1)
                nc.vector.tensor_copy(tlr[:].rearrange("p h s d -> p (h s d)"), pst[:, 1, 0:2 * P]).then_inc(tab_c, 1)
                nc.vector.tensor_tensor(top[:], pst[0:NOPS, 1, 2 * P:2 * P + D], bb[0:NOPS], ALU.add).then_inc(tab_c, 1)
                with v.Fori(0, B // 2) as it:
                    for k in range(2):
                        hi = slice(D, P)
                        src = psy[hi, k].rearrange("p q (j v) -> p v (q j)", v=V)
                        for j in range(2):
                            v.wait_ge(y_done[k], it * 2 + j + 2)
                            v.wait_ge(t_done[k], it + 1)
                            if j == 0:
                                nc.vector.tensor_copy(y[hi, k, :, 0:7], src[:, :, 1:8]).then_inc(hi_out[k], 1)
                            else:
                                nc.vector.tensor_copy(y[hi, k, :, 7:15], src[:, :, 8:16]).then_inc(hi_out[k], 1)
                        v.wait_ge(ye_out, 1)
                        nc.vector.tensor_copy(y[hi, k, :, 15], ye[hi, it * 2 + k, :]).then_inc(hi_out[k], 1)
                    for k in range(2):
                        v.wait_ge(t_done[k], it + 2)
                        nc.vector.tensor_copy(h[:, 0:8, it * 2 + k, :], pst[:, k, :].rearrange("p (a d) -> p a d", d=D)).then_inc(t_out[k], 1)
                v.wait_ge(s_gath, 16 * B * 15)
                v.wait_ge(s_id, 16)
                ch.step(nc.vector.tensor_copy(idf[:], ids[:]))
                ch.step(nc.vector.tensor_scalar(keep[:], idf[:], 1.0, None, ALU.is_gt))
                txv = tx[:].rearrange("p (b j) d -> p b j d", b=B)
                ch.step(nc.vector.tensor_tensor(gl[:], gl[:], gr[:], ALU.add))
                ch.step(nc.vector.tensor_tensor(gl[:], gl[:], go[:, :, 0:4, :], ALU.add))
                layer_norm(tx[:], gl[:].rearrange("p b j d -> p (b j) d"), tq[:], 32, TXT, 2, l_src)
                for lv, (n, off) in enumerate(((16, 4), (8, 6))):
                    v.wait_ge(l_m, lv + 1)
                    m = n // B
                    for q in range(n // 8):
                        bs = slice(q * 8 // m, (q + 1) * 8 // m)
                        ch.step(nc.vector.tensor_tensor(
                            tx[:, 8 * q:8 * q + 8, :].rearrange("p (b j) d -> p b j d", j=m),
                            pst[0:TXT, q, :].rearrange("p (b j d) -> p b j d", j=m, d=D),
                            go[:, bs, off:off + m, :], ALU.add))
                    layer_norm(tx[:, 0:n], tx[:, 0:n], tq[:, 0:n], n, TXT, 3 + lv, l_src)
                v.wait_ge(l_src, 3)
                v.wait_ge(pad_z, 1)
                nc.vector.tensor_tensor(h[0:TXT, NA - 1], tx[:, 0:B], bcast(keep[:], D), ALU.mult).then_inc(txt_ok, 1)


KH = (L + 1) // 2
KC = -(-KH // P)
KREV = LP + P
AP_ = NA + 3
NT = NA // 3
HC = 4
FT = 3
FW = L // FT


def norm_rows(nc, v, ch, pool_var, pool_r, which, out, src, tmp, stat, n, p=P, cut=None):
    fold = (lambda x: x.rearrange("p (a b) -> p a b", b=cut)) if cut else (lambda x: x)
    ch.step(nc.vector.tensor_reduce(stat[0:p, 0, 0:n], src, AX.X, ALU.add))
    ch.step(nc.vector.tensor_scalar(stat[0:p, 1, 0:n], stat[0:p, 0, 0:n], -1.0 / D, None, ALU.mult))
    ch.step(nc.vector.tensor_tensor(src, src, bcast(stat[0:p, 1, 0:n], D), ALU.add))
    ch.step(nc.vector.tensor_tensor(tmp, src, src, ALU.mult))
    ch.step(nc.vector.tensor_reduce(stat[0:p, 0, 0:n], tmp, AX.X, ALU.add))
    nc.vector.tensor_scalar(stat[0:p, 2, 0:n], stat[0:p, 0, 0:n], 1.0 / D, EPS, ALU.mult, ALU.add).then_inc(pool_var, 1)
    v.wait_ge(pool_r, which)
    return ch.done(nc.vector.tensor_tensor(out, *((x.rearrange("p (a b) d -> p a b d", b=cut) if cut else x) for x in (src,)), bcast(fold(stat[0:p, 3, 0:n]), D), ALU.mult))


def stage_taps(nc, t, krev_d):
    NC2 = 2 * KC
    H1 = D + 1
    with ExitStack() as ctx:
        sb = lambda n, s, d=F32: ctx.enter_context(nc.sbuf_tensor(n, s, d))
        ps = lambda n, s: ctx.enter_context(nc.psum_tensor(n, s, F32))
        sem = lambda n: ctx.enter_context(nc.semaphore(n))
        ident = sb("t_ident", [P, P])
        cq = sb("cq", [H1, 2, D])
        cqs = sb("cqs", [H1, 2, D])
        ct = sb("ct", [P, 2, H1])
        cols = sb("cols", [P, 6])
        sc = sb("sc", [P, 16])
        kon = sb("kon", [P, 4])
        tanr = sb("tanr", [P, NC2, P])
        tanc = sb("tanc", [P, NC2])
        cosb = sb("cosb", [P, KC, L])
        sinb = sb("sinb", [P, KC, L])
        stepv = sb("stepv", [P, 1])
        dval = sb("dval", [D, 1])
        w = sb("w", [P, NC2, P])
        den = sb("den", [P, NC2, P])
        inv = sb("inv", [P, NC2, P])
        coef = sb("coef", [P, 4, H1])
        tmp = sb("tmp", [P, H1])
        k4 = sb("k4", [P, NC2, 4, H1])
        sm = sb("sm", [P, 8, NC2])
        t1 = sb("t1", [P, NC2, D])
        t2 = sb("t2", [P, NC2, D])
        dr = sb("dr", [P, NC2, D])
        di = sb("di", [P, NC2, D])
        ar = sb("ar", [P, NC2, D])
        ai = sb("ai", [P, NC2, D])
        ev = sb("ev", [P, KC, D])
        od = sb("od", [P, KC, D])
        kr = sb("kr", [D, KREV])
        psc = ps("psc_t", [P, 512])
        psk = ps("psk", [P, 4, 512])
        pso = ps("pso", [P, FT, 512])
        s_c, s_s, s_t, s_tab = sem("c_loaded"), sem("scalars_loaded"), sem("tan_loaded"), sem("tables_loaded")
        turned, dve, inv_ok = sem("c_turned"), sem("tap_steps"), sem("inv_ready")
        kdone, kout, ev_ok, taps, stored = sem("k_done"), sem("k_copied"), sem("spectrum_ready"), sem("taps_done"), sem("taps_stored")
        kr_ok = sem("taps_ready")

        with nc.Block() as block:
            @block.sync
            def _(sp):
                for i, (n, q) in enumerate((("L0_attn_C", "L0_attn_Q"), )):
                    for u, part in enumerate(("_re", "_im")):
                        for dst, w_ in ((cq, u), (cqs, 1 - u)):
                            sp.dma_start(dst[0:D, w_, :], t[n + part]).then_inc(s_c, 16)
                            sp.dma_start(dst[D:H1, w_, :], rows(t[q + part], 1)).then_inc(s_c, 16)
                sp.dma_start(ident[:], t["c_ident"]).then_inc(s_c, 16)
                for i, n in enumerate(("B_re", "B_im", "P_re", "P_im", "Lambda_re", "Lambda_im")):
                    for u in range(2):
                        sp.dma_start(cols[u * D:(u + 1) * D, i:i + 1], t["L0_attn_" + n].rearrange("(n o) -> n o", o=1), allow_slow_non_contiguous=True).then_inc(s_s, 16)
                sp.dma_start(kon[:], t["c_halves"]).then_inc(s_s, 16)
                sp.dma_start(stepv[:], rows(t["L0_attn_step"], P)).then_inc(s_s, 16)
                sp.dma_start(dval[:], rows(t["L0_attn_D"], D)).then_inc(s_s, 16)
                sp.dma_start(tanc[:], t["c_tancol"]).then_inc(s_s, 16)
                sp.dma_start(tanr[:].rearrange("p c k -> p (c k)"), rows(t["c_tanrow"], P)).then_inc(s_t, 16)
                for dst, n in ((cosb, "c_cos"), (sinb, "c_sin")):
                    sp.dma_start(dst[:, 0:KC - 1], t[n][0:(KC - 1) * P].rearrange("(c p) l -> p c l", p=P)).then_inc(s_tab, 16)
                    sp.dma_start(dst[0:KH - (KC - 1) * P, KC - 1], t[n][(KC - 1) * P:KH]).then_inc(s_tab, 16)
                sp.wait_ge(kr_ok, 1)
                sp.dma_start(krev_d, kr[:]).then_inc(stored, 16)
                sp.wait_ge(stored, 16)

            @block.tensor
            def _(pe):
                pe.wait_ge(s_c, 16 * 9)
                pe.transpose(psc[:, 0:H1], cq[:], ident[0:H1, 0:H1])
                pe.transpose(psc[:, P:P + H1], cqs[:], ident[0:H1, 0:H1]).then_inc(turned, 1)
                pe.wait_ge(inv_ok, 1)
                for c in range(NC2):
                    if c >= 4:
                        pe.wait_ge(kout, c - 3)
                    pe.matmul(psk[:, c % 4, 0:4 * H1], inv[:, c, :], coef[:], start=True, stop=True).then_inc(kdone, 1)
                pe.wait_ge(ev_ok, 1)
                pe.wait_ge(s_tab, 64)
                for f in range(FT):
                    for c in range(KC):
                        kc = min(P, KH - c * P)
                        for src, tab in ((ev, cosb), (od, sinb)):
                            mm = pe.matmul(pso[0:D, f, 0:FW], src[0:kc, c, :], tab[0:kc, c, f * FW:(f + 1) * FW], start=(c == 0 and src is ev), stop=(c == KC - 1 and src is od))
                    mm.then_inc(taps, 1)

            @block.scalar
            def _(act):
                for c in range(NC2):
                    act.wait_ge(kdone, c + 1)
                    nc.scalar.copy(k4[:, c].rearrange("p q h -> p (q h)"), psk[:, c % 4, 0:4 * H1]).then_inc(kout, 1)

            @block.vector
            def _(v):
                ch = Chain(v, dve)
                one, st = ch.step, nc.vector.scalar_tensor_tensor
                ts, tt = nc.vector.tensor_scalar, nc.vector.tensor_tensor
                v.wait_ge(s_s, 16 * 16)
                one(ts(sc[:, 0:1], stepv[:], 1e-6, None, ALU.max))
                one(nc.vector.reciprocal(sc[:, 1:2], sc[:, 0:1]))
                one(ts(sc[:, 2:3], sc[:, 1:2], 2.0, None, ALU.mult))
                one(tt(sc[:, 3:4], cols[:, 4:5], cols[:, 4:5], ALU.mult))
                one(tt(sc[:, 4:5], cols[:, 4:5], kon[:, 2:3], ALU.mult))
                for q in range(2):
                    one(ts(sc[:, 5 + 4 * q:6 + 4 * q], cols[:, 2 * q:2 * q + 1], kon[:, 0:1], None, ALU.mult))
                    one(ts(sc[:, 6 + 4 * q:7 + 4 * q], cols[:, 2 * q + 1:2 * q + 2], -1.0, None, ALU.mult))
                    one(ts(sc[:, 7 + 4 * q:8 + 4 * q], cols[:, 2 * q + 1:2 * q + 2], kon[:, 0:1], None, ALU.mult))
                v.wait_ge(turned, 1)
                one(nc.vector.tensor_copy(ct[:, 0, :], psc[:, 0:H1]))
                one(nc.vector.tensor_copy(ct[:, 1, :], psc[:, P:P + H1]))
                for q in range(2):
                    one(ts(tmp[:], ct[:, 1], sc[:, 6 + 4 * q:7 + 4 * q], None, ALU.mult))
                    one(st(coef[:, 2 * q], ct[:, 0], sc[:, 5 + 4 * q:6 + 4 * q], tmp[:], ALU.mult, ALU.add))
                    one(ts(tmp[:], ct[:, 1], cols[:, 2 * q:2 * q + 1], None, ALU.mult))
                    one(st(coef[:, 2 * q + 1], ct[:, 0], sc[:, 7 + 4 * q:8 + 4 * q], tmp[:], ALU.mult, ALU.add))
                v.wait_ge(s_t, 16)
                one(ts(w[:], tanr[:], sc[:, 2:3], cols[:, 5:6], ALU.mult, ALU.subtract))
                one(tt(den[:], w[:], w[:], ALU.mult))
                one(ts(den[:], den[:], sc[:, 3:4], None, ALU.add))
                one(nc.vector.reciprocal(den[:], den[:]))
                one(ts(w[:], w[:], kon[:, 1:2], sc[:, 4:5], ALU.mult, ALU.add))
                tt(inv[:], w[:], den[:], ALU.mult).then_inc(inv_ok, 1)
                v.wait_ge(kout, NC2)
                q10r, q10i, q11r, q11i = (k4[:, :, q, D] for q in range(4))
                S = lambda i: sm[:, i, :]
                one(ts(S(0), q11r, 1.0, None, ALU.add))
                one(tt(S(1), S(0), S(0), ALU.mult))
                one(tt(S(2), q11i, q11i, ALU.mult))
                one(tt(S(1), S(1), S(2), ALU.add))
                one(nc.vector.reciprocal(S(1), S(1)))
                one(tt(S(2), q10r, S(0), ALU.mult))
                one(tt(S(3), q10i, q11i, ALU.mult))
                one(tt(S(2), S(2), S(3), ALU.add))
                one(tt(S(4), S(2), S(1), ALU.mult))
                one(tt(S(2), q10i, S(0), ALU.mult))
                one(tt(S(3), q10r, q11i, ALU.mult))
                one(tt(S(2), S(2), S(3), ALU.subtract))
                one(tt(S(5), S(2), S(1), ALU.mult))
                wr, wi = bcast(S(4), D), bcast(S(5), D)
                k00r, k00i, k01r, k01i = (k4[:, :, q, 0:D] for q in range(4))
                one(tt(t1[:], k01r, wr, ALU.mult))
                one(tt(t2[:], k01i, wi, ALU.mult))
                one(tt(t1[:], t1[:], t2[:], ALU.subtract))
                one(tt(dr[:], k00r, t1[:], ALU.subtract))
                one(tt(t1[:], k01r, wi, ALU.mult))
                one(tt(t2[:], k01i, wr, ALU.mult))
                one(tt(t1[:], t1[:], t2[:], ALU.add))
                one(tt(di[:], k00i, t1[:], ALU.subtract))
                tb = bcast(tanc[:], D)
                one(tt(t1[:], di[:], tb, ALU.mult))
                one(tt(ar[:], dr[:], t1[:], ALU.subtract))
                one(tt(t1[:], dr[:], tb, ALU.mult))
                one(tt(ai[:], di[:], t1[:], ALU.add))
                one(tt(ev[:], ar[:, 0:KC], ar[:, KC:], ALU.add))
                tt(od[:], ai[:, 0:KC], ai[:, KC:], ALU.subtract).then_inc(ev_ok, 1)
                one(nc.vector.memset(kr[:], 0.0))
                for f in range(FT):
                    v.wait_ge(taps, f + 1)
                    o = LP - L + f * FW
                    one(nc.vector.tensor_copy(kr[:, o:o + FW], pso[0:D, f, 0:FW]))
                tt(kr[:, LP - 1:LP], kr[:, LP - 1:LP], dval[:], ALU.add).then_inc(kr_ok, 1)


def stage_ssm(nc, t, h1d, krev_d, h2d):
    NG = NA * B
    with ExitStack() as outer:
        sbo = lambda n, s, d=F32: outer.enter_context(nc.sbuf_tensor(n, s, d))
        yc = sbo("yc", [NT * 32, P, D])
        with ExitStack() as ctx:
            sb = lambda n, s, d=F32: ctx.enter_context(nc.sbuf_tensor(n, s, d))
            ps = lambda n, s: ctx.enter_context(nc.psum_tensor(n, s, F32))
            sem = lambda n: ctx.enter_context(nc.semaphore(n))
            hh = sb("hh", [P, NG, D])
            sq = sb("sq", [P, NG, D])
            stat = sb("stat", [P, 4, NG])
            mh = sb("mh", [P, NG])
            ut = sb("ut", [P, D, AP_, B])
            ub = sb("ub", [P, 2, HC, AP_ * B])
            tz = sb("tz", [P, 2 * HC, LP])
            psc = ps("psc", [P, 2, HC, P])
            s_h, dve, pv, pr, u_ok = sem("h_loaded"), sem("u_steps"), sem("u_var"), sem("u_rstd"), sem("u_ready")
            s_tz = [sem(f"taps{k}_loaded") for k in range(2 * HC)]
            ub_ok = [sem("u0_copied"), sem("u1_copied")]
            cdone = [sem(f"conv{k}_done") for k in range(2 * HC)]
            cout = [sem("conv0_copied"), sem("conv1_copied")]
            mh_ok, zero_ok = sem("mh_ready"), sem("zero_ready")
            with nc.Block() as block:
                @block.sync
                def _(sp):
                    for b in range(B):
                        sp.dma_start(hh[:].rearrange("p (a b) d -> p b a d", b=B)[:, b], h1d[b].rearrange("(a p) d -> p a d", p=P)).then_inc(s_h, 16)
                    for k in range(2 * HC):
                        sp.sem_inc(cdone[k], 1)
                    for k in range(2):
                        sp.sem_inc(cout[k], 1)
                    with sp.Fori(0, D // (2 * HC)) as it:
                        for k in range(2 * HC):
                            sp.wait_ge(cdone[k], it + 1)
                            c0 = it * (2 * HC) + k
                            sp.dma_start(tz[:, k, :], bass.AP(krev_d.tensor, krev_d.offset + c0 * KREV, [[1, P], [1, LP]])).then_inc(s_tz[k], 16)

                @block.tensor
                def _(pe):
                    with pe.Fori(0, D // (2 * HC)) as it:
                        for k in range(2 * HC):
                            g, c = divmod(k, HC)
                            if c == 0:
                                pe.wait_ge(ub_ok[g], it + 1)
                                pe.wait_ge(cout[g], it + 1)
                            pe.wait_ge(s_tz[k], it * 16 + 16)
                            for dl in range(NA):
                                for i in range(dl // 3, NT):
                                    o = (3 * i + 2 - dl) * B
                                    mm = pe.matmul(psc[32 * i:32 * i + 32, g, c, :], ub[:, g, c, o:o + 32], tz[:, k, LP - P - P * dl:LP - P * dl],
                                                   start=(dl == 0), stop=(dl == 3 * i + 2), skip_group_check=True)
                            mm.then_inc(cdone[k], 1)

                @block.scalar
                def _(act):
                    with act.Fori(0, D // (2 * HC)) as it:
                        for g in range(2):
                            act.wait_ge(cdone[g * HC + HC - 1], it + 2)
                            c0 = it * (2 * HC) + g * HC
                            nc.scalar.copy(yc[:, :, bass.ds(c0, HC)].rearrange("r p c -> r c p"), psc[0:NT * 32, g]).then_inc(cout[g], 1)

                @block.gpsimd
                def _(pool):
                    pool.memset(mh[:], -0.5).then_inc(mh_ok, 1)
                    pool.wait_ge(mh_ok, 1)
                    pool.wait_ge(pv, 1)
                    pool.tensor_tensor(stat[:, 3], stat[:, 2], mh[:], ALU.pow).then_inc(pr, 1)

                @block.vector
                def _(v):
                    ch = Chain(v, dve)
                    ch.done(nc.vector.memset(ut[:, :, 0:2, :], 0.0))
                    ch.step(nc.vector.memset(ut[:, :, AP_ - 1:AP_, :], 0.0))
                    v.wait_ge(s_h, 16 * B)
                    norm_rows(nc, v, ch, pv, pr, 1, ut[:, :, 2:2 + NA, :].rearrange("p d a b -> p a b d"),
                              hh[:], sq[:], stat, NG, cut=B)
                    ch.wait()
                    with v.Fori(0, D // (2 * HC)) as it:
                        for g in range(2):
                            v.wait_ge(cdone[g * HC + HC - 1], it + 1)
                            c0 = it * (2 * HC) + g * HC
                            nc.vector.tensor_copy(ub[:, g].rearrange("p c a -> p (c a)"), ut[:, bass.ds(c0, HC)].rearrange("p c a b -> p (c a b)")).then_inc(ub_ok[g], 1)

        with ExitStack() as ctx:
            sb = lambda n, s, d=F32: ctx.enter_context(nc.sbuf_tensor(n, s, d))
            ps = lambda n, s: ctx.enter_context(nc.psum_tensor(n, s, F32))
            sem = lambda n: ctx.enter_context(nc.semaphore(n))
            ident = sb("f_ident", [P, P])
            wfc = sb("wfc", [D, 2, D])
            wb = sb("wb", [P, 2, D])
            bfc = sb("bfc", [P, D])
            lng = sb("lng", [P, D])
            lnb = sb("lnb", [P, D])
            y1 = sb("y1", [P, NT * 32, P // 2])
            hl = sb("hl", [P, NG, D])
            uc = sb("uc", [P, NG, D])
            ul = sb("ul", [P, NG, D])
            z = sb("z", [P, NG, D])
            stat = sb("fstat", [P, 4, NG])
            mh = sb("fmh", [P, NG])
            pst = ps("f_pst", [P, 2, 4, P])
            psf = ps("psf", [P, 3, 512])
            psw = ps("f_psw", [P, 512])
            s_w, s_h, dve, pv, pr = sem("fc_loaded"), sem("hl_loaded"), sem("fc_steps"), sem("fc_var"), sem("fc_rstd")
            wt, wb_ok, turned, y1_ok, fdone, zadd, zg, h_ok, h_out, mh_ok = (sem(x) for x in (
                "w_turned", "w_ready", "y_turned", "y1_ready", "fc_done", "fc_bias", "fc_gelu", "h2_ready", "h2_stored", "fmh_ready"))
            view = lambda x, b: x[b].rearrange("(a p s) d -> p a (s d)", p=P // 2, s=2)
            grp = lambda x, b: x[64 * (b % 2):64 * (b % 2) + 64].rearrange("p (a q s) d -> p q a (s d)", q=B // 2, s=2)[:, b // 2]
            with nc.Block() as block:
                @block.sync
                def _(sp):
                    sp.dma_start(ident[:], t["c_ident"]).then_inc(s_w, 16)
                    for u in range(2):
                        sp.dma_start(wfc[:, u, :], t["L0_attn_W_fc"]).then_inc(s_w, 16)
                    sp.dma_start(bfc[:], rows(t["L0_attn_b_fc"], P)).then_inc(s_w, 16)
                    sp.dma_start(lng[:], rows(t["L0_attn_ln_g"], P)).then_inc(s_w, 16)
                    sp.dma_start(lnb[:], rows(t["L0_attn_ln_b"], P)).then_inc(s_w, 16)
                    for b in range(B):
                        sp.dma_start(grp(hl, b), view(h1d, b)).then_inc(s_h, 16)
                    sp.wait_ge(h_ok, 1)
                    for b in range(B):
                        sp.dma_start(view(h2d, b), grp(z, b)).then_inc(h_out, 16)
                    sp.wait_ge(h_out, 16 * B)

                @block.tensor
                def _(pe):
                    pe.wait_ge(s_w, 96)
                    pe.transpose(psw[:, 0:D], wfc[:], ident[0:D, 0:D]).then_inc(wt, 1)
                    for g in range(16):
                        if g >= 2:
                            pe.wait_ge(y1_ok, g - 1)
                        for s in range(4):
                            pr_ = P // 2 - 1 - (4 * g + s)
                            mm = pe.transpose(pst[:, g % 2, s, 0:NT * 32], yc[:, 2 * pr_:2 * pr_ + 2, :], ident[0:NT * 32, 0:NT * 32])
                        mm.then_inc(turned, 1)
                    pe.wait_ge(wb_ok, 1)
                    pe.wait_ge(y1_ok, 16)
                    for a in range(NA):
                        if a >= 3:
                            pe.wait_ge(zadd, a - 2)
                        for q in range(B // 2):
                            r0 = 32 * (a // 3) + B * (a % 3) + 2 * q
                            mm = pe.matmul(psf[:, a % 3, q * P:(q + 1) * P], y1[:, r0:r0 + 2, :], wb[:], start=True, stop=True)
                        mm.then_inc(fdone, 1)

                @block.scalar
                def _(act):
                    for g in range(16):
                        act.wait_ge(turned, g + 1)
                        nc.scalar.activation(y1[:, :, 4 * g:4 * g + 4].rearrange("p r s -> p s r"), pst[:, g % 2, :, 0:NT * 32], ACT.Gelu).then_inc(y1_ok, 1)
                    for a in range(NA):
                        act.wait_ge(zadd, a + 1)
                        zz = z[:, 8 * a:8 * a + 8, :]
                        nc.scalar.activation(zz, zz, ACT.Gelu).then_inc(zg, 1)

                @block.gpsimd
                def _(pool):
                    pool.memset(mh[:], -0.5).then_inc(mh_ok, 1)
                    pool.wait_ge(mh_ok, 1)
                    for i in range(2):
                        pool.wait_ge(pv, i + 1)
                        pool.tensor_tensor(stat[:, 3], stat[:, 2], mh[:], ALU.pow).then_inc(pr, 1)

                @block.vector
                def _(v):
                    ch = Chain(v, dve)
                    ch.step(nc.vector.memset(wb[:], 0.0))
                    v.wait_ge(wt, 1)
                    ch.done(nc.vector.tensor_copy(wb[0:D, 1, :], psw[0:D, 0:D]))
                    nc.vector.tensor_copy(wb[D:P, 0, :], psw[D:P, 0:D]).then_inc(wb_ok, 1)
                    v.wait_ge(s_h, 16 * B)
                    ch.step(nc.vector.tensor_copy(uc[:], hl[:]))
                    norm_rows(nc, v, ch, pv, pr, 1, ul[:], uc[:], z[:], stat, NG)
                    ch.wait()
                    for a in range(NA):
                        v.wait_ge(fdone, a + 1)
                        nc.vector.tensor_tensor(z[:, 8 * a:8 * a + 8, :], psf[:, a % 3, :].rearrange("p (g d) -> p g d", d=D), bmid(bfc[:], 8), ALU.add).then_inc(zadd, 1)
                    v.wait_ge(zg, NA)
                    ch.step(nc.vector.tensor_tensor(z[:], z[:], ul[:], ALU.add))
                    norm_rows(nc, v, ch, pv, pr, 2, uc[:], z[:], ul[:], stat, NG)
                    ch.wait()
                    ch.step(nc.vector.tensor_tensor(uc[:], uc[:], bmid(lng[:], NG), ALU.mult))
                    ch.step(nc.vector.tensor_tensor(uc[:], uc[:], bmid(lnb[:], NG), ALU.add))
                    nc.vector.tensor_tensor(z[:], hl[:], uc[:], ALU.add).then_inc(h_ok, 1)


NH, NE, HD = 4, 4, 16
HE = NH * NE
FEPS = 1e-8
TERMS_Q = (0, 1, 0, 2, 0, 1)
TERMS_K = (0, 0, 1, 0, 2, 1)
KT = HD * len(TERMS_Q)
KM = KT + 3
VW = 32
QT = 512
UB = 3
LAST = L - (NA - 1) * P
FB = 384


def score_units():
    banks = []
    for tile in range(2):
        for j in range(4 * tile):
            banks += [[(0, j, e, QT * tile, QT)] for e in range(NE)]
        d = lambda i, e, c: (c, 4 * tile + i, e, QT * tile + P * i, QT - P * i)
        banks += [[d(0, e, 0)] for e in range(NE)]
        banks += [[d(1, e, 0), d(3, e, 384)] for e in range(NE)]
        banks += [[d(2, e, 0), d(2, e + 1, 256)] for e in (0, 2)]
    for j in range(NA):
        banks.append([(0, j, None, 2 * QT, LAST)])
    return [banks[i:i + UB] for i in range(0, len(banks), UB)]


def norm_groups(nc, v, ch, pool_var, pool_r, which, out, src, tmp, stat, n, d, eps):
    ch.step(nc.vector.tensor_reduce(stat[:, 0, 0:n], src, AX.X, ALU.add))
    ch.step(nc.vector.tensor_scalar(stat[:, 1, 0:n], stat[:, 0, 0:n], -1.0 / d, None, ALU.mult))
    ch.step(nc.vector.tensor_tensor(src, src, bcast(stat[:, 1, 0:n], d), ALU.add))
    ch.step(nc.vector.tensor_tensor(tmp, src, src, ALU.mult))
    ch.step(nc.vector.tensor_reduce(stat[:, 0, 0:n], tmp, AX.X, ALU.add))
    nc.vector.tensor_scalar(stat[:, 2, 0:n], stat[:, 0, 0:n], 1.0 / d, eps, ALU.mult, ALU.add).then_inc(pool_var, 1)
    v.wait_ge(pool_r, which)
    ch.step(nc.vector.tensor_tensor(out, src, bcast(stat[:, 3, 0:n], d), ALU.mult))


def stage_ffn(nc, t, h2d, out):
    units = score_units()
    NU = len(units)
    NDVE = 141
    qk_d = nc.dram_tensor("qk_parts", (3, 2 * P + D, LP), BF16).ap()
    xsrc = lambda b: h2d[b].rearrange("(a p) d -> p a d", p=P)
    with ExitStack() as ctx:
        sb = lambda n, s, d=F32: ctx.enter_context(nc.sbuf_tensor(n, s, d))
        ps = lambda n, s, d=F32: ctx.enter_context(nc.psum_tensor(n, s, d))
        sem = lambda n: ctx.enter_context(nc.semaphore(n))
        ident = sb("a_ident", [P, P])
        identb = sb("a_identb", [P, P], BF16)
        maskb = sb("maskb", [P, P], BF16)
        maskf = sb("maskf", [P, P])
        wha = sb("wha", [NH * HD, D + 1])
        wbd = sb("wbd", [NH * HD, 448])
        wall = sb("wall", [D + 1, 448])
        fcw = sb("fcw", [D + 1, 2, D])
        gw = sb("gw", [P, HE * 64])
        gb = sb("gb", [P, HE])
        fgw = sb("fgw", [P, NH, D])
        vec = sb("vec", [P, 4, HD])
        resid = sb("resid", [P, NA, D])
        h4 = sb("h4", [P, 4 * NA, D])
        hb = sb("hb", [P, NA, D])
        xn = sb("xn", [P, NA, D])
        tmp = sb("a_tmp", [P, 4 * NA, D])
        stat = sb("a_stat", [P, 4, 4 * NA])
        mh = sb("a_mh", [P, 4 * NA])
        xt = sb("xt", [D + 1, LP])
        qs = sb("qs", [P, 3, 2, LP], BF16)
        ks = sb("ks", [D, 3, LP], BF16)
        rq = sb("rq", [P, 3, FB])
        qop = sb("qop", [KM, NH, NE, LP], BF16)
        kop = sb("kop", [KM, NH, LP], BF16)
        vop = sb("vop", [P, NA, NH, VW])
        msk = sb("msk", [P, NA, D])
        mpart = sb("mpart", [P, NE, NA])
        mtok = sb("mtok", [P, NA, HE])
        mtp = sb("mtp", [P, NA, 3, HE], BF16)
        mres = sb("mres", [P, NA, HE])
        mt = sb("mt", [3 * HE, LP], BF16)
        pb = sb("pb", [P, 3, UB, QT])
        ofm = sb("ofm", [P, 2, QT])
        ot = sb("ot", [P, NA * NH, NE, VW])
        on = sb("on", [P, NA * NH, NE * HD])
        rec = sb("rec", [P, NA * NH, NE])
        lg = sb("lg", [P, NA * NH, NE])
        mx = sb("mx", [P, NA * NH])
        gs = sb("gs", [P, NA * NH, NE])
        mix = sb("mix", [P, NA * NH, HD])
        fx = sb("fx", [P, NA * NH, HD])
        fxt = sb("fxt", [D + 1, LP])
        hx1 = sb("hx1", [D + 1, LP])
        pm = sb("pm", [D, LP])
        fo = sb("fo", [P, NA * NH, HD])
        pss = ps("pss", [P, 2, UB, QT])
        pso = ps("a_pso", [P, QT])
        psm = ps("psm", [P, QT])
        psmb = psm[:].bitcast(BF16)

        res = sb("res", [P, NA, D])
        names = ("weights_loaded", "wbd_zeroed", "resid_loaded", "h_loaded", "bank_full", "bank_free", "vector_steps",
                 "variance", "rstd", "rest_ready", "rest_free", "parts_ready", "part1", "placed", "parts_used", "max_split", "max_placed",
                 "scored", "exped", "masked", "summed", "sums_copied", "logits", "logits_exped", "gate_exped", "result", "stored", "spilled", "passed", "tile_done", "pool_passed",
                 "mh_ready", "xn_ready", "fx_ready", "hx_ready", "swept", "swept_max", "ident_ready", "const_ready")
        (weights, wbd_zero, r_load, h_load, full, free, dve, var, rstd, rest, rest_free, parts, part1, placed, used, max_split, max_placed,
         scored, exped, masked, summed, acc_free, logit, logit_exp, gate_exp, result, stored, spilled, passed, tile_done, pool_passed,
         mh_ok, xn_ok, fx_ok, hx_ok, swept, swept_max, ident_ok, const_ok) = (sem("a_" + n) for n in names)
        chunks = [(0, 4), (4, 8), (8, 9)]

        PRO = [("turn", c) for c in chunks] + [("tok", c) for c in chunks] + [("feat", (g, k)) for g in range(3) for k in range(3)]
        MXJ = [("mrow", (0, 8)), ("mrow", (8, 9))]
        EPI = [("fturn", c) for c in chunks] + [("fc1", k) for k in range(3)] + [("fc2", k) for k in range(3)] + [("back", c) for c in chunks]
        OUTJ = [("oturn", (n, x)) for n in range(NH) for x in range(3)]
        J = len(PRO) + len(MXJ) + len(OUTJ) + len(EPI)
        JS = 1 + 4 * 6
        SWEEP = NH * NA * (NA + 1) // 2
        NUB = NH * NU
        dj = [[(c, b) for b, bank in enumerate(u) for (c, j, e, q0, w) in bank if (q0 == P * j if e is not None else j == NA - 1)] for u in units]
        NM = NH * sum(bool(d) for d in dj)
        assert NUB % 6 == 0 and SWEEP % 6 == 0
        order_m = {}
        for u, d in enumerate(dj):
            order_m[u] = sum(bool(x) for x in dj[:u + 1])
        tile_of = lambda q0: q0 // QT
        last_unit = {x: max(u for u, un in enumerate(units) for bank in un for p in bank if tile_of(p[3]) == x) for x in range(3)}
        last_bank = max(b for b, bank in enumerate(units[last_unit[0]]) if tile_of(bank[0][3]) == 0)
        assert last_bank < UB - 1 and all(tile_of(units[last_unit[x]][-1][0][3]) == x for x in (1, 2))

        with nc.Block() as block:
            @block.sync
            def _(sp):
                for s_, c in ((exped, 2), (summed, 3), (free, 1), (acc_free, 1), (parts, 3), (stored, 16), (swept_max, 6), (used, 1)):
                    sp.sem_inc(s_, c)
                sp.dma_start(ident[:], t["c_ident"]).then_inc(ident_ok, 16)
                sp.dma_start(wha[:, 0:D], t["L0_ffn_hl_w"].rearrange("n d h -> (n d) h")).then_inc(weights, 16)
                sp.dma_start(wha[:, D:D + 1], t["L0_ffn_hl_b"].rearrange("n (d o) -> (n d) o", o=1), allow_slow_non_contiguous=True).then_inc(weights, 16)
                sp.dma_start(gw[:], rows(t["L0_ffn_gate_w"].rearrange("n e f -> (n e f)"), P)).then_inc(weights, 16)
                sp.dma_start(gb[:], rows(t["L0_ffn_gate_b"].rearrange("n e -> (n e)"), P)).then_inc(weights, 16)
                sp.dma_start(fgw[:].rearrange("p n d -> p (n d)"), rows(t["L0_ffn_fgate_w"].rearrange("n d -> (n d)"), P)).then_inc(weights, 16)
                for i, n in enumerate(("ln_g", "ln_b", "fnorm_g", "fnorm_b")):
                    sp.dma_start(vec[:, i, :], rows(t["L0_ffn_" + n], P)).then_inc(weights, 16)
                for n in range(4):
                    sp.dma_start(h4[:, NA * n:NA * (n + 1), :], xsrc(n)).then_inc(r_load, 16)
                sp.wait_ge(wbd_zero, 2)
                sp.dma_start(wbd[:, 384:448], t["c_ident"][0:D, 0:D]).then_inc(weights, 16)
                for n in range(NH):
                    r = slice(HD * n, HD * n + HD)
                    o = HD * n
                    sp.dma_start(wbd[r, D * n:D * n + D], t["L0_ffn_wq"][n].rearrange("e o d -> d (e o)"), allow_slow_non_contiguous=True).then_inc(weights, 16)
                    sp.dma_start(wbd[r, 256 + o:272 + o], t["L0_ffn_wk"][n].rearrange("o d -> d o"), allow_slow_non_contiguous=True).then_inc(weights, 16)
                    sp.dma_start(wbd[r, 320 + o:336 + o], t["L0_ffn_wv"][n].rearrange("o d -> d o"), allow_slow_non_contiguous=True).then_inc(weights, 16)
                    for i in range(2):
                        w_, b_ = t[f"L0_ffn_fc{i + 1}_w"], t[f"L0_ffn_fc{i + 1}_b"]
                        sp.dma_start(fcw[r, i, o:o + HD], w_.rearrange("o d -> d o"), allow_slow_non_contiguous=True).then_inc(weights, 16)
                        sp.dma_start(fcw[D:D + 1, i, o:o + HD], rows(b_, 1)).then_inc(weights, 16)
                with sp.Fori(0, B) as it:
                    src = xsrc(it)
                    sp.wait_ge(stored, it * 32 + 16)
                    sp.dma_start(hb[:], src).then_inc(h_load, 16)
                    for g in range(2):
                        sp.wait_ge(parts, it * 9 + 3 * g + 6)
                        sp.dma_start(qk_d[:, P * g:P * g + P, :].rearrange("t r q -> r t q"), qs[:, :, g, :]).then_inc(spilled, 16)
                    sp.wait_ge(parts, it * 9 + 12)
                    sp.dma_start(qk_d[:, 2 * P:2 * P + D, :].rearrange("t r q -> r t q"), ks[:]).then_inc(spilled, 16)
                    sp.wait_ge(spilled, it * 48 + 48)
                    for i, (qp, kp) in enumerate(zip(TERMS_Q, TERMS_K)):
                        r = slice(HD * i, HD * i + HD)
                        sp.dma_start(qop[r].rearrange("o n e q -> o (n e) q"), qk_d[qp, 0:2 * P].rearrange("(m o) q -> o m q", o=HD)).then_inc(placed, 16)
                        sp.dma_start(kop[r], qk_d[kp, 2 * P:2 * P + D].rearrange("(n o) q -> o n q", o=HD)).then_inc(placed, 16)
                    sp.wait_ge(max_split, it + 1)
                    for i in range(3):
                        sp.dma_start(qop[KT + i:KT + i + 1].rearrange("k n e q -> k (n e) q"), mt[HE * i:HE * i + HE, :]).then_inc(max_placed, 16)
                    ores = out[it]
                    sp.wait_ge(result, it + 1)
                    sp.dma_start(ores[0:(NA - 1) * P].rearrange("(a p) d -> p a d", p=P), res[:, 0:NA - 1]).then_inc(stored, 16)
                    sp.dma_start(ores[(NA - 1) * P:L], res[0:LAST, NA - 1]).then_inc(stored, 16)
                sp.wait_ge(stored, 32 * B + 16)

            @block.tensor
            def _(pe):
                k = [0]

                def job(base, ins):
                    ins().then_inc(full, 1)
                    k[0] += 1

                def gate(base):
                    pe.wait_ge(free, base + k[0] + 1)

                def turn_rows(src, c, base, rows_=D):
                    gate(base)
                    pe.sem_inc(passed, 1)
                    for a in range(*c):
                        mm = pe.transpose(psm[0:D, (a - c[0]) * P:(a - c[0] + 1) * P], src[:, a, :], ident[:])
                    job(base, lambda: mm)

                pe.wait_ge(weights, 16 * 38)
                pe.wait_ge(ident_ok, 16)
                gate(0)
                job(0, lambda: pe.matmul(psm[0:D + 1, 0:448], wha[:], wbd[:], start=True, stop=True))
                pe.wait_ge(xn_ok, 1)
                for n in range(4):
                    for c in chunks:
                        turn_rows(h4[:, NA * n:NA * (n + 1)], c, 0)
                    for c in chunks:
                        gate(0)
                        for a in range(*c):
                            mm = pe.matmul(psm[:, (a - c[0]) * HD:(a - c[0] + 1) * HD], xt[:, a * P:(a + 1) * P], wall[:, 384 + HD * n:400 + HD * n], start=True, stop=True)
                        job(0, lambda: mm)
                assert k[0] == JS
                pe.wait_ge(const_ok, 3)
                with pe.Fori(0, B) as it:
                    k[0] = 0
                    base = it * J + JS
                    g0 = it * NUB
                    pe.wait_ge(xn_ok, it + 2)
                    for kind, c in PRO:
                        if kind == "turn":
                            turn_rows(xn, c, base)
                        elif kind == "tok":
                            gate(base)
                            for a in range(*c):
                                mm = pe.matmul(psm[:, (a - c[0]) * P:(a - c[0] + 1) * P], xt[:, a * P:(a + 1) * P], wall[:, 320:448], start=True, stop=True)
                            job(base, lambda: mm)
                        else:
                            g, x = c
                            gate(base)
                            m = P if g < 2 else D
                            job(base, lambda: pe.matmul(psm[0:m, 0:FB], wall[:, g * P:g * P + m], xt[:, x * FB:(x + 1) * FB], start=True, stop=True))
                    pe.wait_ge(placed, it * 192 + 192)
                    sw = 0
                    for n in range(NH):
                        for i in range(NA):
                            for j in range(i + 1):
                                pe.wait_ge(swept_max, it * SWEEP + sw + 1)
                                bank = pss[:, sw // 3 % 2, sw % 3, :]
                                for e in range(NE):
                                    mm = pe.matmul(bank[:, e * P:(e + 1) * P], qop[0:KT, n, e, i * P:(i + 1) * P], kop[0:KT, n, j * P:(j + 1) * P],
                                                   start=(e == 0 or i != j), stop=(i != j), skip_group_check=True)
                                if i == j:
                                    mm = pe.matmul(bank, identb[:], bmid(maskb[:], NE), start=False, stop=True, skip_group_check=True)
                                mm.then_inc(swept, 1)
                                sw += 1
                    for kind, c in MXJ:
                        gate(base)
                        pe.wait_ge(used, it + 2)
                        pe.sem_inc(passed, 1)
                        for a in range(*c):
                            mm = pe.transpose(psmb[0:3 * HE, (a - c[0]) * P:(a - c[0] + 1) * P], mtp[:, a], identb[:])
                        job(base, lambda: mm)
                    pe.wait_ge(max_placed, it * 48 + 48)
                    pe.wait_ge(swept_max, it * SWEEP + SWEEP + 6)

                    def scores(u):
                        n, un = divmod(u, NU)
                        pe.wait_ge(exped, g0 + u + 1)
                        for b, bank in enumerate(units[un]):
                            for col, j, e, q0, w in bank:
                                lhs = kop[:, n, j * P:(j + 1) * P]
                                if e is None:
                                    mm = pe.matmul(pss[:, u % 2, b, 0:NE * w], lhs, qop[:, n, :, q0:q0 + w], start=True, stop=True, skip_group_check=True)
                                else:
                                    mm = pe.matmul(pss[:, u % 2, b, col:col + w], lhs, qop[:, n, e, q0:q0 + w], start=True, stop=True, skip_group_check=True)
                        mm.then_inc(scored, 1)

                    def sums(u):
                        n, un = divmod(u, NU)
                        pe.wait_ge(exped, g0 + u + 3)
                        if dj[un]:
                            pe.wait_ge(masked, it * NM + (NM // NH) * n + order_m[un])
                        for b, bank in enumerate(units[un]):
                            for col, j, e, q0, w in bank:
                                x = tile_of(q0)
                                if j == 0 and e in (0, None):
                                    pe.wait_ge(acc_free, it * 3 * NH + 3 * n + x + 1)
                                r = P if j < NA - 1 else LAST
                                for ee in range(NE) if e is None else (e,):
                                    cc = col + (w * ee if e is None else 0)
                                    mm = pe.matmul(pso[VW * ee:VW * (ee + 1), q0 - QT * x:q0 - QT * x + w], vop[0:r, j, n, :], pb[0:r, u % 3, b, cc:cc + w],
                                                   start=(j == 0), stop=(q0 == P * j if e is not None else j == NA - 1), skip_group_check=True)
                            if un == last_unit[0] and b == last_bank:
                                mm.then_inc(tile_done, 1)
                        mm.then_inc(summed, 1)

                    for u in range(NUB + 1):
                        if u < NUB:
                            scores(u)
                        if u >= 1:
                            sums(u - 1)
                            n = (u - 1) // NU
                            for x in (x for x in range(3) if last_unit[x] == (u - 1) % NU):
                                c = (4 * x, min(4 * x + 4, NA))
                                gate(base)
                                pe.wait_ge(acc_free, it * 3 * NH + 3 * n + x + 2)
                                for a in range(*c):
                                    wd = P if a < NA - 1 else LAST
                                    mm = pe.transpose(psm[0:wd, (a - c[0]) * P:(a - c[0] + 1) * P], ofm[:, (3 * n + x) % 2, (a - c[0]) * P:(a - c[0]) * P + wd], ident[:])
                                job(base, lambda: mm)
                    pe.wait_ge(fx_ok, it + 1)
                    for kind, c in EPI:
                        if kind == "fturn":
                            turn_rows(fx[:].rearrange("p (a n) d -> p a (n d)", n=NH), c, base)
                        elif kind in ("fc1", "fc2"):
                            gate(base)
                            i = kind == "fc2"
                            job(base, lambda: pe.matmul(psm[0:D, 0:FB], fcw[:, int(i), :], (hx1 if i else fxt)[:, c * FB:(c + 1) * FB], start=True, stop=True))
                        else:
                            gate(base)
                            pe.sem_inc(passed, 1)
                            for a in range(*c):
                                mm = pe.transpose(psm[:, (a - c[0]) * D:(a - c[0] + 1) * D], pm[:, a * P:(a + 1) * P], ident[0:D, 0:D])
                            job(base, lambda: mm)
                    assert k[0] == J

            @block.scalar
            def _(act):
                with act.Fori(0, B) as it:
                    g0 = it * NUB
                    for u in range(NUB):
                        un = u % NU
                        act.wait_ge(scored, g0 + u + 1)
                        act.wait_ge(summed, g0 + u + 1)
                        w = QT if units[un][0][0][2] is not None else NE * LAST
                        nc.scalar.activation(pb[:, u % 3, :, 0:w], pss[:, u % 2, :, 0:w], ACT.Exp, scale=float(HD) ** 0.5).then_inc(exped, 1)
                    for i, (src, s_) in enumerate(((lg[:], logit_exp), (gs[:, 0:NA, :], gate_exp))):
                        act.wait_ge(logit, it * 2 + i + 1)
                        nc.scalar.activation(src, src, ACT.Exp).then_inc(s_, 1)

            @block.gpsimd
            def _(pool):
                pool.memset(mh[:], -0.5).then_inc(mh_ok, 1)
                pool.wait_ge(mh_ok, 1)
                pool.memset(maskf[:], 0.0).then_inc(mh_ok, 1)
                pool.wait_ge(mh_ok, 2)
                pool.affine_select(out=maskf[:], in_=maskf[:], compare_op=ALU.is_ge, fill=-1e30, base=0, pattern=[[-1, P]], channel_multiplier=1).then_inc(mh_ok, 1)
                pool.wait_ge(mh_ok, 3)
                pool.wait_ge(var, 1)
                pool.tensor_tensor(stat[:, 3], stat[:, 2], mh[:], ALU.pow).then_inc(rstd, 1)

                def root(i, it, n):
                    pool.wait_ge(var, it * 3 + i + 2)
                    pool.tensor_tensor(stat[:, 3, 0:n], stat[:, 2, 0:n], mh[:, 0:n], ALU.pow).then_inc(rstd, 1)

                with pool.Fori(0, B) as it:
                    root(0, it, NA)
                    for i in range(9):
                        g, x = divmod(i, 3)
                        m = P if g < 2 else D
                        dst = (lambda p_: qs[:, p_, g, x * FB:(x + 1) * FB]) if g < 2 else (lambda p_: ks[:, p_, x * FB:(x + 1) * FB])
                        pool.wait_ge(free, it * J + JS + 6 + i + 2)
                        pool.sem_inc(pool_passed, 1)
                        pool.tensor_copy(dst(1), rq[0:m, i % 3, :]).then_inc(part1, 1)
                        pool.wait_ge(part1, it * 9 + i + 1)
                        pool.tensor_tensor(dst(2), rq[0:m, i % 3, :], dst(1), ALU.subtract).then_inc(parts, 1)
                        pool.wait_ge(parts, it * 9 + i + 4)
                    for u in range(NUB):
                        un = u % NU
                        if not dj[un]:
                            continue
                        pool.wait_ge(exped, it * NUB + u + 3)
                        pool.sem_inc(pool_passed, 1)
                        cols = {}
                        for c, b in dj[un]:
                            cols.setdefault(c, []).append(b)
                        n_ = 0
                        for c, bs in sorted(cols.items()):
                            if units[un][bs[0]][0][2] is None:
                                v_ = pb[0:LAST, u % 3, bs[0], 0:NE * LAST].rearrange("p (e q) -> p e q", e=NE)
                                pat = [[0, NE], [1, LAST]]
                            else:
                                v_ = pb[:, u % 3, bs[0]:bs[-1] + 1, c:c + P]
                                pat = [[0, len(bs)], [1, P]]
                            ins = pool.affine_select(out=v_, in_=v_, compare_op=ALU.is_ge, fill=0.0, base=0, pattern=pat, channel_multiplier=-1)
                        ins.then_inc(masked, 1)
                    root(1, it, NA * NH)
                    root(2, it, NA * NH)

            @block.vector
            def _(v):
                tt, ts, stt, cp = nc.vector.tensor_tensor, nc.vector.tensor_scalar, nc.vector.scalar_tensor_tensor, nc.vector.tensor_copy
                red = nc.vector.tensor_reduce
                k = [0]
                nc.vector.memset(wbd[:], 0.0).then_inc(wbd_zero, 1)
                nc.vector.memset(fcw[:], 0.0).then_inc(wbd_zero, 1)
                ch = Chain(v, dve)
                ch.step(nc.vector.memset(xt[D:D + 1], 1.0))
                ch.step(nc.vector.memset(fxt[D:D + 1], 1.0))
                ch.step(nc.vector.memset(hx1[D:D + 1], 1.0))
                ch.step(nc.vector.memset(vop[:], 0.0))
                ch.step(nc.vector.memset(vop[:, :, :, HD:HD + 1], 1.0))
                ch.step(nc.vector.memset(ot[:], 1.0))
                nc.vector.memset(kop[KT:KM], -1.0).then_inc(const_ok, 1)
                v.wait_ge(ident_ok, 16)
                cp(identb[:], ident[:]).then_inc(const_ok, 1)
                v.wait_ge(mh_ok, 3)
                cp(maskb[:], maskf[:]).then_inc(const_ok, 1)

                def take(base):
                    v.wait_ge(full, base + k[0] + 1)

                def give(ins):
                    ins.then_inc(free, 1)
                    k[0] += 1

                take(0)
                give(cp(wall[:], psm[0:D + 1, 0:448]))
                v.wait_ge(r_load, 64)
                norm_groups(nc, v, ch, var, rstd, 1, h4[:], h4[:], tmp[:], stat, 4 * NA, D, EPS)
                ch.wait()
                cp(stat[:, 0, 0:1], stat[:, 1, 0:1]).then_inc(xn_ok, 1)
                for n in range(4):
                    for c in chunks:
                        take(0)
                        give(cp(xt[0:D, c[0] * P:c[1] * P], psm[0:D, 0:(c[1] - c[0]) * P]))
                    for c in chunks:
                        take(0)
                        give(cp(resid[:, c[0]:c[1], HD * n:HD * n + HD], psm[:, 0:(c[1] - c[0]) * HD].rearrange("p (a d) -> p a d", d=HD)))
                assert k[0] == JS
                n_setup = ch.n
                v.wait_ge(free, JS + 1)
                with v.Fori(0, B) as it:
                    k[0] = 0
                    base = it * J + JS
                    ch = Chain(v, dve, it * NDVE + n_setup)
                    v.wait_ge(h_load, it * 16 + 16)
                    ch.step(cp(tmp[:, NA:2 * NA, :], hb[:]))
                    norm_groups(nc, v, ch, var, rstd, it * 3 + 2, xn[:], tmp[:, NA:2 * NA, :], tmp[:, 0:NA, :], stat, NA, D, EPS)
                    cp(stat[:, 0, 0:1], stat[:, 1, 0:1]).then_inc(xn_ok, 1)
                    for kind, c in PRO:
                        take(base)
                        if kind == "turn":
                            give(cp(xt[0:D, c[0] * P:c[1] * P], psm[0:D, 0:(c[1] - c[0]) * P]))
                        elif kind == "tok":
                            pv = psm[:].rearrange("p (a s x) -> p a s x", s=2, x=D)[:, 0:c[1] - c[0]]
                            ch.done(cp(vop[:, c[0]:c[1], :, 0:HD], pv[:, :, 0, :].rearrange("p a (n d) -> p a n d", d=HD)))
                            give(ts(msk[:, c[0]:c[1], :], pv[:, :, 1, :], 0.0, None, ALU.not_equal))
                        else:
                            g, x = c
                            i = 3 * g + x
                            m = P if g < 2 else D
                            p0 = qs[:, 0, g, x * FB:(x + 1) * FB] if g < 2 else ks[:, 0, x * FB:(x + 1) * FB]
                            ch.step(cp(p0, psm[0:m, 0:FB]))
                            v.wait_ge(parts, it * 9 + i + 1)
                            give(tt(rq[0:m, i % 3, :], psm[0:m, 0:FB], p0, ALU.subtract))
                    sw = 0
                    for n in range(NH):
                        for i in range(NA):
                            for j in range(i + 1):
                                v.wait_ge(swept, it * SWEEP + sw + 1)
                                red(mpart[:, :, j:j + 1], pss[:, sw // 3 % 2, sw % 3, :].rearrange("p (e t) -> p e t", e=NE), AX.X, ALU.max).then_inc(swept_max, 1)
                                sw += 1
                            v.wait_ge(swept_max, it * SWEEP + sw + 6)
                            ch.step(red(mtok[:, i, NE * n:NE * n + NE], mpart[:, :, 0:i + 1], AX.X, ALU.max))
                    ch.step(cp(mtp[:, :, 0, :], mtok[:]))
                    ch.step(tt(mres[:], mtok[:], mtp[:, :, 0, :], ALU.subtract))
                    ch.step(cp(mtp[:, :, 1, :], mres[:]))
                    tt(mtp[:, :, 2, :], mres[:], mtp[:, :, 1, :], ALU.subtract).then_inc(used, 1)
                    for kind, c in MXJ:
                        take(base)
                        if c[0] == 0:
                            give(cp(mt[:, 0:8 * P], psmb[0:3 * HE, 0:8 * P]))
                        else:
                            give(cp(mt[:, 8 * P:], psmb[0:3 * HE, 0:P]))
                            v.wait_ge(free, base + k[0] + 1)
                            cp(stat[0:1, 1, 0:1], stat[0:1, 0, 0:1]).then_inc(max_split, 1)
                    for n in range(NH):
                        for x in range(3):
                            w = QT if x < 2 else LAST
                            if x == 0:
                                v.wait_ge(tile_done, it * NH + n + 1)
                            else:
                                v.wait_ge(summed, it * NUB + n * NU + last_unit[x] + 4)
                            cp(ofm[:, (3 * n + x) % 2, 0:w], pso[:, 0:w]).then_inc(acc_free, 1)
                            take(base)
                            c = (4 * x, min(4 * x + 4, NA))
                            dst = ot[:].rearrange("p (a n) e w -> p a n (e w)", n=NH)
                            if x < 2:
                                give(cp(dst[:, c[0]:c[1], n, :], psm[:].rearrange("p (a w) -> p a w", w=P)))
                            else:
                                give(cp(dst[0:LAST, NA - 1, n, :], psm[0:LAST, 0:P]))
                    v.wait_ge(free, base + k[0] + 1)
                    G = NA * NH
                    ch.step(nc.vector.reciprocal(rec[:], ot[:, :, :, HD]))
                    onv = on[:].rearrange("p g (e d) -> p g e d", d=HD)
                    ch.step(tt(onv, ot[:, :, :, 0:HD], bcast(rec[:], HD), ALU.mult))
                    ch.step(tt(onv, onv, bmid(msk[:].rearrange("p a (n d) -> p (a n) d", d=HD), NE), ALU.mult))
                    on4 = on[:].rearrange("p (a n) f -> p a n f", n=NH)
                    tm4 = tmp[:].rearrange("p (a n) f -> p a n f", n=NH)
                    gwv = gw[:].rearrange("p (n e f) -> p e n f", n=NH, f=64)
                    for e in range(NE):
                        for a in range(NA):
                            ch.done(tt(tm4[:, a], on4[:, a], gwv[:, e], ALU.mult))
                        ch.wait()
                        ch.step(red(lg[:, :, e:e + 1], tmp[:], AX.X, ALU.add))
                    ch.step(tt(lg[:].rearrange("p (a n) e -> p a (n e)", n=NH), lg[:].rearrange("p (a n) e -> p a (n e)", n=NH), bmid(gb[:], NA), ALU.add))
                    ch.step(red(mx[:], lg[:], AX.X, ALU.max))
                    tt(lg[:], lg[:], bcast(mx[:], NE), ALU.subtract).then_inc(logit, 1)
                    v.wait_ge(logit_exp, it + 1)
                    ch.step(red(mx[:], lg[:], AX.X, ALU.add))
                    ch.step(nc.vector.reciprocal(mx[:], mx[:]))
                    ch.step(tt(lg[:], lg[:], bcast(mx[:], NE), ALU.mult))
                    ch.step(tt(tmp[:].rearrange("p g (e d) -> p g e d", d=HD), onv, bcast(lg[:], HD), ALU.mult))
                    ch.step(red(mix[:], tmp[:].rearrange("p g (e d) -> p g d e", d=HD), AX.X, ALU.add))
                    ch.step(tt(mix[:], mix[:], resid[:].rearrange("p a (n d) -> p (a n) d", d=HD), ALU.add))
                    t16 = tmp[:, :, 0:HD]
                    norm_groups(nc, v, ch, var, rstd, it * 3 + 3, fx[:], mix[:], t16, stat, G, HD, FEPS)
                    ch.step(tt(fx[:], fx[:], bmid(vec[:, 0, :], G), ALU.mult))
                    tt(fx[:], fx[:], bmid(vec[:, 1, :], G), ALU.add).then_inc(fx_ok, 1)
                    for kind, c in EPI:
                        take(base)
                        if kind == "fturn":
                            give(cp(fxt[0:D, c[0] * P:c[1] * P], psm[0:D, 0:(c[1] - c[0]) * P]))
                        elif kind == "fc1":
                            s_ = slice(c * FB, (c + 1) * FB)
                            if c == 0:
                                v.wait_ge(free, base + k[0] + 1)
                                ch.step(ts(pm[:], fxt[0:D], 0.0, None, ALU.not_equal))
                            give(stt(hx1[0:D, s_], psm[0:D, 0:FB], 0.0, pm[:, s_], ALU.max, ALU.mult))
                        elif kind == "fc2":
                            s_ = slice(c * FB, (c + 1) * FB)
                            ch.step(tt(pm[:, s_], psm[0:D, 0:FB], pm[:, s_], ALU.mult))
                            give(tt(pm[:, s_], pm[:, s_], fxt[0:D, s_], ALU.add))
                        else:
                            give(cp(fo[:].rearrange("p (a n) d -> p a (n d)", n=NH)[:, c[0]:c[1], :], psm[:, 0:(c[1] - c[0]) * D].rearrange("p (a d) -> p a d", d=D)))
                    assert k[0] == J
                    v.wait_ge(free, base + k[0] + 1)
                    norm_groups(nc, v, ch, var, rstd, it * 3 + 4, fx[:], fo[:], t16, stat, G, HD, FEPS)
                    ch.step(tt(fx[:], fx[:], bmid(vec[:, 2, :], G), ALU.mult))
                    ch.step(tt(fx[:], fx[:], bmid(vec[:, 3, :], G), ALU.add))
                    fa = fx[:].rearrange("p (a n) d -> p a (n d)", n=NH)
                    for n in range(NH):
                        ch.step(tt(tmp[:, 0:NA, :], fa, bmid(fgw[:, n, :], NA), ALU.mult))
                        ch.step(red(gs[:, 0:NA, n:n + 1], tmp[:, 0:NA, :], AX.X, ALU.add))
                    gg = gs[:, 0:NA, :]
                    ch.step(red(mx[:, 0:NA], gg, AX.X, ALU.max))
                    tt(gg, gg, bcast(mx[:, 0:NA], NH), ALU.subtract).then_inc(logit, 1)
                    v.wait_ge(gate_exp, it + 1)
                    ch.step(red(mx[:, 0:NA], gg, AX.X, ALU.add))
                    ch.step(nc.vector.reciprocal(mx[:, 0:NA], mx[:, 0:NA]))
                    ch.step(tt(gg, gg, bcast(mx[:, 0:NA], NH), ALU.mult))
                    ch.step(tt(fx[:].rearrange("p (a n) d -> p a n d", n=NH), fx[:].rearrange("p (a n) d -> p a n d", n=NH), bcast(gg, HD), ALU.mult))
                    v.wait_ge(stored, it * 32 + 16)
                    tt(res[:], hb[:], fa, ALU.add).then_inc(result, 1)
                    assert ch.n == NDVE, ch.n


def consts():
    t = np.arange(PATCH)[None, :]
    f = np.arange(F)[:, None]
    w = 2 * np.pi * f * t / PATCH
    k = np.arange(KC * P) * (np.arange(KC * P) < KH)
    tan = np.tan(np.pi * k / L)
    both = np.concatenate([tan, -tan])
    m = (np.arange(KH)[:, None] * (L - 1 - np.arange(L))[None, :]) % L
    wt = np.where(np.arange(KH) == 0, 0.5, 1.0)[:, None] / L
    half = np.repeat([[1.0, 0.0, -1.0, 0.0], [-1.0, -1.0, 0.0, 0.0]], D, 0)
    c = {
        "c_dft": np.concatenate([np.cos(w), -np.sin(w)], 0) / np.sqrt(PATCH),
        "c_ident": np.eye(P),
        "c_fold": np.concatenate([np.eye(D), np.eye(D)], 0),
        "c_tanrow": both,
        "c_tancol": both.reshape(2 * KC, P).T,
        "c_halves": half,
        "c_cos": wt * np.cos(2 * np.pi * m / L),
        "c_sin": -wt * np.sin(2 * np.pi * m / L),
    }
    return {k: np.ascontiguousarray(v.astype(np.float32)) for k, v in c.items()}


def kernel(**inputs):
    import numpy as _np
    import concourse.bacc as _bacc
    from concourse import mybir as _mybir
    from concourse.bass_utils import run_bass_kernel_spmd as _run

    nc = _bacc.Bacc("TRN2", target_bir_lowering=False, num_devices=1)
    arrays, aps = {}, {}
    for name, a in {**inputs, **consts()}.items():
        a = _np.ascontiguousarray(a)
        arrays["in_" + name] = a
        aps[name] = nc.dram_tensor("in_" + name, a.shape, _mybir.dt.from_np(a.dtype), kind="ExternalInput").ap()
    out = nc.dram_tensor("out", (B, L, D), F32, kind="ExternalOutput").ap()
    h1 = nc.dram_tensor("h1", (B, LP, D), F32).ap()
    taps = nc.dram_tensor("taps", (D, KREV), F32).ap()
    h2 = nc.dram_tensor("h2", (B, LP, D), F32).ap()
    stage_embed(nc, aps, h1)
    stage_taps(nc, aps, taps)
    stage_ssm(nc, aps, h1, taps, h2)
    stage_ffn(nc, aps, h2, out)
    r = _run(nc, [arrays], core_ids=[0])
    return r.results[0]["out"]
```

```python
from contextlib import ExitStack

import numpy as np
import concourse.bass as bass
from concourse import mybir

F32 = mybir.dt.float32
BF16 = mybir.dt.bfloat16
I32 = mybir.dt.int32
ACT = mybir.ActivationFunctionType
ALU = mybir.AluOpType
AX = mybir.AxisListType
RMAX = bass.bass_isa.ReduceOp.max

P = 128
B, C, T, V = 8, 64, 128, 64
D = 64
PATCH, STRIDE = 16, 8
NP = (T + STRIDE - PATCH) // STRIDE + 1
F = PATCH // 2 + 1
TXT = 77
IMG = V * NP
L = IMG + TXT
NA = -(-L // P)
LP = NA * P
VOCAB, NOPS = 256, 64
NLEAF, NOP = 8, 7
EPS = 1e-5


def bcast(ap, n):
    return bass.AP(ap.tensor, ap.offset, [*[list(x) for x in ap.ap], [0, n]])


def bmid(ap, n):
    a = [list(x) for x in ap.ap]
    return bass.AP(ap.tensor, ap.offset, [*a[:-1], [0, n], a[-1]])


def rows(ap, n):
    return bass.AP(ap.tensor, ap.offset, [[0, n], *[list(x) for x in ap.ap]])


class Chain:

    def __init__(self, eng, sem, base=0):
        self.eng, self.sem, self.base, self.n = eng, sem, base, 0

    def done(self, ins):
        ins.then_inc(self.sem, 1)
        self.n += 1
        return self.n

    def wait(self, n=None):
        self.eng.wait_ge(self.sem, self.base + (self.n if n is None else n))

    def step(self, ins):
        self.done(ins)
        self.wait()


def stage_embed(nc, t, h1d):
    KB = PATCH * C // P // 2
    with ExitStack() as ctx:
        sb = lambda n, s, d=F32: ctx.enter_context(nc.sbuf_tensor(n, s, d))
        ps = lambda n, s: ctx.enter_context(nc.psum_tensor(n, s, F32))
        sem = lambda n: ctx.enter_context(nc.semaphore(n))
        wf = sb("wf", [2 * F, D, 2, C])
        dft = sb("dft", [2 * F, PATCH])
        g = sb("g", [P, KB, 2, D])
        ident = sb("ident", [P, P])
        fold = sb("fold", [P, D])
        x = sb("x", [P, 2, NP, KB * V])
        xe = sb("xe", [P, B, V])
        ye = sb("ye", [P, B, V])
        y = sb("y", [P, 2, V, NP])
        h = sb("h", [P, NA, B, D])
        comp = sb("comp", [P, 2, D])
        compc = sb("compc", [P, 2, D])
        compq = sb("compq", [P, 2, D])
        compt = sb("compt", [D, 2, P])
        opemb = sb("opemb", [NOPS, D])
        opt = sb("opt", [D, NOPS])
        w0 = sb("w0", [D, D])
        wlr = sb("wlr", [D, 2, D])
        w12 = sb("w12", [P, D])
        bb = sb("bb", [P, D])
        gam = sb("gam", [P, D])
        bet = sb("bet", [P, D])
        tlr = sb("tlr", [P, 2, 2, D])
        top = sb("top", [NOPS, D])
        ids = sb("ids", [TXT, B], I32)
        idf = sb("idf", [TXT, B])
        keep = sb("keep", [TXT, B])
        leaf = sb("leaf", [TXT, B, NLEAF], I32)
        opi = sb("opi", [TXT, B, NOP], I32)
        gl = sb("gl", [TXT, B, 4, D])
        gr = sb("gr", [TXT, B, 4, D])
        go = sb("go", [TXT, B, NOP, D])
        tx = sb("tx", [TXT, 32, D])
        tq = sb("tq", [TXT, 32, D])
        tt = sb("tt", [P, 16, TXT])
        st = sb("st", [P, 4, 32])
        mhalf = sb("mhalf", [P, 32])
        tl_d = nc.dram_tensor("tl_d", [VOCAB, D], F32).ap()
        tr_d = nc.dram_tensor("tr_d", [VOCAB, D], F32).ap()
        to_d = nc.dram_tensor("to_d", [NOPS, D], F32).ap()
        psy = ps("psy", [P, 2, 2, 512])
        pst = ps("pst", [P, 2, 512])
        psw = ps("psw", [P, 2, 512])

        s_w, s_txt, s_e, s_id = sem("weights_loaded"), sem("text_loaded"), sem("edges_loaded"), sem("ids_loaded")
        s_x = [sem("x0_loaded"), sem("x1_loaded")]
        g_ready, g_copied = sem("g_ready"), sem("g_copied")
        y_done = [sem("y0_done"), sem("y1_done")]
        lo_out = [sem("y0_low_copied"), sem("y1_low_copied")]
        hi_out = [sem("y0_high_copied"), sem("y1_high_copied")]
        t_done = [sem("t0_done"), sem("t1_done")]
        t_out = [sem("t0_copied"), sem("t1_copied")]
        h_out = sem("h_stored")
        ye_done, ye_out = sem("ye_done"), sem("ye_copied")
        dve = sem("vector_steps")
        pool_ready, pool_var, pool_r = sem("pool_ready"), sem("variance_ready"), sem("rstd_ready")
        tab_t, tab_tc, tab_m, tab_c, tab_s = sem("tab_turned"), sem("tab_turned_copied"), sem("tab_mult"), sem("tab_copied"), sem("tab_stored")
        s_rows = sem("id_rows")
        s_gath = sem("gathered")
        l_src, l_t, l_tc, l_m = sem("level_ready"), sem("level_turned"), sem("level_copied"), sem("level_mult")
        pad_z = sem("pad_zero")
        txt_ok = sem("text_done")
        comp_ready = sem("vocabulary_normed")

        wfv = t["L0_tok_W"].rearrange("d (f c) -> f d c", c=C)
        xv = t["x"].rearrange("b c (j u r) v -> b u c j (r v)", u=2, r=KB)
        lr = t["L0_txt_W_bin"].rearrange("(s k) d -> k s d", k=D)

        with nc.Block() as block:
            @block.sync
            def _(sp):
                for u in range(2):
                    sp.dma_start(wf[:, :, u, :], wfv).then_inc(s_w, 16)
                sp.dma_start(dft[:], t["c_dft"]).then_inc(s_w, 16)
                sp.dma_start(ident[:], t["c_ident"]).then_inc(s_w, 16)
                sp.dma_start(fold[:], t["c_fold"]).then_inc(s_w, 16)
                sp.dma_start(ids[:], t["x_txt"].rearrange("b k -> k b"), allow_slow_non_contiguous=True).then_inc(s_id, 16)
                for u in range(2):
                    sp.dma_start(xe[u * C:(u + 1) * C], t["x"][:, :, T - 1, :].rearrange("b c v -> c b v")).then_inc(s_e, 16)
                sp.dma_start(comp[:], t["L0_txt_comp_emb"].rearrange("(h p) d -> p h d", p=P)).then_inc(s_txt, 16)
                sp.dma_start(opemb[:], t["L0_txt_op_emb"]).then_inc(s_txt, 16)
                sp.dma_start(w0[:], t["L0_txt_W_bin"][0:D, :]).then_inc(s_txt, 16)
                sp.dma_start(wlr[:], lr[:, 1:3, :]).then_inc(s_txt, 16)
                sp.dma_start(w12[:], t["L0_txt_W_bin"][D:3 * D, :]).then_inc(s_txt, 16)
                sp.dma_start(bb[:], rows(t["L0_txt_b_bin"], P)).then_inc(s_txt, 16)
                sp.dma_start(gam[:], rows(t["L0_txt_gamma"], P)).then_inc(s_txt, 16)
                sp.dma_start(bet[:], rows(t["L0_txt_beta"], P)).then_inc(s_txt, 16)
                for k in range(2):
                    for q in (y_done, lo_out, hi_out, t_done, t_out):
                        sp.sem_inc(q[k], 1)
                with sp.Fori(0, B // 2) as it:
                    for k in range(2):
                        for u in range(2):
                            sp.wait_ge(y_done[k], it * 2 + 1)
                            sp.dma_start(x[u * C:(u + 1) * C, k], xv[it * 2 + k, u]).then_inc(s_x[k], 16)

            @block.tensor
            def _(pe):
                pe.wait_ge(s_w, 80)
                for d in range(D):
                    mm = pe.matmul(psw[:, d // 32, (d % 32) * PATCH:(d % 32 + 1) * PATCH], wf[:, d, :, :], dft[:], start=True, stop=True)
                mm.then_inc(g_ready, 1)
                pe.wait_ge(s_txt, 128)
                pe.wait_ge(comp_ready, 1)
                for v in range(2):
                    pe.transpose(pst[0:D, 0, v * P:(v + 1) * P], comp[:, v, :], ident[:])
                pe.transpose(pst[0:D, 0, 2 * P:2 * P + NOPS], opemb[:], ident[0:NOPS, 0:NOPS]).then_inc(tab_t, 1)
                pe.wait_ge(tab_tc, 2)
                for v in range(2):
                    pe.matmul(pst[:, 1, v * P:(v + 1) * P], compt[:, v, :], wlr[:], start=True, stop=True)
                pe.matmul(pst[0:NOPS, 1, 2 * P:2 * P + D], opt[:], w0[:], start=True, stop=True).then_inc(tab_m, 1)
                pe.wait_ge(g_copied, 4)
                pe.wait_ge(s_e, 32)
                for r in range(KB):
                    mm = pe.matmul(psw[:, 0, :], g[:, r], xe[:], start=(r == 0), stop=(r == KB - 1))
                mm.then_inc(ye_done, 1)
                pe.wait_ge(tab_c, 2)
                pe.wait_ge(ye_out, 1)
                with pe.Fori(0, B // 2) as it:
                    for k in range(2):
                        for j in range(2):
                            pe.wait_ge(s_x[k], it * 32 + 32)
                            pe.wait_ge(lo_out[k], it * 2 + 1)
                            pe.wait_ge(hi_out[k], it * 3 + 1)
                            for r in range(KB):
                                mm = pe.matmul(psy[:, k, j, :], g[:, r], x[:, k, 8 * j:8 * j + 8, r * V:(r + 1) * V], start=(r == 0), stop=(r == KB - 1))
                            mm.then_inc(y_done[k], 1)
                    for k in range(2):
                        pe.wait_ge(lo_out[k], it * 2 + 3)
                        pe.wait_ge(hi_out[k], it * 3 + 4)
                        pe.wait_ge(t_out[k], it + 1)
                        for a in range(8):
                            mm = pe.matmul(pst[:, k, a * D:(a + 1) * D], y[:, k, 8 * a:8 * a + 8, :], fold[:], start=True, stop=True)
                        mm.then_inc(t_done[k], 1)
                for lv, n in ((0, 16), (1, 8)):
                    pe.wait_ge(l_src, lv + 1)
                    for i in range(n):
                        mm = pe.transpose(psw[:, i // 4 % 2, (i % 4) * P:(i % 4) * P + TXT], tx[:, 2 * i:2 * i + 2, :], ident[0:TXT, 0:TXT])
                        if i % 4 == 3:
                            mm.then_inc(l_t, 1)
                            if i // 4 % 2 == 1 and i < n - 1:
                                pe.wait_ge(l_tc, 4 * lv + i // 4 + 1)
                    pe.wait_ge(l_tc, 4 * lv + n // 4)
                    for i in range(n):
                        mm = pe.matmul(pst[0:TXT, i // 8, (i % 8) * D:(i % 8 + 1) * D], tt[:, i, :], w12[:], start=True, stop=True)
                    mm.then_inc(l_m, 1)

            @block.scalar
            def _(act):
                act.wait_ge(ye_done, 1)
                act.wait_ge(tab_c, 2)
                act.dma_start(tl_d.rearrange("(h p) d -> p h d", p=P), tlr[:, :, 0, :]).then_inc(tab_s, 16)
                act.dma_start(tr_d.rearrange("(h p) d -> p h d", p=P), tlr[:, :, 1, :]).then_inc(tab_s, 16)
                act.dma_start(to_d, top[:]).then_inc(tab_s, 16)
                nc.scalar.copy(ye[:].rearrange("p b v -> p (b v)"), psw[:, 0, :]).then_inc(ye_out, 1)
                with act.Fori(0, B // 2) as it:
                    for k in range(2):
                        for j in range(2):
                            act.wait_ge(y_done[k], it * 2 + j + 2)
                            act.wait_ge(t_done[k], it + 1)
                            nc.scalar.copy(y[0:D, k, :, 8 * j:8 * j + 8], psy[0:D, k, j, :].rearrange("p (j v) -> p v j", v=V)).then_inc(lo_out[k], 1)
                for lv, n in ((0, 4), (1, 2)):
                    act.wait_ge(l_m, lv)
                    for i in range(n):
                        act.wait_ge(l_t, 4 * lv + i + 1)
                        nc.scalar.copy(tt[:, 4 * i:4 * i + 4, :], psw[:, i % 2, :].rearrange("p (q k) -> p q k", k=P)[:, :, 0:TXT]).then_inc(l_tc, 1)
                for k in range(2):
                    act.wait_ge(t_out[k], B // 2 + 1)
                act.wait_ge(txt_ok, 1)
                act.dma_start(h1d.rearrange("b (a p) d -> p a b d", p=P)[:, NA - 1], h[:, NA - 1]).then_inc(h_out, 16)
                with act.Fori(0, B) as b:
                    act.dma_start(h1d[b].rearrange("(a p) d -> p a d", p=P)[:, 0:8, :], h[:, 0:8, b, :]).then_inc(h_out, 16)
                act.wait_ge(h_out, 16 * (B + 1))

            @block.gpsimd
            def _(pool):
                pool.memset(mhalf[:], -0.5).then_inc(pool_ready, 1)
                pool.wait_ge(pool_ready, 1)
                pool.memset(h[64:128, NA - 1], 0.0).then_inc(pad_z, 1)
                pool.wait_ge(s_id, 16)
                for b in range(B):
                    pool.indirect_dma_start(leaf[:, b, :], None, t["L0_txt_leaf_ids"], bass.IndirectOffsetOnAxis(ap=ids[:, b:b + 1], axis=0)).then_inc(s_rows, 16)
                    pool.indirect_dma_start(opi[:, b, :], None, t["L0_txt_op_ids"], bass.IndirectOffsetOnAxis(ap=ids[:, b:b + 1], axis=0)).then_inc(s_rows, 16)
                pool.wait_ge(pad_z, 1)
                pool.wait_ge(pool_var, 1)
                pool.tensor_tensor(st[:, 3, 0:2], st[:, 2, 0:2], mhalf[:, 0:2], ALU.pow).then_inc(pool_r, 1)
                pool.wait_ge(tab_s, 48)
                pool.wait_ge(s_rows, 32 * B)
                for b in range(B):
                    for j in range(4):
                        pool.indirect_dma_start(gl[:, b, j, :], None, tl_d, bass.IndirectOffsetOnAxis(ap=leaf[:, b, 2 * j:2 * j + 1], axis=0)).then_inc(s_gath, 16)
                        pool.indirect_dma_start(gr[:, b, j, :], None, tr_d, bass.IndirectOffsetOnAxis(ap=leaf[:, b, 2 * j + 1:2 * j + 2], axis=0)).then_inc(s_gath, 16)
                    for j in range(NOP):
                        pool.indirect_dma_start(go[:, b, j, :], None, to_d, bass.IndirectOffsetOnAxis(ap=opi[:, b, j:j + 1], axis=0)).then_inc(s_gath, 16)
                for lv, n in enumerate((32, 16, 8)):
                    pool.wait_ge(pool_var, 2 + lv)
                    pool.tensor_tensor(st[0:TXT, 3, 0:n], st[0:TXT, 2, 0:n], mhalf[0:TXT, 0:n], ALU.pow).then_inc(pool_r, 1)

            @block.vector
            def _(v):
                ch = Chain(v, dve)

                def layer_norm(out, src, tmp, n, p, which, ready):
                    ch.step(nc.vector.tensor_reduce(st[0:p, 0, 0:n], src, AX.X, ALU.add))
                    ch.step(nc.vector.tensor_scalar(st[0:p, 1, 0:n], st[0:p, 0, 0:n], -1.0 / D, None, ALU.mult))
                    ch.step(nc.vector.tensor_tensor(src, src, bcast(st[0:p, 1, 0:n], D), ALU.add))
                    ch.step(nc.vector.tensor_tensor(tmp, src, src, ALU.mult))
                    ch.step(nc.vector.tensor_reduce(st[0:p, 0, 0:n], tmp, AX.X, ALU.add))
                    nc.vector.tensor_scalar(st[0:p, 2, 0:n], st[0:p, 0, 0:n], 1.0 / D, EPS, ALU.mult, ALU.add).then_inc(pool_var, 1)
                    v.wait_ge(pool_r, which)
                    ch.step(nc.vector.tensor_tensor(tmp, src, bcast(st[0:p, 3, 0:n], D), ALU.mult))
                    ch.step(nc.vector.tensor_tensor(tmp, tmp, bmid(gam[0:p], n), ALU.mult))
                    nc.vector.tensor_tensor(out, tmp, bmid(bet[0:p], n), ALU.add).then_inc(ready, 1)

                v.wait_ge(g_ready, 1)
                for u in range(2):
                    for q in range(2):
                        src = psw[u * C:(u + 1) * C, q, :].rearrange("p (d h w r) -> p w r h d", h=2, w=2, r=KB)[:, u]
                        for hf in range(2):
                            ins = nc.vector.tensor_copy(g[u * C:(u + 1) * C, :, hf, 32 * q:32 * q + 32], src[:, :, hf, :])
                        ins.then_inc(g_copied, 1)
                v.wait_ge(s_txt, 128)
                layer_norm(comp[:], comp[:], compq[:], 2, P, 1, comp_ready)
                v.wait_ge(tab_t, 1)
                nc.vector.tensor_copy(compt[:], pst[0:D, 0, 0:2 * P].rearrange("p (h k) -> p h k", k=P)).then_inc(tab_tc, 1)
                nc.vector.tensor_copy(opt[:], pst[0:D, 0, 2 * P:2 * P + NOPS]).then_inc(tab_tc, 1)
                v.wait_ge(tab_m, 1)
                nc.vector.tensor_copy(tlr[:].rearrange("p h s d -> p (h s d)"), pst[:, 1, 0:2 * P]).then_inc(tab_c, 1)
                nc.vector.tensor_tensor(top[:], pst[0:NOPS, 1, 2 * P:2 * P + D], bb[0:NOPS], ALU.add).then_inc(tab_c, 1)
                with v.Fori(0, B // 2) as it:
                    for k in range(2):
                        hi = slice(D, P)
                        src = psy[hi, k].rearrange("p q (j v) -> p v (q j)", v=V)
                        for j in range(2):
                            v.wait_ge(y_done[k], it * 2 + j + 2)
                            v.wait_ge(t_done[k], it + 1)
                            if j == 0:
                                nc.vector.tensor_copy(y[hi, k, :, 0:7], src[:, :, 1:8]).then_inc(hi_out[k], 1)
                            else:
                                nc.vector.tensor_copy(y[hi, k, :, 7:15], src[:, :, 8:16]).then_inc(hi_out[k], 1)
                        v.wait_ge(ye_out, 1)
                        nc.vector.tensor_copy(y[hi, k, :, 15], ye[hi, it * 2 + k, :]).then_inc(hi_out[k], 1)
                    for k in range(2):
                        v.wait_ge(t_done[k], it + 2)
                        nc.vector.tensor_copy(h[:, 0:8, it * 2 + k, :], pst[:, k, :].rearrange("p (a d) -> p a d", d=D)).then_inc(t_out[k], 1)
                v.wait_ge(s_gath, 16 * B * 15)
                v.wait_ge(s_id, 16)
                ch.step(nc.vector.tensor_copy(idf[:], ids[:]))
                ch.step(nc.vector.tensor_scalar(keep[:], idf[:], 1.0, None, ALU.is_gt))
                txv = tx[:].rearrange("p (b j) d -> p b j d", b=B)
                ch.step(nc.vector.tensor_tensor(gl[:], gl[:], gr[:], ALU.add))
                ch.step(nc.vector.tensor_tensor(gl[:], gl[:], go[:, :, 0:4, :], ALU.add))
                layer_norm(tx[:], gl[:].rearrange("p b j d -> p (b j) d"), tq[:], 32, TXT, 2, l_src)
                for lv, (n, off) in enumerate(((16, 4), (8, 6))):
                    v.wait_ge(l_m, lv + 1)
                    m = n // B
                    for q in range(n // 8):
                        bs = slice(q * 8 // m, (q + 1) * 8 // m)
                        ch.step(nc.vector.tensor_tensor(
                            tx[:, 8 * q:8 * q + 8, :].rearrange("p (b j) d -> p b j d", j=m),
                            pst[0:TXT, q, :].rearrange("p (b j d) -> p b j d", j=m, d=D),
                            go[:, bs, off:off + m, :], ALU.add))
                    layer_norm(tx[:, 0:n], tx[:, 0:n], tq[:, 0:n], n, TXT, 3 + lv, l_src)
                v.wait_ge(l_src, 3)
                v.wait_ge(pad_z, 1)
                nc.vector.tensor_tensor(h[0:TXT, NA - 1], tx[:, 0:B], bcast(keep[:], D), ALU.mult).then_inc(txt_ok, 1)


KH = (L + 1) // 2
KC = -(-KH // P)
KREV = LP + P
AP_ = NA + 3
NT = NA // 3
HC = 4
FT = 3
FW = L // FT


def norm_rows(nc, v, ch, pool_var, pool_r, which, out, src, tmp, stat, n, p=P, cut=None):
    fold = (lambda x: x.rearrange("p (a b) -> p a b", b=cut)) if cut else (lambda x: x)
    ch.step(nc.vector.tensor_reduce(stat[0:p, 0, 0:n], src, AX.X, ALU.add))
    ch.step(nc.vector.tensor_scalar(stat[0:p, 1, 0:n], stat[0:p, 0, 0:n], -1.0 / D, None, ALU.mult))
    ch.step(nc.vector.tensor_tensor(src, src, bcast(stat[0:p, 1, 0:n], D), ALU.add))
    ch.step(nc.vector.tensor_tensor(tmp, src, src, ALU.mult))
    ch.step(nc.vector.tensor_reduce(stat[0:p, 0, 0:n], tmp, AX.X, ALU.add))
    nc.vector.tensor_scalar(stat[0:p, 2, 0:n], stat[0:p, 0, 0:n], 1.0 / D, EPS, ALU.mult, ALU.add).then_inc(pool_var, 1)
    v.wait_ge(pool_r, which)
    return ch.done(nc.vector.tensor_tensor(out, *((x.rearrange("p (a b) d -> p a b d", b=cut) if cut else x) for x in (src,)), bcast(fold(stat[0:p, 3, 0:n]), D), ALU.mult))


def stage_taps(nc, t, krev_d):
    NC2 = 2 * KC
    H1 = D + 1
    with ExitStack() as ctx:
        sb = lambda n, s, d=F32: ctx.enter_context(nc.sbuf_tensor(n, s, d))
        ps = lambda n, s: ctx.enter_context(nc.psum_tensor(n, s, F32))
        sem = lambda n: ctx.enter_context(nc.semaphore(n))
        ident = sb("t_ident", [P, P])
        cq = sb("cq", [H1, 2, D])
        cqs = sb("cqs", [H1, 2, D])
        ct = sb("ct", [P, 2, H1])
        cols = sb("cols", [P, 6])
        sc = sb("sc", [P, 16])
        kon = sb("kon", [P, 4])
        tanr = sb("tanr", [P, NC2, P])
        tanc = sb("tanc", [P, NC2])
        cosb = sb("cosb", [P, KC, L])
        sinb = sb("sinb", [P, KC, L])
        stepv = sb("stepv", [P, 1])
        dval = sb("dval", [D, 1])
        w = sb("w", [P, NC2, P])
        den = sb("den", [P, NC2, P])
        inv = sb("inv", [P, NC2, P])
        coef = sb("coef", [P, 4, H1])
        tmp = sb("tmp", [P, H1])
        k4 = sb("k4", [P, NC2, 4, H1])
        sm = sb("sm", [P, 8, NC2])
        t1 = sb("t1", [P, NC2, D])
        t2 = sb("t2", [P, NC2, D])
        dr = sb("dr", [P, NC2, D])
        di = sb("di", [P, NC2, D])
        ar = sb("ar", [P, NC2, D])
        ai = sb("ai", [P, NC2, D])
        ev = sb("ev", [P, KC, D])
        od = sb("od", [P, KC, D])
        kr = sb("kr", [D, KREV])
        psc = ps("psc_t", [P, 512])
        psk = ps("psk", [P, 4, 512])
        pso = ps("pso", [P, FT, 512])
        s_c, s_s, s_t, s_tab = sem("c_loaded"), sem("scalars_loaded"), sem("tan_loaded"), sem("tables_loaded")
        turned, dve, inv_ok = sem("c_turned"), sem("tap_steps"), sem("inv_ready")
        kdone, kout, ev_ok, taps, stored = sem("k_done"), sem("k_copied"), sem("spectrum_ready"), sem("taps_done"), sem("taps_stored")
        kr_ok = sem("taps_ready")

        with nc.Block() as block:
            @block.sync
            def _(sp):
                for i, (n, q) in enumerate((("L0_attn_C", "L0_attn_Q"), )):
                    for u, part in enumerate(("_re", "_im")):
                        for dst, w_ in ((cq, u), (cqs, 1 - u)):
                            sp.dma_start(dst[0:D, w_, :], t[n + part]).then_inc(s_c, 16)
                            sp.dma_start(dst[D:H1, w_, :], rows(t[q + part], 1)).then_inc(s_c, 16)
                sp.dma_start(ident[:], t["c_ident"]).then_inc(s_c, 16)
                for i, n in enumerate(("B_re", "B_im", "P_re", "P_im", "Lambda_re", "Lambda_im")):
                    for u in range(2):
                        sp.dma_start(cols[u * D:(u + 1) * D, i:i + 1], t["L0_attn_" + n].rearrange("(n o) -> n o", o=1), allow_slow_non_contiguous=True).then_inc(s_s, 16)
                sp.dma_start(kon[:], t["c_halves"]).then_inc(s_s, 16)
                sp.dma_start(stepv[:], rows(t["L0_attn_step"], P)).then_inc(s_s, 16)
                sp.dma_start(dval[:], rows(t["L0_attn_D"], D)).then_inc(s_s, 16)
                sp.dma_start(tanc[:], t["c_tancol"]).then_inc(s_s, 16)
                sp.dma_start(tanr[:].rearrange("p c k -> p (c k)"), rows(t["c_tanrow"], P)).then_inc(s_t, 16)
                for dst, n in ((cosb, "c_cos"), (sinb, "c_sin")):
                    sp.dma_start(dst[:, 0:KC - 1], t[n][0:(KC - 1) * P].rearrange("(c p) l -> p c l", p=P)).then_inc(s_tab, 16)
                    sp.dma_start(dst[0:KH - (KC - 1) * P, KC - 1], t[n][(KC - 1) * P:KH]).then_inc(s_tab, 16)
                sp.wait_ge(kr_ok, 1)
                sp.dma_start(krev_d, kr[:]).then_inc(stored, 16)
                sp.wait_ge(stored, 16)

            @block.tensor
            def _(pe):
                pe.wait_ge(s_c, 16 * 9)
                pe.transpose(psc[:, 0:H1], cq[:], ident[0:H1, 0:H1])
                pe.transpose(psc[:, P:P + H1], cqs[:], ident[0:H1, 0:H1]).then_inc(turned, 1)
                pe.wait_ge(inv_ok, 1)
                for c in range(NC2):
                    if c >= 4:
                        pe.wait_ge(kout, c - 3)
                    pe.matmul(psk[:, c % 4, 0:4 * H1], inv[:, c, :], coef[:], start=True, stop=True).then_inc(kdone, 1)
                pe.wait_ge(ev_ok, 1)
                pe.wait_ge(s_tab, 64)
                for f in range(FT):
                    for c in range(KC):
                        kc = min(P, KH - c * P)
                        for src, tab in ((ev, cosb), (od, sinb)):
                            mm = pe.matmul(pso[0:D, f, 0:FW], src[0:kc, c, :], tab[0:kc, c, f * FW:(f + 1) * FW], start=(c == 0 and src is ev), stop=(c == KC - 1 and src is od))
                    mm.then_inc(taps, 1)

            @block.scalar
            def _(act):
                for c in range(NC2):
                    act.wait_ge(kdone, c + 1)
                    nc.scalar.copy(k4[:, c].rearrange("p q h -> p (q h)"), psk[:, c % 4, 0:4 * H1]).then_inc(kout, 1)

            @block.vector
            def _(v):
                ch = Chain(v, dve)
                one, st = ch.step, nc.vector.scalar_tensor_tensor
                ts, tt = nc.vector.tensor_scalar, nc.vector.tensor_tensor
                v.wait_ge(s_s, 16 * 16)
                one(ts(sc[:, 0:1], stepv[:], 1e-6, None, ALU.max))
                one(nc.vector.reciprocal(sc[:, 1:2], sc[:, 0:1]))
                one(ts(sc[:, 2:3], sc[:, 1:2], 2.0, None, ALU.mult))
                one(tt(sc[:, 3:4], cols[:, 4:5], cols[:, 4:5], ALU.mult))
                one(tt(sc[:, 4:5], cols[:, 4:5], kon[:, 2:3], ALU.mult))
                for q in range(2):
                    one(ts(sc[:, 5 + 4 * q:6 + 4 * q], cols[:, 2 * q:2 * q + 1], kon[:, 0:1], None, ALU.mult))
                    one(ts(sc[:, 6 + 4 * q:7 + 4 * q], cols[:, 2 * q + 1:2 * q + 2], -1.0, None, ALU.mult))
                    one(ts(sc[:, 7 + 4 * q:8 + 4 * q], cols[:, 2 * q + 1:2 * q + 2], kon[:, 0:1], None, ALU.mult))
                v.wait_ge(turned, 1)
                one(nc.vector.tensor_copy(ct[:, 0, :], psc[:, 0:H1]))
                one(nc.vector.tensor_copy(ct[:, 1, :], psc[:, P:P + H1]))
                for q in range(2):
                    one(ts(tmp[:], ct[:, 1], sc[:, 6 + 4 * q:7 + 4 * q], None, ALU.mult))
                    one(st(coef[:, 2 * q], ct[:, 0], sc[:, 5 + 4 * q:6 + 4 * q], tmp[:], ALU.mult, ALU.add))
                    one(ts(tmp[:], ct[:, 1], cols[:, 2 * q:2 * q + 1], None, ALU.mult))
                    one(st(coef[:, 2 * q + 1], ct[:, 0], sc[:, 7 + 4 * q:8 + 4 * q], tmp[:], ALU.mult, ALU.add))
                v.wait_ge(s_t, 16)
                one(ts(w[:], tanr[:], sc[:, 2:3], cols[:, 5:6], ALU.mult, ALU.subtract))
                one(tt(den[:], w[:], w[:], ALU.mult))
                one(ts(den[:], den[:], sc[:, 3:4], None, ALU.add))
                one(nc.vector.reciprocal(den[:], den[:]))
                one(ts(w[:], w[:], kon[:, 1:2], sc[:, 4:5], ALU.mult, ALU.add))
                tt(inv[:], w[:], den[:], ALU.mult).then_inc(inv_ok, 1)
                v.wait_ge(kout, NC2)
                q10r, q10i, q11r, q11i = (k4[:, :, q, D] for q in range(4))
                S = lambda i: sm[:, i, :]
                one(ts(S(0), q11r, 1.0, None, ALU.add))
                one(tt(S(1), S(0), S(0), ALU.mult))
                one(tt(S(2), q11i, q11i, ALU.mult))
                one(tt(S(1), S(1), S(2), ALU.add))
                one(nc.vector.reciprocal(S(1), S(1)))
                one(tt(S(2), q10r, S(0), ALU.mult))
                one(tt(S(3), q10i, q11i, ALU.mult))
                one(tt(S(2), S(2), S(3), ALU.add))
                one(tt(S(4), S(2), S(1), ALU.mult))
                one(tt(S(2), q10i, S(0), ALU.mult))
                one(tt(S(3), q10r, q11i, ALU.mult))
                one(tt(S(2), S(2), S(3), ALU.subtract))
                one(tt(S(5), S(2), S(1), ALU.mult))
                wr, wi = bcast(S(4), D), bcast(S(5), D)
                k00r, k00i, k01r, k01i = (k4[:, :, q, 0:D] for q in range(4))
                one(tt(t1[:], k01r, wr, ALU.mult))
                one(tt(t2[:], k01i, wi, ALU.mult))
                one(tt(t1[:], t1[:], t2[:], ALU.subtract))
                one(tt(dr[:], k00r, t1[:], ALU.subtract))
                one(tt(t1[:], k01r, wi, ALU.mult))
                one(tt(t2[:], k01i, wr, ALU.mult))
                one(tt(t1[:], t1[:], t2[:], ALU.add))
                one(tt(di[:], k00i, t1[:], ALU.subtract))
                tb = bcast(tanc[:], D)
                one(tt(t1[:], di[:], tb, ALU.mult))
                one(tt(ar[:], dr[:], t1[:], ALU.subtract))
                one(tt(t1[:], dr[:], tb, ALU.mult))
                one(tt(ai[:], di[:], t1[:], ALU.add))
                one(tt(ev[:], ar[:, 0:KC], ar[:, KC:], ALU.add))
                tt(od[:], ai[:, 0:KC], ai[:, KC:], ALU.subtract).then_inc(ev_ok, 1)
                one(nc.vector.memset(kr[:], 0.0))
                for f in range(FT):
                    v.wait_ge(taps, f + 1)
                    o = LP - L + f * FW
                    one(nc.vector.tensor_copy(kr[:, o:o + FW], pso[0:D, f, 0:FW]))
                tt(kr[:, LP - 1:LP], kr[:, LP - 1:LP], dval[:], ALU.add).then_inc(kr_ok, 1)


def stage_ssm(nc, t, h1d, krev_d, h2d):
    NG = NA * B
    with ExitStack() as outer:
        sbo = lambda n, s, d=F32: outer.enter_context(nc.sbuf_tensor(n, s, d))
        yc = sbo("yc", [NT * 32, P, D])
        with ExitStack() as ctx:
            sb = lambda n, s, d=F32: ctx.enter_context(nc.sbuf_tensor(n, s, d))
            ps = lambda n, s: ctx.enter_context(nc.psum_tensor(n, s, F32))
            sem = lambda n: ctx.enter_context(nc.semaphore(n))
            hh = sb("hh", [P, NG, D])
            sq = sb("sq", [P, NG, D])
            stat = sb("stat", [P, 4, NG])
            mh = sb("mh", [P, NG])
            ut = sb("ut", [P, D, AP_, B])
            ub = sb("ub", [P, 2, HC, AP_ * B])
            tz = sb("tz", [P, 2 * HC, LP])
            psc = ps("psc", [P, 2, HC, P])
            s_h, dve, pv, pr, u_ok = sem("h_loaded"), sem("u_steps"), sem("u_var"), sem("u_rstd"), sem("u_ready")
            s_tz = [sem(f"taps{k}_loaded") for k in range(2 * HC)]
            ub_ok = [sem("u0_copied"), sem("u1_copied")]
            cdone = [sem(f"conv{k}_done") for k in range(2 * HC)]
            cout = [sem("conv0_copied"), sem("conv1_copied")]
            mh_ok, zero_ok = sem("mh_ready"), sem("zero_ready")
            with nc.Block() as block:
                @block.sync
                def _(sp):
                    for b in range(B):
                        sp.dma_start(hh[:].rearrange("p (a b) d -> p b a d", b=B)[:, b], h1d[b].rearrange("(a p) d -> p a d", p=P)).then_inc(s_h, 16)
                    for k in range(2 * HC):
                        sp.sem_inc(cdone[k], 1)
                    for k in range(2):
                        sp.sem_inc(cout[k], 1)
                    with sp.Fori(0, D // (2 * HC)) as it:
                        for k in range(2 * HC):
                            sp.wait_ge(cdone[k], it + 1)
                            c0 = it * (2 * HC) + k
                            sp.dma_start(tz[:, k, :], bass.AP(krev_d.tensor, krev_d.offset + c0 * KREV, [[1, P], [1, LP]])).then_inc(s_tz[k], 16)

                @block.tensor
                def _(pe):
                    with pe.Fori(0, D // (2 * HC)) as it:
                        for k in range(2 * HC):
                            g, c = divmod(k, HC)
                            if c == 0:
                                pe.wait_ge(ub_ok[g], it + 1)
                                pe.wait_ge(cout[g], it + 1)
                            pe.wait_ge(s_tz[k], it * 16 + 16)
                            for dl in range(NA):
                                for i in range(dl // 3, NT):
                                    o = (3 * i + 2 - dl) * B
                                    mm = pe.matmul(psc[32 * i:32 * i + 32, g, c, :], ub[:, g, c, o:o + 32], tz[:, k, LP - P - P * dl:LP - P * dl],
                                                   start=(dl == 0), stop=(dl == 3 * i + 2), skip_group_check=True)
                            mm.then_inc(cdone[k], 1)

                @block.scalar
                def _(act):
                    with act.Fori(0, D // (2 * HC)) as it:
                        for g in range(2):
                            act.wait_ge(cdone[g * HC + HC - 1], it + 2)
                            c0 = it * (2 * HC) + g * HC
                            nc.scalar.copy(yc[:, :, bass.ds(c0, HC)].rearrange("r p c -> r c p"), psc[0:NT * 32, g]).then_inc(cout[g], 1)

                @block.gpsimd
                def _(pool):
                    pool.memset(mh[:], -0.5).then_inc(mh_ok, 1)
                    pool.wait_ge(mh_ok, 1)
                    pool.wait_ge(pv, 1)
                    pool.tensor_tensor(stat[:, 3], stat[:, 2], mh[:], ALU.pow).then_inc(pr, 1)

                @block.vector
                def _(v):
                    ch = Chain(v, dve)
                    ch.done(nc.vector.memset(ut[:, :, 0:2, :], 0.0))
                    ch.step(nc.vector.memset(ut[:, :, AP_ - 1:AP_, :], 0.0))
                    v.wait_ge(s_h, 16 * B)
                    norm_rows(nc, v, ch, pv, pr, 1, ut[:, :, 2:2 + NA, :].rearrange("p d a b -> p a b d"),
                              hh[:], sq[:], stat, NG, cut=B)
                    ch.wait()
                    with v.Fori(0, D // (2 * HC)) as it:
                        for g in range(2):
                            v.wait_ge(cdone[g * HC + HC - 1], it + 1)
                            c0 = it * (2 * HC) + g * HC
                            nc.vector.tensor_copy(ub[:, g].rearrange("p c a -> p (c a)"), ut[:, bass.ds(c0, HC)].rearrange("p c a b -> p (c a b)")).then_inc(ub_ok[g], 1)

        with ExitStack() as ctx:
            sb = lambda n, s, d=F32: ctx.enter_context(nc.sbuf_tensor(n, s, d))
            ps = lambda n, s: ctx.enter_context(nc.psum_tensor(n, s, F32))
            sem = lambda n: ctx.enter_context(nc.semaphore(n))
            ident = sb("f_ident", [P, P])
            wfc = sb("wfc", [D, 2, D])
            wb = sb("wb", [P, 2, D])
            bfc = sb("bfc", [P, D])
            lng = sb("lng", [P, D])
            lnb = sb("lnb", [P, D])
            y1 = sb("y1", [P, NT * 32, P // 2])
            hl = sb("hl", [P, NG, D])
            uc = sb("uc", [P, NG, D])
            ul = sb("ul", [P, NG, D])
            z = sb("z", [P, NG, D])
            stat = sb("fstat", [P, 4, NG])
            mh = sb("fmh", [P, NG])
            pst = ps("f_pst", [P, 2, 4, P])
            psf = ps("psf", [P, 3, 512])
            psw = ps("f_psw", [P, 512])
            s_w, s_h, dve, pv, pr = sem("fc_loaded"), sem("hl_loaded"), sem("fc_steps"), sem("fc_var"), sem("fc_rstd")
            wt, wb_ok, turned, y1_ok, fdone, zadd, zg, h_ok, h_out, mh_ok = (sem(x) for x in (
                "w_turned", "w_ready", "y_turned", "y1_ready", "fc_done", "fc_bias", "fc_gelu", "h2_ready", "h2_stored", "fmh_ready"))
            view = lambda x, b: x[b].rearrange("(a p s) d -> p a (s d)", p=P // 2, s=2)
            grp = lambda x, b: x[64 * (b % 2):64 * (b % 2) + 64].rearrange("p (a q s) d -> p q a (s d)", q=B // 2, s=2)[:, b // 2]
            with nc.Block() as block:
                @block.sync
                def _(sp):
                    sp.dma_start(ident[:], t["c_ident"]).then_inc(s_w, 16)
                    for u in range(2):
                        sp.dma_start(wfc[:, u, :], t["L0_attn_W_fc"]).then_inc(s_w, 16)
                    sp.dma_start(bfc[:], rows(t["L0_attn_b_fc"], P)).then_inc(s_w, 16)
                    sp.dma_start(lng[:], rows(t["L0_attn_ln_g"], P)).then_inc(s_w, 16)
                    sp.dma_start(lnb[:], rows(t["L0_attn_ln_b"], P)).then_inc(s_w, 16)
                    for b in range(B):
                        sp.dma_start(grp(hl, b), view(h1d, b)).then_inc(s_h, 16)
                    sp.wait_ge(h_ok, 1)
                    for b in range(B):
                        sp.dma_start(view(h2d, b), grp(z, b)).then_inc(h_out, 16)
                    sp.wait_ge(h_out, 16 * B)

                @block.tensor
                def _(pe):
                    pe.wait_ge(s_w, 96)
                    pe.transpose(psw[:, 0:D], wfc[:], ident[0:D, 0:D]).then_inc(wt, 1)
                    for g in range(16):
                        if g >= 2:
                            pe.wait_ge(y1_ok, g - 1)
                        for s in range(4):
                            pr_ = P // 2 - 1 - (4 * g + s)
                            mm = pe.transpose(pst[:, g % 2, s, 0:NT * 32], yc[:, 2 * pr_:2 * pr_ + 2, :], ident[0:NT * 32, 0:NT * 32])
                        mm.then_inc(turned, 1)
                    pe.wait_ge(wb_ok, 1)
                    pe.wait_ge(y1_ok, 16)
                    for a in range(NA):
                        if a >= 3:
                            pe.wait_ge(zadd, a - 2)
                        for q in range(B // 2):
                            r0 = 32 * (a // 3) + B * (a % 3) + 2 * q
                            mm = pe.matmul(psf[:, a % 3, q * P:(q + 1) * P], y1[:, r0:r0 + 2, :], wb[:], start=True, stop=True)
                        mm.then_inc(fdone, 1)

                @block.scalar
                def _(act):
                    for g in range(16):
                        act.wait_ge(turned, g + 1)
                        nc.scalar.activation(y1[:, :, 4 * g:4 * g + 4].rearrange("p r s -> p s r"), pst[:, g % 2, :, 0:NT * 32], ACT.Gelu).then_inc(y1_ok, 1)
                    for a in range(NA):
                        act.wait_ge(zadd, a + 1)
                        zz = z[:, 8 * a:8 * a + 8, :]
                        nc.scalar.activation(zz, zz, ACT.Gelu).then_inc(zg, 1)

                @block.gpsimd
                def _(pool):
                    pool.memset(mh[:], -0.5).then_inc(mh_ok, 1)
                    pool.wait_ge(mh_ok, 1)
                    for i in range(2):
                        pool.wait_ge(pv, i + 1)
                        pool.tensor_tensor(stat[:, 3], stat[:, 2], mh[:], ALU.pow).then_inc(pr, 1)

                @block.vector
                def _(v):
                    ch = Chain(v, dve)
                    ch.step(nc.vector.memset(wb[:], 0.0))
                    v.wait_ge(wt, 1)
                    ch.done(nc.vector.tensor_copy(wb[0:D, 1, :], psw[0:D, 0:D]))
                    nc.vector.tensor_copy(wb[D:P, 0, :], psw[D:P, 0:D]).then_inc(wb_ok, 1)
                    v.wait_ge(s_h, 16 * B)
                    ch.step(nc.vector.tensor_copy(uc[:], hl[:]))
                    norm_rows(nc, v, ch, pv, pr, 1, ul[:], uc[:], z[:], stat, NG)
                    ch.wait()
                    for a in range(NA):
                        v.wait_ge(fdone, a + 1)
                        nc.vector.tensor_tensor(z[:, 8 * a:8 * a + 8, :], psf[:, a % 3, :].rearrange("p (g d) -> p g d", d=D), bmid(bfc[:], 8), ALU.add).then_inc(zadd, 1)
                    v.wait_ge(zg, NA)
                    ch.step(nc.vector.tensor_tensor(z[:], z[:], ul[:], ALU.add))
                    norm_rows(nc, v, ch, pv, pr, 2, uc[:], z[:], ul[:], stat, NG)
                    ch.wait()
                    ch.step(nc.vector.tensor_tensor(uc[:], uc[:], bmid(lng[:], NG), ALU.mult))
                    ch.step(nc.vector.tensor_tensor(uc[:], uc[:], bmid(lnb[:], NG), ALU.add))
                    nc.vector.tensor_tensor(z[:], hl[:], uc[:], ALU.add).then_inc(h_ok, 1)


NH, NE, HD = 4, 4, 16
HE = NH * NE
FEPS = 1e-8
TERMS_Q = (0, 1, 0, 2, 0, 1)
TERMS_K = (0, 0, 1, 0, 2, 1)
KT = HD * len(TERMS_Q)
KM = KT + 3
VW = 32
QT = 512
UB = 3
LAST = L - (NA - 1) * P
FB = 384


def score_units():
    banks = []
    for tile in range(2):
        for j in range(4 * tile):
            banks += [[(0, j, e, QT * tile, QT)] for e in range(NE)]
        d = lambda i, e, c: (c, 4 * tile + i, e, QT * tile + P * i, QT - P * i)
        banks += [[d(0, e, 0)] for e in range(NE)]
        banks += [[d(1, e, 0), d(3, e, 384)] for e in range(NE)]
        banks += [[d(2, e, 0), d(2, e + 1, 256)] for e in (0, 2)]
    for j in range(NA):
        banks.append([(0, j, None, 2 * QT, LAST)])
    return [banks[i:i + UB] for i in range(0, len(banks), UB)]


def norm_groups(nc, v, ch, pool_var, pool_r, which, out, src, tmp, stat, n, d, eps):
    ch.step(nc.vector.tensor_reduce(stat[:, 0, 0:n], src, AX.X, ALU.add))
    ch.step(nc.vector.tensor_scalar(stat[:, 1, 0:n], stat[:, 0, 0:n], -1.0 / d, None, ALU.mult))
    ch.step(nc.vector.tensor_tensor(src, src, bcast(stat[:, 1, 0:n], d), ALU.add))
    ch.step(nc.vector.tensor_tensor(tmp, src, src, ALU.mult))
    ch.step(nc.vector.tensor_reduce(stat[:, 0, 0:n], tmp, AX.X, ALU.add))
    nc.vector.tensor_scalar(stat[:, 2, 0:n], stat[:, 0, 0:n], 1.0 / d, eps, ALU.mult, ALU.add).then_inc(pool_var, 1)
    v.wait_ge(pool_r, which)
    ch.step(nc.vector.tensor_tensor(out, src, bcast(stat[:, 3, 0:n], d), ALU.mult))


def stage_ffn_exact(nc, t, h2d, out, flag_d):
    units = score_units()
    NU = len(units)
    NDVE = 141
    qk_d = nc.dram_tensor("qk_parts", (3, 2 * P + D, LP), BF16).ap()
    xsrc = lambda b: h2d[b].rearrange("(a p) d -> p a d", p=P)
    with ExitStack() as ctx:
        sb = lambda n, s, d=F32: ctx.enter_context(nc.sbuf_tensor(n, s, d))
        ps = lambda n, s, d=F32: ctx.enter_context(nc.psum_tensor(n, s, d))
        sem = lambda n: ctx.enter_context(nc.semaphore(n))
        ident = sb("a_ident", [P, P])
        identb = sb("a_identb", [P, P], BF16)
        maskb = sb("maskb", [P, P], BF16)
        maskf = sb("maskf", [P, P])
        wha = sb("wha", [NH * HD, D + 1])
        wbd = sb("wbd", [NH * HD, 448])
        wall = sb("wall", [D + 1, 448])
        fcw = sb("fcw", [D + 1, 2, D])
        gw = sb("gw", [P, HE * 64])
        gb = sb("gb", [P, HE])
        fgw = sb("fgw", [P, NH, D])
        vec = sb("vec", [P, 4, HD])
        resid = sb("resid", [P, NA, D])
        h4 = sb("h4", [P, 4 * NA, D])
        hb = sb("hb", [P, NA, D])
        xn = sb("xn", [P, NA, D])
        tmp = sb("a_tmp", [P, 4 * NA, D])
        stat = sb("a_stat", [P, 4, 4 * NA])
        mh = sb("a_mh", [P, 4 * NA])
        xt = sb("xt", [D + 1, LP])
        qs = sb("qs", [P, 3, 2, LP], BF16)
        ks = sb("ks", [D, 3, LP], BF16)
        rq = sb("rq", [P, 3, FB])
        qop = sb("qop", [KM, NH, NE, LP], BF16)
        kop = sb("kop", [KM, NH, LP], BF16)
        vop = sb("vop", [P, NA, NH, VW])
        msk = sb("msk", [P, NA, D])
        mpart = sb("mpart", [P, NE, NA])
        mtok = sb("mtok", [P, NA, HE])
        mtp = sb("mtp", [P, NA, 3, HE], BF16)
        mres = sb("mres", [P, NA, HE])
        mt = sb("mt", [3 * HE, LP], BF16)
        pb = sb("pb", [P, 3, UB, QT])
        ofm = sb("ofm", [P, 2, QT])
        ot = sb("ot", [P, NA * NH, NE, VW])
        on = sb("on", [P, NA * NH, NE * HD])
        rec = sb("rec", [P, NA * NH, NE])
        lg = sb("lg", [P, NA * NH, NE])
        mx = sb("mx", [P, NA * NH])
        gs = sb("gs", [P, NA * NH, NE])
        mix = sb("mix", [P, NA * NH, HD])
        fx = sb("fx", [P, NA * NH, HD])
        fxt = sb("fxt", [D + 1, LP])
        hx1 = sb("hx1", [D + 1, LP])
        pm = sb("pm", [D, LP])
        fo = sb("fo", [P, NA * NH, HD])
        pss = ps("pss", [P, 2, UB, QT])
        pso = ps("a_pso", [P, QT])
        psm = ps("psm", [P, QT])
        psmb = psm[:].bitcast(BF16)

        res = sb("res", [P, NA, D])
        names = ("weights_loaded", "wbd_zeroed", "resid_loaded", "h_loaded", "bank_full", "bank_free", "vector_steps",
                 "variance", "rstd", "rest_ready", "rest_free", "parts_ready", "part1", "placed", "parts_used", "max_split", "max_placed",
                 "scored", "exped", "masked", "summed", "sums_copied", "logits", "logits_exped", "gate_exped", "result", "stored", "spilled", "passed", "tile_done", "pool_passed",
                 "mh_ready", "xn_ready", "fx_ready", "hx_ready", "swept", "swept_max", "ident_ready", "const_ready")
        (weights, wbd_zero, r_load, h_load, full, free, dve, var, rstd, rest, rest_free, parts, part1, placed, used, max_split, max_placed,
         scored, exped, masked, summed, acc_free, logit, logit_exp, gate_exp, result, stored, spilled, passed, tile_done, pool_passed,
         mh_ok, xn_ok, fx_ok, hx_ok, swept, swept_max, ident_ok, const_ok) = (sem("a_" + n) for n in names)
        chunks = [(0, 4), (4, 8), (8, 9)]

        PRO = [("turn", c) for c in chunks] + [("tok", c) for c in chunks] + [("feat", (g, k)) for g in range(3) for k in range(3)]
        MXJ = [("mrow", (0, 8)), ("mrow", (8, 9))]
        EPI = [("fturn", c) for c in chunks] + [("fc1", k) for k in range(3)] + [("fc2", k) for k in range(3)] + [("back", c) for c in chunks]
        OUTJ = [("oturn", (n, x)) for n in range(NH) for x in range(3)]
        J = len(PRO) + len(MXJ) + len(OUTJ) + len(EPI)
        JS = 1 + 4 * 6
        SWEEP = NH * NA * (NA + 1) // 2
        NUB = NH * NU
        dj = [[(c, b) for b, bank in enumerate(u) for (c, j, e, q0, w) in bank if (q0 == P * j if e is not None else j == NA - 1)] for u in units]
        NM = NH * sum(bool(d) for d in dj)
        assert NUB % 6 == 0 and SWEEP % 6 == 0
        order_m = {}
        for u, d in enumerate(dj):
            order_m[u] = sum(bool(x) for x in dj[:u + 1])
        tile_of = lambda q0: q0 // QT
        last_unit = {x: max(u for u, un in enumerate(units) for bank in un for p in bank if tile_of(p[3]) == x) for x in range(3)}
        last_bank = max(b for b, bank in enumerate(units[last_unit[0]]) if tile_of(bank[0][3]) == 0)
        assert last_bank < UB - 1 and all(tile_of(units[last_unit[x]][-1][0][3]) == x for x in (1, 2))

        with nc.Block() as block:
            @block.sync
            def _(sp):
                with sp.If(sp.value_load(flag_d, min_val=0, max_val=1) > 0):
                    for s_, c in ((exped, 2), (summed, 3), (free, 1), (acc_free, 1), (parts, 3), (stored, 16), (swept_max, 6), (used, 1)):
                        sp.sem_inc(s_, c)
                    sp.dma_start(ident[:], t["c_ident"]).then_inc(ident_ok, 16)
                    sp.dma_start(wha[:, 0:D], t["L0_ffn_hl_w"].rearrange("n d h -> (n d) h")).then_inc(weights, 16)
                    sp.dma_start(wha[:, D:D + 1], t["L0_ffn_hl_b"].rearrange("n (d o) -> (n d) o", o=1), allow_slow_non_contiguous=True).then_inc(weights, 16)
                    sp.dma_start(gw[:], rows(t["L0_ffn_gate_w"].rearrange("n e f -> (n e f)"), P)).then_inc(weights, 16)
                    sp.dma_start(gb[:], rows(t["L0_ffn_gate_b"].rearrange("n e -> (n e)"), P)).then_inc(weights, 16)
                    sp.dma_start(fgw[:].rearrange("p n d -> p (n d)"), rows(t["L0_ffn_fgate_w"].rearrange("n d -> (n d)"), P)).then_inc(weights, 16)
                    for i, n in enumerate(("ln_g", "ln_b", "fnorm_g", "fnorm_b")):
                        sp.dma_start(vec[:, i, :], rows(t["L0_ffn_" + n], P)).then_inc(weights, 16)
                    for n in range(4):
                        sp.dma_start(h4[:, NA * n:NA * (n + 1), :], xsrc(n)).then_inc(r_load, 16)
                    sp.wait_ge(wbd_zero, 2)
                    sp.dma_start(wbd[:, 384:448], t["c_ident"][0:D, 0:D]).then_inc(weights, 16)
                    for n in range(NH):
                        r = slice(HD * n, HD * n + HD)
                        o = HD * n
                        sp.dma_start(wbd[r, D * n:D * n + D], t["L0_ffn_wq"][n].rearrange("e o d -> d (e o)"), allow_slow_non_contiguous=True).then_inc(weights, 16)
                        sp.dma_start(wbd[r, 256 + o:272 + o], t["L0_ffn_wk"][n].rearrange("o d -> d o"), allow_slow_non_contiguous=True).then_inc(weights, 16)
                        sp.dma_start(wbd[r, 320 + o:336 + o], t["L0_ffn_wv"][n].rearrange("o d -> d o"), allow_slow_non_contiguous=True).then_inc(weights, 16)
                        for i in range(2):
                            w_, b_ = t[f"L0_ffn_fc{i + 1}_w"], t[f"L0_ffn_fc{i + 1}_b"]
                            sp.dma_start(fcw[r, i, o:o + HD], w_.rearrange("o d -> d o"), allow_slow_non_contiguous=True).then_inc(weights, 16)
                            sp.dma_start(fcw[D:D + 1, i, o:o + HD], rows(b_, 1)).then_inc(weights, 16)
                    with sp.Fori(0, B) as it:
                        src = xsrc(it)
                        sp.wait_ge(stored, it * 32 + 16)
                        sp.dma_start(hb[:], src).then_inc(h_load, 16)
                        for g in range(2):
                            sp.wait_ge(parts, it * 9 + 3 * g + 6)
                            sp.dma_start(qk_d[:, P * g:P * g + P, :].rearrange("t r q -> r t q"), qs[:, :, g, :]).then_inc(spilled, 16)
                        sp.wait_ge(parts, it * 9 + 12)
                        sp.dma_start(qk_d[:, 2 * P:2 * P + D, :].rearrange("t r q -> r t q"), ks[:]).then_inc(spilled, 16)
                        sp.wait_ge(spilled, it * 48 + 48)
                        for i, (qp, kp) in enumerate(zip(TERMS_Q, TERMS_K)):
                            r = slice(HD * i, HD * i + HD)
                            sp.dma_start(qop[r].rearrange("o n e q -> o (n e) q"), qk_d[qp, 0:2 * P].rearrange("(m o) q -> o m q", o=HD)).then_inc(placed, 16)
                            sp.dma_start(kop[r], qk_d[kp, 2 * P:2 * P + D].rearrange("(n o) q -> o n q", o=HD)).then_inc(placed, 16)
                        sp.wait_ge(max_split, it + 1)
                        for i in range(3):
                            sp.dma_start(qop[KT + i:KT + i + 1].rearrange("k n e q -> k (n e) q"), mt[HE * i:HE * i + HE, :]).then_inc(max_placed, 16)
                        ores = out[it]
                        sp.wait_ge(result, it + 1)
                        sp.dma_start(ores[0:(NA - 1) * P].rearrange("(a p) d -> p a d", p=P), res[:, 0:NA - 1]).then_inc(stored, 16)
                        sp.dma_start(ores[(NA - 1) * P:L], res[0:LAST, NA - 1]).then_inc(stored, 16)
                    sp.wait_ge(stored, 32 * B + 16)

            @block.tensor
            def _(pe):
                with pe.If(pe.value_load(flag_d, min_val=0, max_val=1) > 0):
                    k = [0]

                    def job(base, ins):
                        ins().then_inc(full, 1)
                        k[0] += 1

                    def gate(base):
                        pe.wait_ge(free, base + k[0] + 1)

                    def turn_rows(src, c, base, rows_=D):
                        gate(base)
                        pe.sem_inc(passed, 1)
                        for a in range(*c):
                            mm = pe.transpose(psm[0:D, (a - c[0]) * P:(a - c[0] + 1) * P], src[:, a, :], ident[:])
                        job(base, lambda: mm)

                    pe.wait_ge(weights, 16 * 38)
                    pe.wait_ge(ident_ok, 16)
                    gate(0)
                    job(0, lambda: pe.matmul(psm[0:D + 1, 0:448], wha[:], wbd[:], start=True, stop=True))
                    pe.wait_ge(xn_ok, 1)
                    for n in range(4):
                        for c in chunks:
                            turn_rows(h4[:, NA * n:NA * (n + 1)], c, 0)
                        for c in chunks:
                            gate(0)
                            for a in range(*c):
                                mm = pe.matmul(psm[:, (a - c[0]) * HD:(a - c[0] + 1) * HD], xt[:, a * P:(a + 1) * P], wall[:, 384 + HD * n:400 + HD * n], start=True, stop=True)
                            job(0, lambda: mm)
                    assert k[0] == JS
                    pe.wait_ge(const_ok, 3)
                    with pe.Fori(0, B) as it:
                        k[0] = 0
                        base = it * J + JS
                        g0 = it * NUB
                        pe.wait_ge(xn_ok, it + 2)
                        for kind, c in PRO:
                            if kind == "turn":
                                turn_rows(xn, c, base)
                            elif kind == "tok":
                                gate(base)
                                for a in range(*c):
                                    mm = pe.matmul(psm[:, (a - c[0]) * P:(a - c[0] + 1) * P], xt[:, a * P:(a + 1) * P], wall[:, 320:448], start=True, stop=True)
                                job(base, lambda: mm)
                            else:
                                g, x = c
                                gate(base)
                                m = P if g < 2 else D
                                job(base, lambda: pe.matmul(psm[0:m, 0:FB], wall[:, g * P:g * P + m], xt[:, x * FB:(x + 1) * FB], start=True, stop=True))
                        pe.wait_ge(placed, it * 192 + 192)
                        sw = 0
                        for n in range(NH):
                            for i in range(NA):
                                for j in range(i + 1):
                                    pe.wait_ge(swept_max, it * SWEEP + sw + 1)
                                    bank = pss[:, sw // 3 % 2, sw % 3, :]
                                    for e in range(NE):
                                        mm = pe.matmul(bank[:, e * P:(e + 1) * P], qop[0:KT, n, e, i * P:(i + 1) * P], kop[0:KT, n, j * P:(j + 1) * P],
                                                       start=(e == 0 or i != j), stop=(i != j), skip_group_check=True)
                                    if i == j:
                                        mm = pe.matmul(bank, identb[:], bmid(maskb[:], NE), start=False, stop=True, skip_group_check=True)
                                    mm.then_inc(swept, 1)
                                    sw += 1
                        for kind, c in MXJ:
                            gate(base)
                            pe.wait_ge(used, it + 2)
                            pe.sem_inc(passed, 1)
                            for a in range(*c):
                                mm = pe.transpose(psmb[0:3 * HE, (a - c[0]) * P:(a - c[0] + 1) * P], mtp[:, a], identb[:])
                            job(base, lambda: mm)
                        pe.wait_ge(max_placed, it * 48 + 48)
                        pe.wait_ge(swept_max, it * SWEEP + SWEEP + 6)

                        def scores(u):
                            n, un = divmod(u, NU)
                            pe.wait_ge(exped, g0 + u + 1)
                            for b, bank in enumerate(units[un]):
                                for col, j, e, q0, w in bank:
                                    lhs = kop[:, n, j * P:(j + 1) * P]
                                    if e is None:
                                        mm = pe.matmul(pss[:, u % 2, b, 0:NE * w], lhs, qop[:, n, :, q0:q0 + w], start=True, stop=True, skip_group_check=True)
                                    else:
                                        mm = pe.matmul(pss[:, u % 2, b, col:col + w], lhs, qop[:, n, e, q0:q0 + w], start=True, stop=True, skip_group_check=True)
                            mm.then_inc(scored, 1)

                        def sums(u):
                            n, un = divmod(u, NU)
                            pe.wait_ge(exped, g0 + u + 3)
                            if dj[un]:
                                pe.wait_ge(masked, it * NM + (NM // NH) * n + order_m[un])
                            for b, bank in enumerate(units[un]):
                                for col, j, e, q0, w in bank:
                                    x = tile_of(q0)
                                    if j == 0 and e in (0, None):
                                        pe.wait_ge(acc_free, it * 3 * NH + 3 * n + x + 1)
                                    r = P if j < NA - 1 else LAST
                                    for ee in range(NE) if e is None else (e,):
                                        cc = col + (w * ee if e is None else 0)
                                        mm = pe.matmul(pso[VW * ee:VW * (ee + 1), q0 - QT * x:q0 - QT * x + w], vop[0:r, j, n, :], pb[0:r, u % 3, b, cc:cc + w],
                                                       start=(j == 0), stop=(q0 == P * j if e is not None else j == NA - 1), skip_group_check=True)
                                if un == last_unit[0] and b == last_bank:
                                    mm.then_inc(tile_done, 1)
                            mm.then_inc(summed, 1)

                        for u in range(NUB + 1):
                            if u < NUB:
                                scores(u)
                            if u >= 1:
                                sums(u - 1)
                                n = (u - 1) // NU
                                for x in (x for x in range(3) if last_unit[x] == (u - 1) % NU):
                                    c = (4 * x, min(4 * x + 4, NA))
                                    gate(base)
                                    pe.wait_ge(acc_free, it * 3 * NH + 3 * n + x + 2)
                                    for a in range(*c):
                                        wd = P if a < NA - 1 else LAST
                                        mm = pe.transpose(psm[0:wd, (a - c[0]) * P:(a - c[0] + 1) * P], ofm[:, (3 * n + x) % 2, (a - c[0]) * P:(a - c[0]) * P + wd], ident[:])
                                    job(base, lambda: mm)
                        pe.wait_ge(fx_ok, it + 1)
                        for kind, c in EPI:
                            if kind == "fturn":
                                turn_rows(fx[:].rearrange("p (a n) d -> p a (n d)", n=NH), c, base)
                            elif kind in ("fc1", "fc2"):
                                gate(base)
                                i = kind == "fc2"
                                job(base, lambda: pe.matmul(psm[0:D, 0:FB], fcw[:, int(i), :], (hx1 if i else fxt)[:, c * FB:(c + 1) * FB], start=True, stop=True))
                            else:
                                gate(base)
                                pe.sem_inc(passed, 1)
                                for a in range(*c):
                                    mm = pe.transpose(psm[:, (a - c[0]) * D:(a - c[0] + 1) * D], pm[:, a * P:(a + 1) * P], ident[0:D, 0:D])
                                job(base, lambda: mm)
                        assert k[0] == J

            @block.scalar
            def _(act):
                with act.If(act.value_load(flag_d, min_val=0, max_val=1) > 0):
                    with act.Fori(0, B) as it:
                        g0 = it * NUB
                        for u in range(NUB):
                            un = u % NU
                            act.wait_ge(scored, g0 + u + 1)
                            act.wait_ge(summed, g0 + u + 1)
                            w = QT if units[un][0][0][2] is not None else NE * LAST
                            nc.scalar.activation(pb[:, u % 3, :, 0:w], pss[:, u % 2, :, 0:w], ACT.Exp, scale=float(HD) ** 0.5).then_inc(exped, 1)
                        for i, (src, s_) in enumerate(((lg[:], logit_exp), (gs[:, 0:NA, :], gate_exp))):
                            act.wait_ge(logit, it * 2 + i + 1)
                            nc.scalar.activation(src, src, ACT.Exp).then_inc(s_, 1)

            @block.gpsimd
            def _(pool):
                with pool.If(pool.value_load(flag_d, min_val=0, max_val=1) > 0):
                    pool.memset(mh[:], -0.5).then_inc(mh_ok, 1)
                    pool.wait_ge(mh_ok, 1)
                    pool.memset(maskf[:], 0.0).then_inc(mh_ok, 1)
                    pool.wait_ge(mh_ok, 2)
                    pool.affine_select(out=maskf[:], in_=maskf[:], compare_op=ALU.is_ge, fill=-1e30, base=0, pattern=[[-1, P]], channel_multiplier=1).then_inc(mh_ok, 1)
                    pool.wait_ge(mh_ok, 3)
                    pool.wait_ge(var, 1)
                    pool.tensor_tensor(stat[:, 3], stat[:, 2], mh[:], ALU.pow).then_inc(rstd, 1)

                    def root(i, it, n):
                        pool.wait_ge(var, it * 3 + i + 2)
                        pool.tensor_tensor(stat[:, 3, 0:n], stat[:, 2, 0:n], mh[:, 0:n], ALU.pow).then_inc(rstd, 1)

                    with pool.Fori(0, B) as it:
                        root(0, it, NA)
                        for i in range(9):
                            g, x = divmod(i, 3)
                            m = P if g < 2 else D
                            dst = (lambda p_: qs[:, p_, g, x * FB:(x + 1) * FB]) if g < 2 else (lambda p_: ks[:, p_, x * FB:(x + 1) * FB])
                            pool.wait_ge(free, it * J + JS + 6 + i + 2)
                            pool.sem_inc(pool_passed, 1)
                            pool.tensor_copy(dst(1), rq[0:m, i % 3, :]).then_inc(part1, 1)
                            pool.wait_ge(part1, it * 9 + i + 1)
                            pool.tensor_tensor(dst(2), rq[0:m, i % 3, :], dst(1), ALU.subtract).then_inc(parts, 1)
                            pool.wait_ge(parts, it * 9 + i + 4)
                        for u in range(NUB):
                            un = u % NU
                            if not dj[un]:
                                continue
                            pool.wait_ge(exped, it * NUB + u + 3)
                            pool.sem_inc(pool_passed, 1)
                            cols = {}
                            for c, b in dj[un]:
                                cols.setdefault(c, []).append(b)
                            n_ = 0
                            for c, bs in sorted(cols.items()):
                                if units[un][bs[0]][0][2] is None:
                                    v_ = pb[0:LAST, u % 3, bs[0], 0:NE * LAST].rearrange("p (e q) -> p e q", e=NE)
                                    pat = [[0, NE], [1, LAST]]
                                else:
                                    v_ = pb[:, u % 3, bs[0]:bs[-1] + 1, c:c + P]
                                    pat = [[0, len(bs)], [1, P]]
                                ins = pool.affine_select(out=v_, in_=v_, compare_op=ALU.is_ge, fill=0.0, base=0, pattern=pat, channel_multiplier=-1)
                            ins.then_inc(masked, 1)
                        root(1, it, NA * NH)
                        root(2, it, NA * NH)

            @block.vector
            def _(v):
                with v.If(v.value_load(flag_d, min_val=0, max_val=1) > 0):
                    tt, ts, stt, cp = nc.vector.tensor_tensor, nc.vector.tensor_scalar, nc.vector.scalar_tensor_tensor, nc.vector.tensor_copy
                    red = nc.vector.tensor_reduce
                    k = [0]
                    nc.vector.memset(wbd[:], 0.0).then_inc(wbd_zero, 1)
                    nc.vector.memset(fcw[:], 0.0).then_inc(wbd_zero, 1)
                    ch = Chain(v, dve)
                    ch.step(nc.vector.memset(xt[D:D + 1], 1.0))
                    ch.step(nc.vector.memset(fxt[D:D + 1], 1.0))
                    ch.step(nc.vector.memset(hx1[D:D + 1], 1.0))
                    ch.step(nc.vector.memset(vop[:], 0.0))
                    ch.step(nc.vector.memset(vop[:, :, :, HD:HD + 1], 1.0))
                    ch.step(nc.vector.memset(ot[:], 1.0))
                    nc.vector.memset(kop[KT:KM], -1.0).then_inc(const_ok, 1)
                    v.wait_ge(ident_ok, 16)
                    cp(identb[:], ident[:]).then_inc(const_ok, 1)
                    v.wait_ge(mh_ok, 3)
                    cp(maskb[:], maskf[:]).then_inc(const_ok, 1)

                    def take(base):
                        v.wait_ge(full, base + k[0] + 1)

                    def give(ins):
                        ins.then_inc(free, 1)
                        k[0] += 1

                    take(0)
                    give(cp(wall[:], psm[0:D + 1, 0:448]))
                    v.wait_ge(r_load, 64)
                    norm_groups(nc, v, ch, var, rstd, 1, h4[:], h4[:], tmp[:], stat, 4 * NA, D, EPS)
                    ch.wait()
                    cp(stat[:, 0, 0:1], stat[:, 1, 0:1]).then_inc(xn_ok, 1)
                    for n in range(4):
                        for c in chunks:
                            take(0)
                            give(cp(xt[0:D, c[0] * P:c[1] * P], psm[0:D, 0:(c[1] - c[0]) * P]))
                        for c in chunks:
                            take(0)
                            give(cp(resid[:, c[0]:c[1], HD * n:HD * n + HD], psm[:, 0:(c[1] - c[0]) * HD].rearrange("p (a d) -> p a d", d=HD)))
                    assert k[0] == JS
                    n_setup = ch.n
                    v.wait_ge(free, JS + 1)
                    with v.Fori(0, B) as it:
                        k[0] = 0
                        base = it * J + JS
                        ch = Chain(v, dve, it * NDVE + n_setup)
                        v.wait_ge(h_load, it * 16 + 16)
                        ch.step(cp(tmp[:, NA:2 * NA, :], hb[:]))
                        norm_groups(nc, v, ch, var, rstd, it * 3 + 2, xn[:], tmp[:, NA:2 * NA, :], tmp[:, 0:NA, :], stat, NA, D, EPS)
                        cp(stat[:, 0, 0:1], stat[:, 1, 0:1]).then_inc(xn_ok, 1)
                        for kind, c in PRO:
                            take(base)
                            if kind == "turn":
                                give(cp(xt[0:D, c[0] * P:c[1] * P], psm[0:D, 0:(c[1] - c[0]) * P]))
                            elif kind == "tok":
                                pv = psm[:].rearrange("p (a s x) -> p a s x", s=2, x=D)[:, 0:c[1] - c[0]]
                                ch.done(cp(vop[:, c[0]:c[1], :, 0:HD], pv[:, :, 0, :].rearrange("p a (n d) -> p a n d", d=HD)))
                                give(ts(msk[:, c[0]:c[1], :], pv[:, :, 1, :], 0.0, None, ALU.not_equal))
                            else:
                                g, x = c
                                i = 3 * g + x
                                m = P if g < 2 else D
                                p0 = qs[:, 0, g, x * FB:(x + 1) * FB] if g < 2 else ks[:, 0, x * FB:(x + 1) * FB]
                                ch.step(cp(p0, psm[0:m, 0:FB]))
                                v.wait_ge(parts, it * 9 + i + 1)
                                give(tt(rq[0:m, i % 3, :], psm[0:m, 0:FB], p0, ALU.subtract))
                        sw = 0
                        for n in range(NH):
                            for i in range(NA):
                                for j in range(i + 1):
                                    v.wait_ge(swept, it * SWEEP + sw + 1)
                                    red(mpart[:, :, j:j + 1], pss[:, sw // 3 % 2, sw % 3, :].rearrange("p (e t) -> p e t", e=NE), AX.X, ALU.max).then_inc(swept_max, 1)
                                    sw += 1
                                v.wait_ge(swept_max, it * SWEEP + sw + 6)
                                ch.step(red(mtok[:, i, NE * n:NE * n + NE], mpart[:, :, 0:i + 1], AX.X, ALU.max))
                        ch.step(cp(mtp[:, :, 0, :], mtok[:]))
                        ch.step(tt(mres[:], mtok[:], mtp[:, :, 0, :], ALU.subtract))
                        ch.step(cp(mtp[:, :, 1, :], mres[:]))
                        tt(mtp[:, :, 2, :], mres[:], mtp[:, :, 1, :], ALU.subtract).then_inc(used, 1)
                        for kind, c in MXJ:
                            take(base)
                            if c[0] == 0:
                                give(cp(mt[:, 0:8 * P], psmb[0:3 * HE, 0:8 * P]))
                            else:
                                give(cp(mt[:, 8 * P:], psmb[0:3 * HE, 0:P]))
                                v.wait_ge(free, base + k[0] + 1)
                                cp(stat[0:1, 1, 0:1], stat[0:1, 0, 0:1]).then_inc(max_split, 1)
                        for n in range(NH):
                            for x in range(3):
                                w = QT if x < 2 else LAST
                                if x == 0:
                                    v.wait_ge(tile_done, it * NH + n + 1)
                                else:
                                    v.wait_ge(summed, it * NUB + n * NU + last_unit[x] + 4)
                                cp(ofm[:, (3 * n + x) % 2, 0:w], pso[:, 0:w]).then_inc(acc_free, 1)
                                take(base)
                                c = (4 * x, min(4 * x + 4, NA))
                                dst = ot[:].rearrange("p (a n) e w -> p a n (e w)", n=NH)
                                if x < 2:
                                    give(cp(dst[:, c[0]:c[1], n, :], psm[:].rearrange("p (a w) -> p a w", w=P)))
                                else:
                                    give(cp(dst[0:LAST, NA - 1, n, :], psm[0:LAST, 0:P]))
                        v.wait_ge(free, base + k[0] + 1)
                        G = NA * NH
                        ch.step(nc.vector.reciprocal(rec[:], ot[:, :, :, HD]))
                        onv = on[:].rearrange("p g (e d) -> p g e d", d=HD)
                        ch.step(tt(onv, ot[:, :, :, 0:HD], bcast(rec[:], HD), ALU.mult))
                        ch.step(tt(onv, onv, bmid(msk[:].rearrange("p a (n d) -> p (a n) d", d=HD), NE), ALU.mult))
                        on4 = on[:].rearrange("p (a n) f -> p a n f", n=NH)
                        tm4 = tmp[:].rearrange("p (a n) f -> p a n f", n=NH)
                        gwv = gw[:].rearrange("p (n e f) -> p e n f", n=NH, f=64)
                        for e in range(NE):
                            for a in range(NA):
                                ch.done(tt(tm4[:, a], on4[:, a], gwv[:, e], ALU.mult))
                            ch.wait()
                            ch.step(red(lg[:, :, e:e + 1], tmp[:], AX.X, ALU.add))
                        ch.step(tt(lg[:].rearrange("p (a n) e -> p a (n e)", n=NH), lg[:].rearrange("p (a n) e -> p a (n e)", n=NH), bmid(gb[:], NA), ALU.add))
                        ch.step(red(mx[:], lg[:], AX.X, ALU.max))
                        tt(lg[:], lg[:], bcast(mx[:], NE), ALU.subtract).then_inc(logit, 1)
                        v.wait_ge(logit_exp, it + 1)
                        ch.step(red(mx[:], lg[:], AX.X, ALU.add))
                        ch.step(nc.vector.reciprocal(mx[:], mx[:]))
                        ch.step(tt(lg[:], lg[:], bcast(mx[:], NE), ALU.mult))
                        ch.step(tt(tmp[:].rearrange("p g (e d) -> p g e d", d=HD), onv, bcast(lg[:], HD), ALU.mult))
                        ch.step(red(mix[:], tmp[:].rearrange("p g (e d) -> p g d e", d=HD), AX.X, ALU.add))
                        ch.step(tt(mix[:], mix[:], resid[:].rearrange("p a (n d) -> p (a n) d", d=HD), ALU.add))
                        t16 = tmp[:, :, 0:HD]
                        norm_groups(nc, v, ch, var, rstd, it * 3 + 3, fx[:], mix[:], t16, stat, G, HD, FEPS)
                        ch.step(tt(fx[:], fx[:], bmid(vec[:, 0, :], G), ALU.mult))
                        tt(fx[:], fx[:], bmid(vec[:, 1, :], G), ALU.add).then_inc(fx_ok, 1)
                        for kind, c in EPI:
                            take(base)
                            if kind == "fturn":
                                give(cp(fxt[0:D, c[0] * P:c[1] * P], psm[0:D, 0:(c[1] - c[0]) * P]))
                            elif kind == "fc1":
                                s_ = slice(c * FB, (c + 1) * FB)
                                if c == 0:
                                    v.wait_ge(free, base + k[0] + 1)
                                    ch.step(ts(pm[:], fxt[0:D], 0.0, None, ALU.not_equal))
                                give(stt(hx1[0:D, s_], psm[0:D, 0:FB], 0.0, pm[:, s_], ALU.max, ALU.mult))
                            elif kind == "fc2":
                                s_ = slice(c * FB, (c + 1) * FB)
                                ch.step(tt(pm[:, s_], psm[0:D, 0:FB], pm[:, s_], ALU.mult))
                                give(tt(pm[:, s_], pm[:, s_], fxt[0:D, s_], ALU.add))
                            else:
                                give(cp(fo[:].rearrange("p (a n) d -> p a (n d)", n=NH)[:, c[0]:c[1], :], psm[:, 0:(c[1] - c[0]) * D].rearrange("p (a d) -> p a d", d=D)))
                        assert k[0] == J
                        v.wait_ge(free, base + k[0] + 1)
                        norm_groups(nc, v, ch, var, rstd, it * 3 + 4, fx[:], fo[:], t16, stat, G, HD, FEPS)
                        ch.step(tt(fx[:], fx[:], bmid(vec[:, 2, :], G), ALU.mult))
                        ch.step(tt(fx[:], fx[:], bmid(vec[:, 3, :], G), ALU.add))
                        fa = fx[:].rearrange("p (a n) d -> p a (n d)", n=NH)
                        for n in range(NH):
                            ch.step(tt(tmp[:, 0:NA, :], fa, bmid(fgw[:, n, :], NA), ALU.mult))
                            ch.step(red(gs[:, 0:NA, n:n + 1], tmp[:, 0:NA, :], AX.X, ALU.add))
                        gg = gs[:, 0:NA, :]
                        ch.step(red(mx[:, 0:NA], gg, AX.X, ALU.max))
                        tt(gg, gg, bcast(mx[:, 0:NA], NH), ALU.subtract).then_inc(logit, 1)
                        v.wait_ge(gate_exp, it + 1)
                        ch.step(red(mx[:, 0:NA], gg, AX.X, ALU.add))
                        ch.step(nc.vector.reciprocal(mx[:, 0:NA], mx[:, 0:NA]))
                        ch.step(tt(gg, gg, bcast(mx[:, 0:NA], NH), ALU.mult))
                        ch.step(tt(fx[:].rearrange("p (a n) d -> p a n d", n=NH), fx[:].rearrange("p (a n) d -> p a n d", n=NH), bcast(gg, HD), ALU.mult))
                        v.wait_ge(stored, it * 32 + 16)
                        tt(res[:], hb[:], fa, ALU.add).then_inc(result, 1)
                        assert ch.n == NDVE, ch.n


SHIFT = 56.0
SUM_MIN = 1e-27
VALUE_MAX = 1e10
ROUNDING = 1.0 + 2.0 ** -5


def stage_ffn_bounded(nc, t, h2d, out, flag_d):
    units = score_units()
    NU = len(units)
    NDVE = 123
    qk_d = nc.dram_tensor("qk_parts_b", (3, 2 * P + D, LP), BF16).ap()
    xsrc = lambda b: h2d[b].rearrange("(a p) d -> p a d", p=P)
    with ExitStack() as ctx:
        sb = lambda n, s, d=F32: ctx.enter_context(nc.sbuf_tensor(n, s, d))
        ps = lambda n, s, d=F32: ctx.enter_context(nc.psum_tensor(n, s, d))
        sem = lambda n: ctx.enter_context(nc.semaphore(n))
        ident = sb("b_ident", [P, P])
        blkq = sb("b_blkq", [P, 2, HE])
        blkk = sb("b_blkk", [D, HE])
        wha = sb("b_wha", [NH * HD, D + 1])
        wbd = sb("b_wbd", [NH * HD, 448])
        wall = sb("b_wall", [D + 1, 448])
        fcw = sb("b_fcw", [D + 1, 2, D])
        gw = sb("b_gw", [P, HE * 64])
        gb = sb("b_gb", [P, HE])
        fgw = sb("b_fgw", [P, NH, D])
        vec = sb("b_vec", [P, 4, HD])
        resid = sb("b_resid", [P, NA, D])
        h4 = sb("b_h4", [P, 4 * NA, D])
        hb = sb("b_hb", [P, NA, D])
        xn = sb("b_xn", [P, NA, D])
        tmp = sb("b_tmp", [P, 4 * NA, D])
        stat = sb("b_stat", [P, 4, 4 * NA])
        mh = sb("b_mh", [P, 4 * NA])
        xt = sb("b_xt", [D + 1, LP])
        qs = sb("b_qs", [P, 3, 2, LP], BF16)
        ks = sb("b_ks", [D, 3, LP], BF16)
        rq = sb("b_rq", [P, 3, FB])
        qop = sb("b_qop", [KM, NH, NE, LP], BF16)
        kop = sb("b_kop", [KM, NH, LP], BF16)
        vop = sb("b_vop", [P, NA, NH, VW])
        msk = sb("b_msk", [P, NA, D])
        kmax = sb("b_kmax", [HE, 4])
        bound = sb("b_bound", [HE, LP])
        mt = sb("b_mt", [HE, 3, LP], BF16)
        good = sb("b_good", [P, 3])
        bad = sb("b_bad", [P, 2])
        flag = sb("b_flag", [P, 1], I32)
        pb = sb("b_pb", [P, 3, UB, QT])
        ofm = sb("b_ofm", [P, 2, QT])
        ot = sb("b_ot", [P, NA * NH, NE, VW])
        on = sb("b_on", [P, NA * NH, NE * HD])
        rec = sb("b_rec", [P, NA * NH, NE])
        lg = sb("b_lg", [P, NA * NH, NE])
        mx = sb("b_mx", [P, NA * NH])
        gs = sb("b_gs", [P, NA * NH, NE])
        mix = sb("b_mix", [P, NA * NH, HD])
        fx = sb("b_fx", [P, NA * NH, HD])
        fxt = sb("b_fxt", [D + 1, LP])
        hx1 = sb("b_hx1", [D + 1, LP])
        pm = sb("b_pm", [D, LP])
        fo = sb("b_fo", [P, NA * NH, HD])
        pss = ps("b_pss", [P, 2, UB, QT])
        pso = ps("b_pso", [P, QT])
        psm = ps("b_psm", [P, QT])

        res = sb("b_res", [P, NA, D])
        names = ("weights_loaded", "wbd_zeroed", "resid_loaded", "h_loaded", "bank_full", "bank_free", "vector_steps",
                 "variance", "rstd", "rest_ready", "rest_free", "parts_ready", "part1", "placed", "max_split", "max_placed",
                 "scored", "exped", "masked", "summed", "sums_copied", "logits", "logits_exped", "gate_exped", "result", "stored", "spilled", "passed", "tile_done", "pool_passed",
                 "mh_ready", "xn_ready", "fx_ready", "hx_ready", "squared_bound", "rooted", "flag_ready", "bad_ready", "flag_done", "const_ready")
        (weights, wbd_zero, r_load, h_load, full, free, dve, var, rstd, rest, rest_free, parts, part1, placed, max_split, max_placed,
         scored, exped, masked, summed, acc_free, logit, logit_exp, gate_exp, result, stored, spilled, passed, tile_done, pool_passed,
         mh_ok, xn_ok, fx_ok, hx_ok, squared_bound, rooted, flag_ready, bad_ready, flag_ok, const_ok) = (sem("b_" + n) for n in names)
        chunks = [(0, 4), (4, 8), (8, 9)]

        PRO = [("turn", c) for c in chunks] + [("tok", c) for c in chunks]
        PRO += [("feat", (2, x)) for x in range(3)] + [("knorm", x) for x in range(3)]
        for x in range(3):
            PRO += [("feat", (0, x)), ("feat", (1, x)), ("qnorm", x)]
        FEATS = [(i, c) for i, (kind, c) in enumerate(PRO) if kind == "feat"]
        squares = h4[:].rearrange("p a d -> p (a d)").rearrange("p (s f) -> p s f", f=FB)
        slot = {c: i % 6 for i, (_, c) in enumerate(FEATS)}
        EPI = [("fturn", c) for c in chunks] + [("fc1", k) for k in range(3)] + [("fc2", k) for k in range(3)] + [("back", c) for c in chunks]
        OUTJ = [("oturn", (n, x)) for n in range(NH) for x in range(3)]
        J = len(PRO) + len(OUTJ) + len(EPI)
        JS = 1 + 4 * 6
        NUB = NH * NU
        dj = [[(c, b) for b, bank in enumerate(u) for (c, j, e, q0, w) in bank if (q0 == P * j if e is not None else j == NA - 1)] for u in units]
        NM = NH * sum(bool(d) for d in dj)
        assert NUB % 6 == 0
        order_m = {}
        for u, d in enumerate(dj):
            order_m[u] = sum(bool(x) for x in dj[:u + 1])
        tile_of = lambda q0: q0 // QT
        last_unit = {x: max(u for u, un in enumerate(units) for bank in un for p in bank if tile_of(p[3]) == x) for x in range(3)}
        last_bank = max(b for b, bank in enumerate(units[last_unit[0]]) if tile_of(bank[0][3]) == 0)
        assert last_bank < UB - 1 and all(tile_of(units[last_unit[x]][-1][0][3]) == x for x in (1, 2))

        with nc.Block() as block:
            @block.sync
            def _(sp):
                for s_, c in ((exped, 2), (summed, 3), (free, 1), (acc_free, 1), (parts, 3), (stored, 16)):
                    sp.sem_inc(s_, c)
                sp.dma_start(ident[:], t["c_ident"]).then_inc(weights, 16)
                sp.dma_start(blkq[:], t["c_blkq"]).then_inc(weights, 16)
                sp.dma_start(blkk[:], t["c_blkk"]).then_inc(weights, 16)
                sp.dma_start(wha[:, 0:D], t["L0_ffn_hl_w"].rearrange("n d h -> (n d) h")).then_inc(weights, 16)
                sp.dma_start(wha[:, D:D + 1], t["L0_ffn_hl_b"].rearrange("n (d o) -> (n d) o", o=1), allow_slow_non_contiguous=True).then_inc(weights, 16)
                sp.dma_start(gw[:], rows(t["L0_ffn_gate_w"].rearrange("n e f -> (n e f)"), P)).then_inc(weights, 16)
                sp.dma_start(gb[:], rows(t["L0_ffn_gate_b"].rearrange("n e -> (n e)"), P)).then_inc(weights, 16)
                sp.dma_start(fgw[:].rearrange("p n d -> p (n d)"), rows(t["L0_ffn_fgate_w"].rearrange("n d -> (n d)"), P)).then_inc(weights, 16)
                for i, n in enumerate(("ln_g", "ln_b", "fnorm_g", "fnorm_b")):
                    sp.dma_start(vec[:, i, :], rows(t["L0_ffn_" + n], P)).then_inc(weights, 16)
                for n in range(4):
                    sp.dma_start(h4[:, NA * n:NA * (n + 1), :], xsrc(n)).then_inc(r_load, 16)
                sp.wait_ge(wbd_zero, 2)
                sp.dma_start(wbd[:, 384:448], t["c_ident"][0:D, 0:D]).then_inc(weights, 16)
                for n in range(NH):
                    r = slice(HD * n, HD * n + HD)
                    o = HD * n
                    sp.dma_start(wbd[r, D * n:D * n + D], t["L0_ffn_wq"][n].rearrange("e o d -> d (e o)"), allow_slow_non_contiguous=True).then_inc(weights, 16)
                    sp.dma_start(wbd[r, 256 + o:272 + o], t["L0_ffn_wk"][n].rearrange("o d -> d o"), allow_slow_non_contiguous=True).then_inc(weights, 16)
                    sp.dma_start(wbd[r, 320 + o:336 + o], t["L0_ffn_wv"][n].rearrange("o d -> d o"), allow_slow_non_contiguous=True).then_inc(weights, 16)
                    for i in range(2):
                        w_, b_ = t[f"L0_ffn_fc{i + 1}_w"], t[f"L0_ffn_fc{i + 1}_b"]
                        sp.dma_start(fcw[r, i, o:o + HD], w_.rearrange("o d -> d o"), allow_slow_non_contiguous=True).then_inc(weights, 16)
                        sp.dma_start(fcw[D:D + 1, i, o:o + HD], rows(b_, 1)).then_inc(weights, 16)
                with sp.Fori(0, B) as it:
                    src = xsrc(it)
                    sp.wait_ge(stored, it * 32 + 16)
                    sp.dma_start(hb[:], src).then_inc(h_load, 16)
                    sp.wait_ge(parts, it * 9 + 6)
                    sp.dma_start(qk_d[:, 2 * P:2 * P + D, :].rearrange("t r q -> r t q"), ks[:]).then_inc(spilled, 16)
                    sp.wait_ge(parts, it * 9 + 12)
                    for g in range(2):
                        sp.dma_start(qk_d[:, P * g:P * g + P, :].rearrange("t r q -> r t q"), qs[:, :, g, :]).then_inc(spilled, 16)
                    sp.wait_ge(spilled, it * 48 + 48)
                    for i, (qp, kp) in enumerate(zip(TERMS_Q, TERMS_K)):
                        r = slice(HD * i, HD * i + HD)
                        sp.dma_start(qop[r].rearrange("o n e q -> o (n e) q"), qk_d[qp, 0:2 * P].rearrange("(m o) q -> o m q", o=HD)).then_inc(placed, 16)
                        sp.dma_start(kop[r], qk_d[kp, 2 * P:2 * P + D].rearrange("(n o) q -> o n q", o=HD)).then_inc(placed, 16)
                    sp.wait_ge(max_split, it + 1)
                    for i in range(3):
                        sp.dma_start(qop[KT + i:KT + i + 1].rearrange("k n e q -> k (n e) q"), mt[:, i, :]).then_inc(max_placed, 16)
                    ores = out[it]
                    sp.wait_ge(result, it + 1)
                    sp.dma_start(ores[0:(NA - 1) * P].rearrange("(a p) d -> p a d", p=P), res[:, 0:NA - 1]).then_inc(stored, 16)
                    sp.dma_start(ores[(NA - 1) * P:L], res[0:LAST, NA - 1]).then_inc(stored, 16)
                sp.wait_ge(flag_ok, 1)
                sp.dma_start(flag_d, flag[0:1, 0:1]).then_inc(stored, 16)
                sp.wait_ge(stored, 32 * B + 32)

            @block.tensor
            def _(pe):
                k = [0]

                def job(base, ins):
                    ins().then_inc(full, 1)
                    k[0] += 1

                def gate(base):
                    pe.wait_ge(free, base + k[0] + 1)

                def turn_rows(src, c, base, rows_=D):
                    gate(base)
                    pe.sem_inc(passed, 1)
                    for a in range(*c):
                        mm = pe.transpose(psm[0:D, (a - c[0]) * P:(a - c[0] + 1) * P], src[:, a, :], ident[:])
                    job(base, lambda: mm)

                pe.wait_ge(weights, 16 * 41)
                gate(0)
                job(0, lambda: pe.matmul(psm[0:D + 1, 0:448], wha[:], wbd[:], start=True, stop=True))
                pe.wait_ge(xn_ok, 1)
                for n in range(4):
                    for c in chunks:
                        turn_rows(h4[:, NA * n:NA * (n + 1)], c, 0)
                    for c in chunks:
                        gate(0)
                        for a in range(*c):
                            mm = pe.matmul(psm[:, (a - c[0]) * HD:(a - c[0] + 1) * HD], xt[:, a * P:(a + 1) * P], wall[:, 384 + HD * n:400 + HD * n], start=True, stop=True)
                        job(0, lambda: mm)
                assert k[0] == JS
                pe.wait_ge(const_ok, 2)
                with pe.Fori(0, B) as it:
                    k[0] = 0
                    base = it * J + JS
                    g0 = it * NUB
                    pe.wait_ge(xn_ok, it + 2)
                    for kind, c in PRO:
                        if kind == "turn":
                            turn_rows(xn, c, base)
                        elif kind == "tok":
                            gate(base)
                            for a in range(*c):
                                mm = pe.matmul(psm[:, (a - c[0]) * P:(a - c[0] + 1) * P], xt[:, a * P:(a + 1) * P], wall[:, 320:448], start=True, stop=True)
                            job(base, lambda: mm)
                        elif kind == "knorm":
                            gate(base)
                            pe.sem_inc(passed, 1)
                            job(base, lambda: pe.matmul(psm[0:HE, 0:FB], blkk[:], squares[0:D, slot[2, c], :], start=True, stop=True))
                        elif kind == "qnorm":
                            gate(base)
                            pe.matmul(psm[0:HE, 0:FB], blkq[:, 0, :], squares[:, slot[0, c], :], start=True, stop=False)
                            job(base, lambda: pe.matmul(psm[0:HE, 0:FB], blkq[:, 1, :], squares[:, slot[1, c], :], start=False, stop=True))
                        else:
                            g, x = c
                            gate(base)
                            m = P if g < 2 else D
                            job(base, lambda: pe.matmul(psm[0:m, 0:FB], wall[:, g * P:g * P + m], xt[:, x * FB:(x + 1) * FB], start=True, stop=True))
                    pe.wait_ge(placed, it * 192 + 192)
                    pe.wait_ge(max_placed, it * 48 + 48)

                    def scores(u):
                        n, un = divmod(u, NU)
                        pe.wait_ge(exped, g0 + u + 1)
                        for b, bank in enumerate(units[un]):
                            for col, j, e, q0, w in bank:
                                lhs = kop[:, n, j * P:(j + 1) * P]
                                if e is None:
                                    mm = pe.matmul(pss[:, u % 2, b, 0:NE * w], lhs, qop[:, n, :, q0:q0 + w], start=True, stop=True, skip_group_check=True)
                                else:
                                    mm = pe.matmul(pss[:, u % 2, b, col:col + w], lhs, qop[:, n, e, q0:q0 + w], start=True, stop=True, skip_group_check=True)
                        mm.then_inc(scored, 1)

                    def sums(u):
                        n, un = divmod(u, NU)
                        pe.wait_ge(exped, g0 + u + 3)
                        if dj[un]:
                            pe.wait_ge(masked, it * NM + (NM // NH) * n + order_m[un])
                        for b, bank in enumerate(units[un]):
                            for col, j, e, q0, w in bank:
                                x = tile_of(q0)
                                if j == 0 and e in (0, None):
                                    pe.wait_ge(acc_free, it * 3 * NH + 3 * n + x + 1)
                                r = P if j < NA - 1 else LAST
                                for ee in range(NE) if e is None else (e,):
                                    cc = col + (w * ee if e is None else 0)
                                    mm = pe.matmul(pso[VW * ee:VW * (ee + 1), q0 - QT * x:q0 - QT * x + w], vop[0:r, j, n, :], pb[0:r, u % 3, b, cc:cc + w],
                                                   start=(j == 0), stop=(q0 == P * j if e is not None else j == NA - 1), skip_group_check=True)
                            if un == last_unit[0] and b == last_bank:
                                mm.then_inc(tile_done, 1)
                        mm.then_inc(summed, 1)

                    for u in range(NUB + 1):
                        if u < NUB:
                            scores(u)
                        if u >= 1:
                            sums(u - 1)
                            n = (u - 1) // NU
                            for x in (x for x in range(3) if last_unit[x] == (u - 1) % NU):
                                c = (4 * x, min(4 * x + 4, NA))
                                gate(base)
                                pe.wait_ge(acc_free, it * 3 * NH + 3 * n + x + 2)
                                for a in range(*c):
                                    wd = P if a < NA - 1 else LAST
                                    mm = pe.transpose(psm[0:wd, (a - c[0]) * P:(a - c[0] + 1) * P], ofm[:, (3 * n + x) % 2, (a - c[0]) * P:(a - c[0]) * P + wd], ident[:])
                                job(base, lambda: mm)
                    pe.wait_ge(fx_ok, it + 1)
                    for kind, c in EPI:
                        if kind == "fturn":
                            turn_rows(fx[:].rearrange("p (a n) d -> p a (n d)", n=NH), c, base)
                        elif kind in ("fc1", "fc2"):
                            gate(base)
                            i = kind == "fc2"
                            job(base, lambda: pe.matmul(psm[0:D, 0:FB], fcw[:, int(i), :], (hx1 if i else fxt)[:, c * FB:(c + 1) * FB], start=True, stop=True))
                        else:
                            gate(base)
                            pe.sem_inc(passed, 1)
                            for a in range(*c):
                                mm = pe.transpose(psm[:, (a - c[0]) * D:(a - c[0] + 1) * D], pm[:, a * P:(a + 1) * P], ident[0:D, 0:D])
                            job(base, lambda: mm)
                    assert k[0] == J

            @block.scalar
            def _(act):
                with act.Fori(0, B) as it:
                    g0 = it * NUB
                    act.wait_ge(squared_bound, it + 1)
                    nc.scalar.activation(bound[:], bound[:], ACT.Sqrt).then_inc(rooted, 1)
                    for u in range(NUB):
                        un = u % NU
                        act.wait_ge(scored, g0 + u + 1)
                        act.wait_ge(summed, g0 + u + 1)
                        w = QT if units[un][0][0][2] is not None else NE * LAST
                        nc.scalar.activation(pb[:, u % 3, :, 0:w], pss[:, u % 2, :, 0:w], ACT.Exp, scale=float(HD) ** 0.5).then_inc(exped, 1)
                    for i, (src, s_) in enumerate(((lg[:], logit_exp), (gs[:, 0:NA, :], gate_exp))):
                        act.wait_ge(logit, it * 2 + i + 1)
                        nc.scalar.activation(src, src, ACT.Exp).then_inc(s_, 1)

            @block.gpsimd
            def _(pool):
                pool.memset(mh[:], -0.5).then_inc(mh_ok, 1)
                pool.wait_ge(mh_ok, 1)
                pool.wait_ge(var, 1)
                pool.tensor_tensor(stat[:, 3], stat[:, 2], mh[:], ALU.pow).then_inc(rstd, 1)

                def root(i, it, n):
                    pool.wait_ge(var, it * 3 + i + 2)
                    pool.tensor_tensor(stat[:, 3, 0:n], stat[:, 2, 0:n], mh[:, 0:n], ALU.pow).then_inc(rstd, 1)

                with pool.Fori(0, B) as it:
                    root(0, it, NA)
                    for i, (jb, (g, x)) in enumerate(FEATS):
                        m = P if g < 2 else D
                        dst = (lambda p_: qs[:, p_, g, x * FB:(x + 1) * FB]) if g < 2 else (lambda p_: ks[:, p_, x * FB:(x + 1) * FB])
                        pool.wait_ge(free, it * J + JS + jb + 2)
                        pool.sem_inc(pool_passed, 1)
                        pool.tensor_copy(dst(1), rq[0:m, i % 3, :]).then_inc(part1, 1)
                        pool.wait_ge(part1, it * 9 + i + 1)
                        pool.tensor_tensor(dst(2), rq[0:m, i % 3, :], dst(1), ALU.subtract).then_inc(parts, 1)
                        pool.wait_ge(parts, it * 9 + i + 4)
                    for u in range(NUB):
                        un = u % NU
                        if not dj[un]:
                            continue
                        pool.wait_ge(exped, it * NUB + u + 3)
                        pool.sem_inc(pool_passed, 1)
                        cols = {}
                        for c, b in dj[un]:
                            cols.setdefault(c, []).append(b)
                        n_ = 0
                        for c, bs in sorted(cols.items()):
                            if units[un][bs[0]][0][2] is None:
                                v_ = pb[0:LAST, u % 3, bs[0], 0:NE * LAST].rearrange("p (e q) -> p e q", e=NE)
                                pat = [[0, NE], [1, LAST]]
                            else:
                                v_ = pb[:, u % 3, bs[0]:bs[-1] + 1, c:c + P]
                                pat = [[0, len(bs)], [1, P]]
                            ins = pool.affine_select(out=v_, in_=v_, compare_op=ALU.is_ge, fill=0.0, base=0, pattern=pat, channel_multiplier=-1)
                        ins.then_inc(masked, 1)
                    root(1, it, NA * NH)
                    root(2, it, NA * NH)
                pool.wait_ge(flag_ready, 1)
                pool.partition_all_reduce(bad[:, 1:2], bad[:, 0:1], channels=P, reduce_op=RMAX).then_inc(bad_ready, 1)

            @block.vector
            def _(v):
                tt, ts, stt, cp = nc.vector.tensor_tensor, nc.vector.tensor_scalar, nc.vector.scalar_tensor_tensor, nc.vector.tensor_copy
                red = nc.vector.tensor_reduce
                k = [0]
                nc.vector.memset(wbd[:], 0.0).then_inc(wbd_zero, 1)
                nc.vector.memset(fcw[:], 0.0).then_inc(wbd_zero, 1)
                ch = Chain(v, dve)
                ch.step(nc.vector.memset(xt[D:D + 1], 1.0))
                ch.step(nc.vector.memset(fxt[D:D + 1], 1.0))
                ch.step(nc.vector.memset(hx1[D:D + 1], 1.0))
                ch.step(nc.vector.memset(vop[:], 0.0))
                ch.step(nc.vector.memset(vop[:, :, :, HD:HD + 1], 1.0))
                ch.step(nc.vector.memset(ot[:], 1.0))
                nc.vector.memset(kop[KT:KM], -1.0).then_inc(const_ok, 1)
                nc.vector.memset(good[:], 1.0).then_inc(const_ok, 1)

                def take(base):
                    v.wait_ge(full, base + k[0] + 1)

                def give(ins):
                    ins.then_inc(free, 1)
                    k[0] += 1

                take(0)
                give(cp(wall[:], psm[0:D + 1, 0:448]))
                v.wait_ge(r_load, 64)
                norm_groups(nc, v, ch, var, rstd, 1, h4[:], h4[:], tmp[:], stat, 4 * NA, D, EPS)
                ch.wait()
                cp(stat[:, 0, 0:1], stat[:, 1, 0:1]).then_inc(xn_ok, 1)
                for n in range(4):
                    for c in chunks:
                        take(0)
                        give(cp(xt[0:D, c[0] * P:c[1] * P], psm[0:D, 0:(c[1] - c[0]) * P]))
                    for c in chunks:
                        take(0)
                        give(cp(resid[:, c[0]:c[1], HD * n:HD * n + HD], psm[:, 0:(c[1] - c[0]) * HD].rearrange("p (a d) -> p a d", d=HD)))
                assert k[0] == JS
                n_setup = ch.n
                v.wait_ge(free, JS + 1)
                with v.Fori(0, B) as it:
                    k[0] = 0
                    base = it * J + JS
                    ch = Chain(v, dve, it * NDVE + n_setup)
                    v.wait_ge(h_load, it * 16 + 16)
                    ch.step(cp(tmp[:, NA:2 * NA, :], hb[:]))
                    norm_groups(nc, v, ch, var, rstd, it * 3 + 2, xn[:], tmp[:, NA:2 * NA, :], tmp[:, 0:NA, :], stat, NA, D, EPS)
                    cp(stat[:, 0, 0:1], stat[:, 1, 0:1]).then_inc(xn_ok, 1)
                    for kind, c in PRO:
                        take(base)
                        if kind == "turn":
                            give(cp(xt[0:D, c[0] * P:c[1] * P], psm[0:D, 0:(c[1] - c[0]) * P]))
                        elif kind == "tok":
                            pv = psm[:].rearrange("p (a s x) -> p a s x", s=2, x=D)[:, 0:c[1] - c[0]]
                            ch.done(cp(vop[:, c[0]:c[1], :, 0:HD], pv[:, :, 0, :].rearrange("p a (n d) -> p a n d", d=HD)))
                            give(ts(msk[:, c[0]:c[1], :], pv[:, :, 1, :], 0.0, None, ALU.not_equal))
                        elif kind == "knorm":
                            give(red(kmax[:, c:c + 1], psm[0:HE, 0:FB], AX.X, ALU.max))
                            if c == 2:
                                v.wait_ge(free, base + k[0] + 1)
                                ch.step(red(kmax[:, 3:4], kmax[:, 0:3], AX.X, ALU.max))
                        elif kind == "qnorm":
                            give(ts(bound[:, c * FB:(c + 1) * FB], psm[0:HE, 0:FB], kmax[:, 3:4], ROUNDING, ALU.mult, ALU.mult))
                        else:
                            g, x = c
                            i = [f for _, f in FEATS].index(c)
                            m = P if g < 2 else D
                            p0 = qs[:, 0, g, x * FB:(x + 1) * FB] if g < 2 else ks[:, 0, x * FB:(x + 1) * FB]
                            ch.step(cp(p0, psm[0:m, 0:FB]))
                            ch.step(tt(squares[0:m, slot[c], :], p0, p0, ALU.mult))
                            v.wait_ge(parts, it * 9 + i + 1)
                            give(tt(rq[0:m, i % 3, :], psm[0:m, 0:FB], p0, ALU.subtract))
                    v.wait_ge(free, base + k[0] + 1)
                    tt(bound[0:1, 0:1], bound[0:1, 0:1], bound[0:1, 0:1], ALU.max).then_inc(squared_bound, 1)
                    v.wait_ge(rooted, it + 1)
                    ch.step(ts(bound[:], bound[:], -SHIFT / float(HD) ** 0.5, None, ALU.add))
                    ch.step(cp(mt[:, 0, :], bound[:]))
                    ch.step(tt(bound[:], bound[:], mt[:, 0, :], ALU.subtract))
                    ch.step(cp(mt[:, 1, :], bound[:]))
                    tt(mt[:, 2, :], bound[:], mt[:, 1, :], ALU.subtract).then_inc(max_split, 1)
                    vals = tmp[:].rearrange("p a d -> p (a d)")[:, 0:NA * D]
                    ch.step(tt(vals.rearrange("p (a n d) -> p a n d", n=NH, d=HD), vop[:, :, :, 0:HD], vop[:, :, :, 0:HD], ALU.mult))
                    ch.step(ts(vals, vals, VALUE_MAX ** 2, None, ALU.is_le))
                    ch.step(red(good[:, 1:2], vals, AX.X, ALU.min))
                    ch.step(tt(good[:, 0:1], good[:, 0:1], good[:, 1:2], ALU.min))
                    for n in range(NH):
                        for x in range(3):
                            w = QT if x < 2 else LAST
                            if x == 0:
                                v.wait_ge(tile_done, it * NH + n + 1)
                            else:
                                v.wait_ge(summed, it * NUB + n * NU + last_unit[x] + 4)
                            cp(ofm[:, (3 * n + x) % 2, 0:w], pso[:, 0:w]).then_inc(acc_free, 1)
                            take(base)
                            c = (4 * x, min(4 * x + 4, NA))
                            dst = ot[:].rearrange("p (a n) e w -> p a n (e w)", n=NH)
                            if x < 2:
                                give(cp(dst[:, c[0]:c[1], n, :], psm[:].rearrange("p (a w) -> p a w", w=P)))
                            else:
                                give(cp(dst[0:LAST, NA - 1, n, :], psm[0:LAST, 0:P]))
                    v.wait_ge(free, base + k[0] + 1)
                    G = NA * NH
                    ch.step(ts(lg[:], ot[:, :, :, HD], SUM_MIN, None, ALU.is_ge))
                    ch.step(red(good[:, 1:2], lg[:].rearrange("p g e -> p (g e)"), AX.X, ALU.min))
                    ch.step(tt(good[:, 0:1], good[:, 0:1], good[:, 1:2], ALU.min))
                    ch.step(nc.vector.reciprocal(rec[:], ot[:, :, :, HD]))
                    onv = on[:].rearrange("p g (e d) -> p g e d", d=HD)
                    ch.step(tt(onv, ot[:, :, :, 0:HD], bcast(rec[:], HD), ALU.mult))
                    ch.step(tt(onv, onv, bmid(msk[:].rearrange("p a (n d) -> p (a n) d", d=HD), NE), ALU.mult))
                    on4 = on[:].rearrange("p (a n) f -> p a n f", n=NH)
                    tm4 = tmp[:].rearrange("p (a n) f -> p a n f", n=NH)
                    gwv = gw[:].rearrange("p (n e f) -> p e n f", n=NH, f=64)
                    for e in range(NE):
                        for a in range(NA):
                            ch.done(tt(tm4[:, a], on4[:, a], gwv[:, e], ALU.mult))
                        ch.wait()
                        ch.step(red(lg[:, :, e:e + 1], tmp[:], AX.X, ALU.add))
                    ch.step(tt(lg[:].rearrange("p (a n) e -> p a (n e)", n=NH), lg[:].rearrange("p (a n) e -> p a (n e)", n=NH), bmid(gb[:], NA), ALU.add))
                    ch.step(red(mx[:], lg[:], AX.X, ALU.max))
                    tt(lg[:], lg[:], bcast(mx[:], NE), ALU.subtract).then_inc(logit, 1)
                    v.wait_ge(logit_exp, it + 1)
                    ch.step(red(mx[:], lg[:], AX.X, ALU.add))
                    ch.step(nc.vector.reciprocal(mx[:], mx[:]))
                    ch.step(tt(lg[:], lg[:], bcast(mx[:], NE), ALU.mult))
                    ch.step(tt(tmp[:].rearrange("p g (e d) -> p g e d", d=HD), onv, bcast(lg[:], HD), ALU.mult))
                    ch.step(red(mix[:], tmp[:].rearrange("p g (e d) -> p g d e", d=HD), AX.X, ALU.add))
                    ch.step(tt(mix[:], mix[:], resid[:].rearrange("p a (n d) -> p (a n) d", d=HD), ALU.add))
                    t16 = tmp[:, :, 0:HD]
                    norm_groups(nc, v, ch, var, rstd, it * 3 + 3, fx[:], mix[:], t16, stat, G, HD, FEPS)
                    ch.step(tt(fx[:], fx[:], bmid(vec[:, 0, :], G), ALU.mult))
                    tt(fx[:], fx[:], bmid(vec[:, 1, :], G), ALU.add).then_inc(fx_ok, 1)
                    for kind, c in EPI:
                        take(base)
                        if kind == "fturn":
                            give(cp(fxt[0:D, c[0] * P:c[1] * P], psm[0:D, 0:(c[1] - c[0]) * P]))
                        elif kind == "fc1":
                            s_ = slice(c * FB, (c + 1) * FB)
                            if c == 0:
                                v.wait_ge(free, base + k[0] + 1)
                                ch.step(ts(pm[:], fxt[0:D], 0.0, None, ALU.not_equal))
                            give(stt(hx1[0:D, s_], psm[0:D, 0:FB], 0.0, pm[:, s_], ALU.max, ALU.mult))
                        elif kind == "fc2":
                            s_ = slice(c * FB, (c + 1) * FB)
                            ch.step(tt(pm[:, s_], psm[0:D, 0:FB], pm[:, s_], ALU.mult))
                            give(tt(pm[:, s_], pm[:, s_], fxt[0:D, s_], ALU.add))
                        else:
                            give(cp(fo[:].rearrange("p (a n) d -> p a (n d)", n=NH)[:, c[0]:c[1], :], psm[:, 0:(c[1] - c[0]) * D].rearrange("p (a d) -> p a d", d=D)))
                    assert k[0] == J
                    v.wait_ge(free, base + k[0] + 1)
                    norm_groups(nc, v, ch, var, rstd, it * 3 + 4, fx[:], fo[:], t16, stat, G, HD, FEPS)
                    ch.step(tt(fx[:], fx[:], bmid(vec[:, 2, :], G), ALU.mult))
                    ch.step(tt(fx[:], fx[:], bmid(vec[:, 3, :], G), ALU.add))
                    fa = fx[:].rearrange("p (a n) d -> p a (n d)", n=NH)
                    for n in range(NH):
                        ch.step(tt(tmp[:, 0:NA, :], fa, bmid(fgw[:, n, :], NA), ALU.mult))
                        ch.step(red(gs[:, 0:NA, n:n + 1], tmp[:, 0:NA, :], AX.X, ALU.add))
                    gg = gs[:, 0:NA, :]
                    ch.step(red(mx[:, 0:NA], gg, AX.X, ALU.max))
                    tt(gg, gg, bcast(mx[:, 0:NA], NH), ALU.subtract).then_inc(logit, 1)
                    v.wait_ge(gate_exp, it + 1)
                    ch.step(red(mx[:, 0:NA], gg, AX.X, ALU.add))
                    ch.step(nc.vector.reciprocal(mx[:, 0:NA], mx[:, 0:NA]))
                    ch.step(tt(gg, gg, bcast(mx[:, 0:NA], NH), ALU.mult))
                    ch.step(tt(fx[:].rearrange("p (a n) d -> p a n d", n=NH), fx[:].rearrange("p (a n) d -> p a n d", n=NH), bcast(gg, HD), ALU.mult))
                    v.wait_ge(stored, it * 32 + 16)
                    tt(res[:], hb[:], fa, ALU.add).then_inc(result, 1)
                    assert ch.n == NDVE, ch.n
                ts(bad[:, 0:1], good[:, 0:1], -1.0, 1.0, ALU.mult, ALU.add).then_inc(flag_ready, 1)
                v.wait_ge(bad_ready, 1)
                cp(flag[:], bad[:, 1:2]).then_inc(flag_ok, 1)


def consts():
    t = np.arange(PATCH)[None, :]
    f = np.arange(F)[:, None]
    w = 2 * np.pi * f * t / PATCH
    k = np.arange(KC * P) * (np.arange(KC * P) < KH)
    tan = np.tan(np.pi * k / L)
    both = np.concatenate([tan, -tan])
    m = (np.arange(KH)[:, None] * (L - 1 - np.arange(L))[None, :]) % L
    wt = np.where(np.arange(KH) == 0, 0.5, 1.0)[:, None] / L
    half = np.repeat([[1.0, 0.0, -1.0, 0.0], [-1.0, -1.0, 0.0, 0.0]], D, 0)
    heads = np.arange(P) // (P // 8)
    c = {
        "c_blkq": (heads[:, None, None] + 8 * np.arange(2)[None, :, None]) == np.arange(16),
        "c_blkk": (np.arange(D) // 16)[:, None] == np.arange(16) // 4,
        "c_dft": np.concatenate([np.cos(w), -np.sin(w)], 0) / np.sqrt(PATCH),
        "c_ident": np.eye(P),
        "c_fold": np.concatenate([np.eye(D), np.eye(D)], 0),
        "c_tanrow": both,
        "c_tancol": both.reshape(2 * KC, P).T,
        "c_halves": half,
        "c_cos": wt * np.cos(2 * np.pi * m / L),
        "c_sin": -wt * np.sin(2 * np.pi * m / L),
    }
    return {k: np.ascontiguousarray(v.astype(np.float32)) for k, v in c.items()}


def kernel(**inputs):
    import numpy as _np
    import concourse.bacc as _bacc
    from concourse import mybir as _mybir
    from concourse.bass_utils import run_bass_kernel_spmd as _run

    nc = _bacc.Bacc("TRN2", target_bir_lowering=False, num_devices=1)
    arrays, aps = {}, {}
    for name, a in {**inputs, **consts()}.items():
        a = _np.ascontiguousarray(a)
        arrays["in_" + name] = a
        aps[name] = nc.dram_tensor("in_" + name, a.shape, _mybir.dt.from_np(a.dtype), kind="ExternalInput").ap()
    out = nc.dram_tensor("out", (B, L, D), F32, kind="ExternalOutput").ap()
    h1 = nc.dram_tensor("h1", (B, LP, D), F32).ap()
    taps = nc.dram_tensor("taps", (D, KREV), F32).ap()
    h2 = nc.dram_tensor("h2", (B, LP, D), F32).ap()
    stage_embed(nc, aps, h1)
    stage_taps(nc, aps, taps)
    stage_ssm(nc, aps, h1, taps, h2)
    retry = nc.dram_tensor("retry", (1, 1), I32).ap()
    stage_ffn_bounded(nc, aps, h2, out, retry)
    stage_ffn_exact(nc, aps, h2, out, retry)
    r = _run(nc, [arrays], core_ids=[0])
    return r.results[0]["out"]
```

```python
from contextlib import ExitStack

import numpy as np
import concourse.bass as bass
from concourse import mybir

F32 = mybir.dt.float32
BF16 = mybir.dt.bfloat16
I32 = mybir.dt.int32
ACT = mybir.ActivationFunctionType
ALU = mybir.AluOpType
AX = mybir.AxisListType
RMAX = bass.bass_isa.ReduceOp.max

P = 128
B, C, T, V = 8, 64, 128, 64
D = 64
PATCH, STRIDE = 16, 8
NP = (T + STRIDE - PATCH) // STRIDE + 1
F = PATCH // 2 + 1
TXT = 77
IMG = V * NP
L = IMG + TXT
NA = -(-L // P)
LP = NA * P
VOCAB, NOPS = 256, 64
NLEAF, NOP = 8, 7
EPS = 1e-5


def bcast(ap, n):
    return bass.AP(ap.tensor, ap.offset, [*[list(x) for x in ap.ap], [0, n]])


def bmid(ap, n):
    a = [list(x) for x in ap.ap]
    return bass.AP(ap.tensor, ap.offset, [*a[:-1], [0, n], a[-1]])


def rows(ap, n):
    return bass.AP(ap.tensor, ap.offset, [[0, n], *[list(x) for x in ap.ap]])


class Chain:

    def __init__(self, eng, sem, base=0):
        self.eng, self.sem, self.base, self.n = eng, sem, base, 0

    def done(self, ins):
        ins.then_inc(self.sem, 1)
        self.n += 1
        return self.n

    def wait(self, n=None):
        self.eng.wait_ge(self.sem, self.base + (self.n if n is None else n))

    def step(self, ins):
        self.done(ins)
        self.wait()


def stage_embed(nc, t, h1d):
    KB = PATCH * C // P // 2
    with ExitStack() as ctx:
        sb = lambda n, s, d=F32: ctx.enter_context(nc.sbuf_tensor(n, s, d))
        ps = lambda n, s: ctx.enter_context(nc.psum_tensor(n, s, F32))
        sem = lambda n: ctx.enter_context(nc.semaphore(n))
        wf = sb("wf", [2 * F, D, 2, C])
        dft = sb("dft", [2 * F, PATCH])
        g = sb("g", [P, KB, 2, D])
        ident = sb("ident", [P, P])
        fold = sb("fold", [P, D])
        x = sb("x", [P, 2, NP, KB * V])
        xe = sb("xe", [P, B, V])
        ye = sb("ye", [P, B, V])
        y = sb("y", [P, 2, V, NP])
        h = sb("h", [P, NA, B, D])
        comp = sb("comp", [P, 2, D])
        compc = sb("compc", [P, 2, D])
        compq = sb("compq", [P, 2, D])
        compt = sb("compt", [D, 2, P])
        opemb = sb("opemb", [NOPS, D])
        opt = sb("opt", [D, NOPS])
        w0 = sb("w0", [D, D])
        wlr = sb("wlr", [D, 2, D])
        w12 = sb("w12", [P, D])
        bb = sb("bb", [P, D])
        gam = sb("gam", [P, D])
        bet = sb("bet", [P, D])
        tlr = sb("tlr", [P, 2, 2, D])
        top = sb("top", [NOPS, D])
        ids = sb("ids", [TXT, B], I32)
        idf = sb("idf", [TXT, B])
        keep = sb("keep", [TXT, B])
        leaf = sb("leaf", [TXT, B, NLEAF], I32)
        opi = sb("opi", [TXT, B, NOP], I32)
        gl = sb("gl", [TXT, B, 4, D])
        gr = sb("gr", [TXT, B, 4, D])
        go = sb("go", [TXT, B, NOP, D])
        tx = sb("tx", [TXT, 32, D])
        tq = sb("tq", [TXT, 32, D])
        tt = sb("tt", [P, 16, TXT])
        st = sb("st", [P, 4, 32])
        mhalf = sb("mhalf", [P, 32])
        tl_d = nc.dram_tensor("tl_d", [VOCAB, D], F32).ap()
        tr_d = nc.dram_tensor("tr_d", [VOCAB, D], F32).ap()
        to_d = nc.dram_tensor("to_d", [NOPS, D], F32).ap()
        psy = ps("psy", [P, 2, 2, 512])
        pst = ps("pst", [P, 2, 512])
        psw = ps("psw", [P, 2, 512])

        s_w, s_txt, s_e, s_id = sem("weights_loaded"), sem("text_loaded"), sem("edges_loaded"), sem("ids_loaded")
        s_x = [sem("x0_loaded"), sem("x1_loaded")]
        g_ready, g_copied = sem("g_ready"), sem("g_copied")
        y_done = [sem("y0_done"), sem("y1_done")]
        lo_out = [sem("y0_low_copied"), sem("y1_low_copied")]
        hi_out = [sem("y0_high_copied"), sem("y1_high_copied")]
        t_done = [sem("t0_done"), sem("t1_done")]
        t_out = [sem("t0_copied"), sem("t1_copied")]
        h_out = sem("h_stored")
        ye_done, ye_out = sem("ye_done"), sem("ye_copied")
        dve = sem("vector_steps")
        pool_ready, pool_var, pool_r = sem("pool_ready"), sem("variance_ready"), sem("rstd_ready")
        tab_t, tab_tc, tab_m, tab_c, tab_s = sem("tab_turned"), sem("tab_turned_copied"), sem("tab_mult"), sem("tab_copied"), sem("tab_stored")
        s_rows = sem("id_rows")
        s_gath = sem("gathered")
        l_src, l_t, l_tc, l_m = sem("level_ready"), sem("level_turned"), sem("level_copied"), sem("level_mult")
        pad_z = sem("pad_zero")
        txt_ok = sem("text_done")
        comp_ready = sem("vocabulary_normed")

        wfv = t["L0_tok_W"].rearrange("d (f c) -> f d c", c=C)
        xv = t["x"].rearrange("b c (j u r) v -> b u c j (r v)", u=2, r=KB)
        lr = t["L0_txt_W_bin"].rearrange("(s k) d -> k s d", k=D)

        with nc.Block() as block:
            @block.sync
            def _(sp):
                for u in range(2):
                    sp.dma_start(wf[:, :, u, :], wfv).then_inc(s_w, 16)
                sp.dma_start(dft[:], t["c_dft"]).then_inc(s_w, 16)
                sp.dma_start(ident[:], t["c_ident"]).then_inc(s_w, 16)
                sp.dma_start(fold[:], t["c_fold"]).then_inc(s_w, 16)
                sp.dma_start(ids[:], t["x_txt"].rearrange("b k -> k b"), allow_slow_non_contiguous=True).then_inc(s_id, 16)
                for u in range(2):
                    sp.dma_start(xe[u * C:(u + 1) * C], t["x"][:, :, T - 1, :].rearrange("b c v -> c b v")).then_inc(s_e, 16)
                sp.dma_start(comp[:], t["L0_txt_comp_emb"].rearrange("(h p) d -> p h d", p=P)).then_inc(s_txt, 16)
                sp.dma_start(opemb[:], t["L0_txt_op_emb"]).then_inc(s_txt, 16)
                sp.dma_start(w0[:], t["L0_txt_W_bin"][0:D, :]).then_inc(s_txt, 16)
                sp.dma_start(wlr[:], lr[:, 1:3, :]).then_inc(s_txt, 16)
                sp.dma_start(w12[:], t["L0_txt_W_bin"][D:3 * D, :]).then_inc(s_txt, 16)
                sp.dma_start(bb[:], rows(t["L0_txt_b_bin"], P)).then_inc(s_txt, 16)
                sp.dma_start(gam[:], rows(t["L0_txt_gamma"], P)).then_inc(s_txt, 16)
                sp.dma_start(bet[:], rows(t["L0_txt_beta"], P)).then_inc(s_txt, 16)
                for k in range(2):
                    for q in (y_done, lo_out, hi_out, t_done, t_out):
                        sp.sem_inc(q[k], 1)
                with sp.Fori(0, B // 2) as it:
                    for k in range(2):
                        for u in range(2):
                            sp.wait_ge(y_done[k], it * 2 + 1)
                            sp.dma_start(x[u * C:(u + 1) * C, k], xv[it * 2 + k, u]).then_inc(s_x[k], 16)

            @block.tensor
            def _(pe):
                pe.wait_ge(s_w, 80)
                for d in range(D):
                    mm = pe.matmul(psw[:, d // 32, (d % 32) * PATCH:(d % 32 + 1) * PATCH], wf[:, d, :, :], dft[:], start=True, stop=True)
                mm.then_inc(g_ready, 1)
                pe.wait_ge(s_txt, 128)
                pe.wait_ge(comp_ready, 1)
                for v in range(2):
                    pe.transpose(pst[0:D, 0, v * P:(v + 1) * P], comp[:, v, :], ident[:])
                pe.transpose(pst[0:D, 0, 2 * P:2 * P + NOPS], opemb[:], ident[0:NOPS, 0:NOPS]).then_inc(tab_t, 1)
                pe.wait_ge(tab_tc, 2)
                for v in range(2):
                    pe.matmul(pst[:, 1, v * P:(v + 1) * P], compt[:, v, :], wlr[:], start=True, stop=True)
                pe.matmul(pst[0:NOPS, 1, 2 * P:2 * P + D], opt[:], w0[:], start=True, stop=True).then_inc(tab_m, 1)
                pe.wait_ge(g_copied, 4)
                pe.wait_ge(s_e, 32)
                for r in range(KB):
                    mm = pe.matmul(psw[:, 0, :], g[:, r], xe[:], start=(r == 0), stop=(r == KB - 1))
                mm.then_inc(ye_done, 1)
                pe.wait_ge(tab_c, 2)
                pe.wait_ge(ye_out, 1)
                with pe.Fori(0, B // 2) as it:
                    for k in range(2):
                        for j in range(2):
                            pe.wait_ge(s_x[k], it * 32 + 32)
                            pe.wait_ge(lo_out[k], it * 2 + 1)
                            pe.wait_ge(hi_out[k], it * 3 + 1)
                            for r in range(KB):
                                mm = pe.matmul(psy[:, k, j, :], g[:, r], x[:, k, 8 * j:8 * j + 8, r * V:(r + 1) * V], start=(r == 0), stop=(r == KB - 1))
                            mm.then_inc(y_done[k], 1)
                    for k in range(2):
                        pe.wait_ge(lo_out[k], it * 2 + 3)
                        pe.wait_ge(hi_out[k], it * 3 + 4)
                        pe.wait_ge(t_out[k], it + 1)
                        for a in range(8):
                            mm = pe.matmul(pst[:, k, a * D:(a + 1) * D], y[:, k, 8 * a:8 * a + 8, :], fold[:], start=True, stop=True)
                        mm.then_inc(t_done[k], 1)
                for lv, n in ((0, 16), (1, 8)):
                    pe.wait_ge(l_src, lv + 1)
                    for i in range(n):
                        mm = pe.transpose(psw[:, i // 4 % 2, (i % 4) * P:(i % 4) * P + TXT], tx[:, 2 * i:2 * i + 2, :], ident[0:TXT, 0:TXT])
                        if i % 4 == 3:
                            mm.then_inc(l_t, 1)
                            if i // 4 % 2 == 1 and i < n - 1:
                                pe.wait_ge(l_tc, 4 * lv + i // 4 + 1)
                    pe.wait_ge(l_tc, 4 * lv + n // 4)
                    for i in range(n):
                        mm = pe.matmul(pst[0:TXT, i // 8, (i % 8) * D:(i % 8 + 1) * D], tt[:, i, :], w12[:], start=True, stop=True)
                    mm.then_inc(l_m, 1)

            @block.scalar
            def _(act):
                act.wait_ge(ye_done, 1)
                act.wait_ge(tab_c, 2)
                act.dma_start(tl_d.rearrange("(h p) d -> p h d", p=P), tlr[:, :, 0, :]).then_inc(tab_s, 16)
                act.dma_start(tr_d.rearrange("(h p) d -> p h d", p=P), tlr[:, :, 1, :]).then_inc(tab_s, 16)
                act.dma_start(to_d, top[:]).then_inc(tab_s, 16)
                nc.scalar.copy(ye[:].rearrange("p b v -> p (b v)"), psw[:, 0, :]).then_inc(ye_out, 1)
                with act.Fori(0, B // 2) as it:
                    for k in range(2):
                        for j in range(2):
                            act.wait_ge(y_done[k], it * 2 + j + 2)
                            act.wait_ge(t_done[k], it + 1)
                            nc.scalar.copy(y[0:D, k, :, 8 * j:8 * j + 8], psy[0:D, k, j, :].rearrange("p (j v) -> p v j", v=V)).then_inc(lo_out[k], 1)
                for lv, n in ((0, 4), (1, 2)):
                    act.wait_ge(l_m, lv)
                    for i in range(n):
                        act.wait_ge(l_t, 4 * lv + i + 1)
                        nc.scalar.copy(tt[:, 4 * i:4 * i + 4, :], psw[:, i % 2, :].rearrange("p (q k) -> p q k", k=P)[:, :, 0:TXT]).then_inc(l_tc, 1)
                for k in range(2):
                    act.wait_ge(t_out[k], B // 2 + 1)
                act.wait_ge(txt_ok, 1)
                act.dma_start(h1d.rearrange("b (a p) d -> p a b d", p=P)[:, NA - 1], h[:, NA - 1]).then_inc(h_out, 16)
                with act.Fori(0, B) as b:
                    act.dma_start(h1d[b].rearrange("(a p) d -> p a d", p=P)[:, 0:8, :], h[:, 0:8, b, :]).then_inc(h_out, 16)
                act.wait_ge(h_out, 16 * (B + 1))

            @block.gpsimd
            def _(pool):
                pool.memset(mhalf[:], -0.5).then_inc(pool_ready, 1)
                pool.wait_ge(pool_ready, 1)
                pool.memset(h[64:128, NA - 1], 0.0).then_inc(pad_z, 1)
                pool.wait_ge(s_id, 16)
                for b in range(B):
                    pool.indirect_dma_start(leaf[:, b, :], None, t["L0_txt_leaf_ids"], bass.IndirectOffsetOnAxis(ap=ids[:, b:b + 1], axis=0)).then_inc(s_rows, 16)
                    pool.indirect_dma_start(opi[:, b, :], None, t["L0_txt_op_ids"], bass.IndirectOffsetOnAxis(ap=ids[:, b:b + 1], axis=0)).then_inc(s_rows, 16)
                pool.wait_ge(pad_z, 1)
                pool.wait_ge(pool_var, 1)
                pool.tensor_tensor(st[:, 3, 0:2], st[:, 2, 0:2], mhalf[:, 0:2], ALU.pow).then_inc(pool_r, 1)
                pool.wait_ge(tab_s, 48)
                pool.wait_ge(s_rows, 32 * B)
                for b in range(B):
                    for j in range(4):
                        pool.indirect_dma_start(gl[:, b, j, :], None, tl_d, bass.IndirectOffsetOnAxis(ap=leaf[:, b, 2 * j:2 * j + 1], axis=0)).then_inc(s_gath, 16)
                        pool.indirect_dma_start(gr[:, b, j, :], None, tr_d, bass.IndirectOffsetOnAxis(ap=leaf[:, b, 2 * j + 1:2 * j + 2], axis=0)).then_inc(s_gath, 16)
                    for j in range(NOP):
                        pool.indirect_dma_start(go[:, b, j, :], None, to_d, bass.IndirectOffsetOnAxis(ap=opi[:, b, j:j + 1], axis=0)).then_inc(s_gath, 16)
                for lv, n in enumerate((32, 16, 8)):
                    pool.wait_ge(pool_var, 2 + lv)
                    pool.tensor_tensor(st[0:TXT, 3, 0:n], st[0:TXT, 2, 0:n], mhalf[0:TXT, 0:n], ALU.pow).then_inc(pool_r, 1)

            @block.vector
            def _(v):
                ch = Chain(v, dve)

                def layer_norm(out, src, tmp, n, p, which, ready):
                    ch.step(nc.vector.tensor_reduce(st[0:p, 0, 0:n], src, AX.X, ALU.add))
                    ch.step(nc.vector.tensor_scalar(st[0:p, 1, 0:n], st[0:p, 0, 0:n], -1.0 / D, None, ALU.mult))
                    ch.step(nc.vector.tensor_tensor(src, src, bcast(st[0:p, 1, 0:n], D), ALU.add))
                    ch.step(nc.vector.tensor_tensor(tmp, src, src, ALU.mult))
                    ch.step(nc.vector.tensor_reduce(st[0:p, 0, 0:n], tmp, AX.X, ALU.add))
                    nc.vector.tensor_scalar(st[0:p, 2, 0:n], st[0:p, 0, 0:n], 1.0 / D, EPS, ALU.mult, ALU.add).then_inc(pool_var, 1)
                    v.wait_ge(pool_r, which)
                    ch.step(nc.vector.tensor_tensor(tmp, src, bcast(st[0:p, 3, 0:n], D), ALU.mult))
                    ch.step(nc.vector.tensor_tensor(tmp, tmp, bmid(gam[0:p], n), ALU.mult))
                    nc.vector.tensor_tensor(out, tmp, bmid(bet[0:p], n), ALU.add).then_inc(ready, 1)

                v.wait_ge(g_ready, 1)
                for u in range(2):
                    for q in range(2):
                        src = psw[u * C:(u + 1) * C, q, :].rearrange("p (d h w r) -> p w r h d", h=2, w=2, r=KB)[:, u]
                        for hf in range(2):
                            ins = nc.vector.tensor_copy(g[u * C:(u + 1) * C, :, hf, 32 * q:32 * q + 32], src[:, :, hf, :])
                        ins.then_inc(g_copied, 1)
                v.wait_ge(s_txt, 128)
                layer_norm(comp[:], comp[:], compq[:], 2, P, 1, comp_ready)
                v.wait_ge(tab_t, 1)
                nc.vector.tensor_copy(compt[:], pst[0:D, 0, 0:2 * P].rearrange("p (h k) -> p h k", k=P)).then_inc(tab_tc, 1)
                nc.vector.tensor_copy(opt[:], pst[0:D, 0, 2 * P:2 * P + NOPS]).then_inc(tab_tc, 1)
                v.wait_ge(tab_m, 1)
                nc.vector.tensor_copy(tlr[:].rearrange("p h s d -> p (h s d)"), pst[:, 1, 0:2 * P]).then_inc(tab_c, 1)
                nc.vector.tensor_tensor(top[:], pst[0:NOPS, 1, 2 * P:2 * P + D], bb[0:NOPS], ALU.add).then_inc(tab_c, 1)
                with v.Fori(0, B // 2) as it:
                    for k in range(2):
                        hi = slice(D, P)
                        src = psy[hi, k].rearrange("p q (j v) -> p v (q j)", v=V)
                        for j in range(2):
                            v.wait_ge(y_done[k], it * 2 + j + 2)
                            v.wait_ge(t_done[k], it + 1)
                            if j == 0:
                                nc.vector.tensor_copy(y[hi, k, :, 0:7], src[:, :, 1:8]).then_inc(hi_out[k], 1)
                            else:
                                nc.vector.tensor_copy(y[hi, k, :, 7:15], src[:, :, 8:16]).then_inc(hi_out[k], 1)
                        v.wait_ge(ye_out, 1)
                        nc.vector.tensor_copy(y[hi, k, :, 15], ye[hi, it * 2 + k, :]).then_inc(hi_out[k], 1)
                    for k in range(2):
                        v.wait_ge(t_done[k], it + 2)
                        nc.vector.tensor_copy(h[:, 0:8, it * 2 + k, :], pst[:, k, :].rearrange("p (a d) -> p a d", d=D)).then_inc(t_out[k], 1)
                v.wait_ge(s_gath, 16 * B * 15)
                v.wait_ge(s_id, 16)
                ch.step(nc.vector.tensor_copy(idf[:], ids[:]))
                ch.step(nc.vector.tensor_scalar(keep[:], idf[:], 1.0, None, ALU.is_gt))
                txv = tx[:].rearrange("p (b j) d -> p b j d", b=B)
                ch.step(nc.vector.tensor_tensor(gl[:], gl[:], gr[:], ALU.add))
                ch.step(nc.vector.tensor_tensor(gl[:], gl[:], go[:, :, 0:4, :], ALU.add))
                layer_norm(tx[:], gl[:].rearrange("p b j d -> p (b j) d"), tq[:], 32, TXT, 2, l_src)
                for lv, (n, off) in enumerate(((16, 4), (8, 6))):
                    v.wait_ge(l_m, lv + 1)
                    m = n // B
                    for q in range(n // 8):
                        bs = slice(q * 8 // m, (q + 1) * 8 // m)
                        ch.step(nc.vector.tensor_tensor(
                            tx[:, 8 * q:8 * q + 8, :].rearrange("p (b j) d -> p b j d", j=m),
                            pst[0:TXT, q, :].rearrange("p (b j d) -> p b j d", j=m, d=D),
                            go[:, bs, off:off + m, :], ALU.add))
                    layer_norm(tx[:, 0:n], tx[:, 0:n], tq[:, 0:n], n, TXT, 3 + lv, l_src)
                v.wait_ge(l_src, 3)
                v.wait_ge(pad_z, 1)
                nc.vector.tensor_tensor(h[0:TXT, NA - 1], tx[:, 0:B], bcast(keep[:], D), ALU.mult).then_inc(txt_ok, 1)


KH = (L + 1) // 2
KC = -(-KH // P)
KREV = LP + P
AP_ = NA + 3
NT = NA // 3
HC = 4
FT = 3
FW = L // FT


def norm_rows(nc, v, ch, pool_var, pool_r, which, out, src, tmp, stat, n, p=P, cut=None):
    fold = (lambda x: x.rearrange("p (a b) -> p a b", b=cut)) if cut else (lambda x: x)
    ch.step(nc.vector.tensor_reduce(stat[0:p, 0, 0:n], src, AX.X, ALU.add))
    ch.step(nc.vector.tensor_scalar(stat[0:p, 1, 0:n], stat[0:p, 0, 0:n], -1.0 / D, None, ALU.mult))
    ch.step(nc.vector.tensor_tensor(src, src, bcast(stat[0:p, 1, 0:n], D), ALU.add))
    ch.step(nc.vector.tensor_tensor(tmp, src, src, ALU.mult))
    ch.step(nc.vector.tensor_reduce(stat[0:p, 0, 0:n], tmp, AX.X, ALU.add))
    nc.vector.tensor_scalar(stat[0:p, 2, 0:n], stat[0:p, 0, 0:n], 1.0 / D, EPS, ALU.mult, ALU.add).then_inc(pool_var, 1)
    v.wait_ge(pool_r, which)
    return ch.done(nc.vector.tensor_tensor(out, *((x.rearrange("p (a b) d -> p a b d", b=cut) if cut else x) for x in (src,)), bcast(fold(stat[0:p, 3, 0:n]), D), ALU.mult))


def stage_taps(nc, t, krev_d):
    NC2 = 2 * KC
    H1 = D + 1
    with ExitStack() as ctx:
        sb = lambda n, s, d=F32: ctx.enter_context(nc.sbuf_tensor(n, s, d))
        ps = lambda n, s: ctx.enter_context(nc.psum_tensor(n, s, F32))
        sem = lambda n: ctx.enter_context(nc.semaphore(n))
        ident = sb("t_ident", [P, P])
        cq = sb("cq", [H1, 2, D])
        cqs = sb("cqs", [H1, 2, D])
        ct = sb("ct", [P, 2, H1])
        cols = sb("cols", [P, 6])
        sc = sb("sc", [P, 16])
        kon = sb("kon", [P, 4])
        tanr = sb("tanr", [P, NC2, P])
        tanc = sb("tanc", [P, NC2])
        cosb = sb("cosb", [P, KC, L])
        sinb = sb("sinb", [P, KC, L])
        stepv = sb("stepv", [P, 1])
        dval = sb("dval", [D, 1])
        w = sb("w", [P, NC2, P])
        den = sb("den", [P, NC2, P])
        inv = sb("inv", [P, NC2, P])
        coef = sb("coef", [P, 4, H1])
        tmp = sb("tmp", [P, H1])
        k4 = sb("k4", [P, NC2, 4, H1])
        sm = sb("sm", [P, 8, NC2])
        t1 = sb("t1", [P, NC2, D])
        t2 = sb("t2", [P, NC2, D])
        dr = sb("dr", [P, NC2, D])
        di = sb("di", [P, NC2, D])
        ar = sb("ar", [P, NC2, D])
        ai = sb("ai", [P, NC2, D])
        ev = sb("ev", [P, KC, D])
        od = sb("od", [P, KC, D])
        kr = sb("kr", [D, KREV])
        psc = ps("psc_t", [P, 512])
        psk = ps("psk", [P, 4, 512])
        pso = ps("pso", [P, FT, 512])
        s_c, s_s, s_t, s_tab = sem("c_loaded"), sem("scalars_loaded"), sem("tan_loaded"), sem("tables_loaded")
        turned, dve, inv_ok = sem("c_turned"), sem("tap_steps"), sem("inv_ready")
        kdone, kout, ev_ok, taps, stored = sem("k_done"), sem("k_copied"), sem("spectrum_ready"), sem("taps_done"), sem("taps_stored")
        kr_ok = sem("taps_ready")

        with nc.Block() as block:
            @block.sync
            def _(sp):
                for i, (n, q) in enumerate((("L0_attn_C", "L0_attn_Q"), )):
                    for u, part in enumerate(("_re", "_im")):
                        for dst, w_ in ((cq, u), (cqs, 1 - u)):
                            sp.dma_start(dst[0:D, w_, :], t[n + part]).then_inc(s_c, 16)
                            sp.dma_start(dst[D:H1, w_, :], rows(t[q + part], 1)).then_inc(s_c, 16)
                sp.dma_start(ident[:], t["c_ident"]).then_inc(s_c, 16)
                for i, n in enumerate(("B_re", "B_im", "P_re", "P_im", "Lambda_re", "Lambda_im")):
                    for u in range(2):
                        sp.dma_start(cols[u * D:(u + 1) * D, i:i + 1], t["L0_attn_" + n].rearrange("(n o) -> n o", o=1), allow_slow_non_contiguous=True).then_inc(s_s, 16)
                sp.dma_start(kon[:], t["c_halves"]).then_inc(s_s, 16)
                sp.dma_start(stepv[:], rows(t["L0_attn_step"], P)).then_inc(s_s, 16)
                sp.dma_start(dval[:], rows(t["L0_attn_D"], D)).then_inc(s_s, 16)
                sp.dma_start(tanc[:], t["c_tancol"]).then_inc(s_s, 16)
                sp.dma_start(tanr[:].rearrange("p c k -> p (c k)"), rows(t["c_tanrow"], P)).then_inc(s_t, 16)
                for dst, n in ((cosb, "c_cos"), (sinb, "c_sin")):
                    sp.dma_start(dst[:, 0:KC - 1], t[n][0:(KC - 1) * P].rearrange("(c p) l -> p c l", p=P)).then_inc(s_tab, 16)
                    sp.dma_start(dst[0:KH - (KC - 1) * P, KC - 1], t[n][(KC - 1) * P:KH]).then_inc(s_tab, 16)
                sp.wait_ge(kr_ok, 1)
                sp.dma_start(krev_d, kr[:]).then_inc(stored, 16)
                sp.wait_ge(stored, 16)

            @block.tensor
            def _(pe):
                pe.wait_ge(s_c, 16 * 9)
                pe.transpose(psc[:, 0:H1], cq[:], ident[0:H1, 0:H1])
                pe.transpose(psc[:, P:P + H1], cqs[:], ident[0:H1, 0:H1]).then_inc(turned, 1)
                pe.wait_ge(inv_ok, 1)
                for c in range(NC2):
                    if c >= 4:
                        pe.wait_ge(kout, c - 3)
                    pe.matmul(psk[:, c % 4, 0:4 * H1], inv[:, c, :], coef[:], start=True, stop=True).then_inc(kdone, 1)
                pe.wait_ge(ev_ok, 1)
                pe.wait_ge(s_tab, 64)
                for f in range(FT):
                    for c in range(KC):
                        kc = min(P, KH - c * P)
                        for src, tab in ((ev, cosb), (od, sinb)):
                            mm = pe.matmul(pso[0:D, f, 0:FW], src[0:kc, c, :], tab[0:kc, c, f * FW:(f + 1) * FW], start=(c == 0 and src is ev), stop=(c == KC - 1 and src is od))
                    mm.then_inc(taps, 1)

            @block.scalar
            def _(act):
                for c in range(NC2):
                    act.wait_ge(kdone, c + 1)
                    nc.scalar.copy(k4[:, c].rearrange("p q h -> p (q h)"), psk[:, c % 4, 0:4 * H1]).then_inc(kout, 1)

            @block.vector
            def _(v):
                ch = Chain(v, dve)
                one, st = ch.step, nc.vector.scalar_tensor_tensor
                ts, tt = nc.vector.tensor_scalar, nc.vector.tensor_tensor
                v.wait_ge(s_s, 16 * 16)
                one(ts(sc[:, 0:1], stepv[:], 1e-6, None, ALU.max))
                one(nc.vector.reciprocal(sc[:, 1:2], sc[:, 0:1]))
                one(ts(sc[:, 2:3], sc[:, 1:2], 2.0, None, ALU.mult))
                one(tt(sc[:, 3:4], cols[:, 4:5], cols[:, 4:5], ALU.mult))
                one(tt(sc[:, 4:5], cols[:, 4:5], kon[:, 2:3], ALU.mult))
                for q in range(2):
                    one(ts(sc[:, 5 + 4 * q:6 + 4 * q], cols[:, 2 * q:2 * q + 1], kon[:, 0:1], None, ALU.mult))
                    one(ts(sc[:, 6 + 4 * q:7 + 4 * q], cols[:, 2 * q + 1:2 * q + 2], -1.0, None, ALU.mult))
                    one(ts(sc[:, 7 + 4 * q:8 + 4 * q], cols[:, 2 * q + 1:2 * q + 2], kon[:, 0:1], None, ALU.mult))
                v.wait_ge(turned, 1)
                one(nc.vector.tensor_copy(ct[:, 0, :], psc[:, 0:H1]))
                one(nc.vector.tensor_copy(ct[:, 1, :], psc[:, P:P + H1]))
                for q in range(2):
                    one(ts(tmp[:], ct[:, 1], sc[:, 6 + 4 * q:7 + 4 * q], None, ALU.mult))
                    one(st(coef[:, 2 * q], ct[:, 0], sc[:, 5 + 4 * q:6 + 4 * q], tmp[:], ALU.mult, ALU.add))
                    one(ts(tmp[:], ct[:, 1], cols[:, 2 * q:2 * q + 1], None, ALU.mult))
                    one(st(coef[:, 2 * q + 1], ct[:, 0], sc[:, 7 + 4 * q:8 + 4 * q], tmp[:], ALU.mult, ALU.add))
                v.wait_ge(s_t, 16)
                one(ts(w[:], tanr[:], sc[:, 2:3], cols[:, 5:6], ALU.mult, ALU.subtract))
                one(tt(den[:], w[:], w[:], ALU.mult))
                one(ts(den[:], den[:], sc[:, 3:4], None, ALU.add))
                one(nc.vector.reciprocal(den[:], den[:]))
                one(ts(w[:], w[:], kon[:, 1:2], sc[:, 4:5], ALU.mult, ALU.add))
                tt(inv[:], w[:], den[:], ALU.mult).then_inc(inv_ok, 1)
                v.wait_ge(kout, NC2)
                q10r, q10i, q11r, q11i = (k4[:, :, q, D] for q in range(4))
                S = lambda i: sm[:, i, :]
                one(ts(S(0), q11r, 1.0, None, ALU.add))
                one(tt(S(1), S(0), S(0), ALU.mult))
                one(tt(S(2), q11i, q11i, ALU.mult))
                one(tt(S(1), S(1), S(2), ALU.add))
                one(nc.vector.reciprocal(S(1), S(1)))
                one(tt(S(2), q10r, S(0), ALU.mult))
                one(tt(S(3), q10i, q11i, ALU.mult))
                one(tt(S(2), S(2), S(3), ALU.add))
                one(tt(S(4), S(2), S(1), ALU.mult))
                one(tt(S(2), q10i, S(0), ALU.mult))
                one(tt(S(3), q10r, q11i, ALU.mult))
                one(tt(S(2), S(2), S(3), ALU.subtract))
                one(tt(S(5), S(2), S(1), ALU.mult))
                wr, wi = bcast(S(4), D), bcast(S(5), D)
                k00r, k00i, k01r, k01i = (k4[:, :, q, 0:D] for q in range(4))
                one(tt(t1[:], k01r, wr, ALU.mult))
                one(tt(t2[:], k01i, wi, ALU.mult))
                one(tt(t1[:], t1[:], t2[:], ALU.subtract))
                one(tt(dr[:], k00r, t1[:], ALU.subtract))
                one(tt(t1[:], k01r, wi, ALU.mult))
                one(tt(t2[:], k01i, wr, ALU.mult))
                one(tt(t1[:], t1[:], t2[:], ALU.add))
                one(tt(di[:], k00i, t1[:], ALU.subtract))
                tb = bcast(tanc[:], D)
                one(tt(t1[:], di[:], tb, ALU.mult))
                one(tt(ar[:], dr[:], t1[:], ALU.subtract))
                one(tt(t1[:], dr[:], tb, ALU.mult))
                one(tt(ai[:], di[:], t1[:], ALU.add))
                one(tt(ev[:], ar[:, 0:KC], ar[:, KC:], ALU.add))
                tt(od[:], ai[:, 0:KC], ai[:, KC:], ALU.subtract).then_inc(ev_ok, 1)
                one(nc.vector.memset(kr[:], 0.0))
                for f in range(FT):
                    v.wait_ge(taps, f + 1)
                    o = LP - L + f * FW
                    one(nc.vector.tensor_copy(kr[:, o:o + FW], pso[0:D, f, 0:FW]))
                tt(kr[:, LP - 1:LP], kr[:, LP - 1:LP], dval[:], ALU.add).then_inc(kr_ok, 1)


def stage_ssm(nc, t, h1d, krev_d, h2d):
    NG = NA * B
    with ExitStack() as outer:
        sbo = lambda n, s, d=F32: outer.enter_context(nc.sbuf_tensor(n, s, d))
        yc = sbo("yc", [NT * 32, P, D])
        with ExitStack() as ctx:
            sb = lambda n, s, d=F32: ctx.enter_context(nc.sbuf_tensor(n, s, d))
            ps = lambda n, s: ctx.enter_context(nc.psum_tensor(n, s, F32))
            sem = lambda n: ctx.enter_context(nc.semaphore(n))
            hh = sb("hh", [P, NG, D])
            sq = sb("sq", [P, NG, D])
            stat = sb("stat", [P, 4, NG])
            mh = sb("mh", [P, NG])
            ut = sb("ut", [P, D, AP_, B])
            ub = sb("ub", [P, 2, HC, AP_ * B])
            tz = sb("tz", [P, 2 * HC, LP])
            psc = ps("psc", [P, 2, HC, P])
            s_h, dve, pv, pr, u_ok = sem("h_loaded"), sem("u_steps"), sem("u_var"), sem("u_rstd"), sem("u_ready")
            s_tz = [sem(f"taps{k}_loaded") for k in range(2 * HC)]
            ub_ok = [sem("u0_copied"), sem("u1_copied")]
            cdone = [sem(f"conv{k}_done") for k in range(2 * HC)]
            cout = [sem("conv0_copied"), sem("conv1_copied")]
            mh_ok, zero_ok = sem("mh_ready"), sem("zero_ready")
            with nc.Block() as block:
                @block.sync
                def _(sp):
                    for b in range(B):
                        sp.dma_start(hh[:].rearrange("p (a b) d -> p b a d", b=B)[:, b], h1d[b].rearrange("(a p) d -> p a d", p=P)).then_inc(s_h, 16)
                    for k in range(2 * HC):
                        sp.sem_inc(cdone[k], 1)
                    for k in range(2):
                        sp.sem_inc(cout[k], 1)
                    with sp.Fori(0, D // (2 * HC)) as it:
                        for k in range(2 * HC):
                            sp.wait_ge(cdone[k], it + 1)
                            c0 = it * (2 * HC) + k
                            sp.dma_start(tz[:, k, :], bass.AP(krev_d.tensor, krev_d.offset + c0 * KREV, [[1, P], [1, LP]])).then_inc(s_tz[k], 16)

                @block.tensor
                def _(pe):
                    with pe.Fori(0, D // (2 * HC)) as it:
                        for k in range(2 * HC):
                            g, c = divmod(k, HC)
                            if c == 0:
                                pe.wait_ge(ub_ok[g], it + 1)
                                pe.wait_ge(cout[g], it + 1)
                            pe.wait_ge(s_tz[k], it * 16 + 16)
                            for dl in range(NA):
                                for i in range(dl // 3, NT):
                                    o = (3 * i + 2 - dl) * B
                                    mm = pe.matmul(psc[32 * i:32 * i + 32, g, c, :], ub[:, g, c, o:o + 32], tz[:, k, LP - P - P * dl:LP - P * dl],
                                                   start=(dl == 0), stop=(dl == 3 * i + 2), skip_group_check=True)
                            mm.then_inc(cdone[k], 1)

                @block.scalar
                def _(act):
                    with act.Fori(0, D // (2 * HC)) as it:
                        for g in range(2):
                            act.wait_ge(cdone[g * HC + HC - 1], it + 2)
                            c0 = it * (2 * HC) + g * HC
                            nc.scalar.copy(yc[:, :, bass.ds(c0, HC)].rearrange("r p c -> r c p"), psc[0:NT * 32, g]).then_inc(cout[g], 1)

                @block.gpsimd
                def _(pool):
                    pool.memset(mh[:], -0.5).then_inc(mh_ok, 1)
                    pool.wait_ge(mh_ok, 1)
                    pool.wait_ge(pv, 1)
                    pool.tensor_tensor(stat[:, 3], stat[:, 2], mh[:], ALU.pow).then_inc(pr, 1)

                @block.vector
                def _(v):
                    ch = Chain(v, dve)
                    ch.done(nc.vector.memset(ut[:, :, 0:2, :], 0.0))
                    ch.step(nc.vector.memset(ut[:, :, AP_ - 1:AP_, :], 0.0))
                    v.wait_ge(s_h, 16 * B)
                    norm_rows(nc, v, ch, pv, pr, 1, ut[:, :, 2:2 + NA, :].rearrange("p d a b -> p a b d"),
                              hh[:], sq[:], stat, NG, cut=B)
                    ch.wait()
                    with v.Fori(0, D // (2 * HC)) as it:
                        for g in range(2):
                            v.wait_ge(cdone[g * HC + HC - 1], it + 1)
                            c0 = it * (2 * HC) + g * HC
                            nc.vector.tensor_copy(ub[:, g].rearrange("p c a -> p (c a)"), ut[:, bass.ds(c0, HC)].rearrange("p c a b -> p (c a b)")).then_inc(ub_ok[g], 1)

        with ExitStack() as ctx:
            sb = lambda n, s, d=F32: ctx.enter_context(nc.sbuf_tensor(n, s, d))
            ps = lambda n, s: ctx.enter_context(nc.psum_tensor(n, s, F32))
            sem = lambda n: ctx.enter_context(nc.semaphore(n))
            ident = sb("f_ident", [P, P])
            wfc = sb("wfc", [D, 2, D])
            wb = sb("wb", [P, 2, D])
            bfc = sb("bfc", [P, D])
            lng = sb("lng", [P, D])
            lnb = sb("lnb", [P, D])
            y1 = sb("y1", [P, NT * 32, P // 2])
            hl = sb("hl", [P, NG, D])
            uc = sb("uc", [P, NG, D])
            ul = sb("ul", [P, NG, D])
            z = sb("z", [P, NG, D])
            stat = sb("fstat", [P, 4, NG])
            mh = sb("fmh", [P, NG])
            pst = ps("f_pst", [P, 2, 4, P])
            psf = ps("psf", [P, 3, 512])
            psw = ps("f_psw", [P, 512])
            s_w, s_h, dve, pv, pr = sem("fc_loaded"), sem("hl_loaded"), sem("fc_steps"), sem("fc_var"), sem("fc_rstd")
            wt, wb_ok, turned, y1_ok, fdone, zadd, zg, h_ok, h_out, mh_ok = (sem(x) for x in (
                "w_turned", "w_ready", "y_turned", "y1_ready", "fc_done", "fc_bias", "fc_gelu", "h2_ready", "h2_stored", "fmh_ready"))
            view = lambda x, b: x[b].rearrange("(a p s) d -> p a (s d)", p=P // 2, s=2)
            grp = lambda x, b: x[64 * (b % 2):64 * (b % 2) + 64].rearrange("p (a q s) d -> p q a (s d)", q=B // 2, s=2)[:, b // 2]
            with nc.Block() as block:
                @block.sync
                def _(sp):
                    sp.dma_start(ident[:], t["c_ident"]).then_inc(s_w, 16)
                    for u in range(2):
                        sp.dma_start(wfc[:, u, :], t["L0_attn_W_fc"]).then_inc(s_w, 16)
                    sp.dma_start(bfc[:], rows(t["L0_attn_b_fc"], P)).then_inc(s_w, 16)
                    sp.dma_start(lng[:], rows(t["L0_attn_ln_g"], P)).then_inc(s_w, 16)
                    sp.dma_start(lnb[:], rows(t["L0_attn_ln_b"], P)).then_inc(s_w, 16)
                    for b in range(B):
                        sp.dma_start(grp(hl, b), view(h1d, b)).then_inc(s_h, 16)
                    sp.wait_ge(h_ok, 1)
                    for b in range(B):
                        sp.dma_start(view(h2d, b), grp(z, b)).then_inc(h_out, 16)
                    sp.wait_ge(h_out, 16 * B)

                @block.tensor
                def _(pe):
                    pe.wait_ge(s_w, 96)
                    pe.transpose(psw[:, 0:D], wfc[:], ident[0:D, 0:D]).then_inc(wt, 1)
                    for g in range(16):
                        if g >= 2:
                            pe.wait_ge(y1_ok, g - 1)
                        for s in range(4):
                            pr_ = P // 2 - 1 - (4 * g + s)
                            mm = pe.transpose(pst[:, g % 2, s, 0:NT * 32], yc[:, 2 * pr_:2 * pr_ + 2, :], ident[0:NT * 32, 0:NT * 32])
                        mm.then_inc(turned, 1)
                    pe.wait_ge(wb_ok, 1)
                    pe.wait_ge(y1_ok, 16)
                    for a in range(NA):
                        if a >= 3:
                            pe.wait_ge(zadd, a - 2)
                        for q in range(B // 2):
                            r0 = 32 * (a // 3) + B * (a % 3) + 2 * q
                            mm = pe.matmul(psf[:, a % 3, q * P:(q + 1) * P], y1[:, r0:r0 + 2, :], wb[:], start=True, stop=True)
                        mm.then_inc(fdone, 1)

                @block.scalar
                def _(act):
                    for g in range(16):
                        act.wait_ge(turned, g + 1)
                        nc.scalar.activation(y1[:, :, 4 * g:4 * g + 4].rearrange("p r s -> p s r"), pst[:, g % 2, :, 0:NT * 32], ACT.Gelu).then_inc(y1_ok, 1)
                    for a in range(NA):
                        act.wait_ge(zadd, a + 1)
                        zz = z[:, 8 * a:8 * a + 8, :]
                        nc.scalar.activation(zz, zz, ACT.Gelu).then_inc(zg, 1)

                @block.gpsimd
                def _(pool):
                    pool.memset(mh[:], -0.5).then_inc(mh_ok, 1)
                    pool.wait_ge(mh_ok, 1)
                    for i in range(2):
                        pool.wait_ge(pv, i + 1)
                        pool.tensor_tensor(stat[:, 3], stat[:, 2], mh[:], ALU.pow).then_inc(pr, 1)

                @block.vector
                def _(v):
                    ch = Chain(v, dve)
                    ch.step(nc.vector.memset(wb[:], 0.0))
                    v.wait_ge(wt, 1)
                    ch.done(nc.vector.tensor_copy(wb[0:D, 1, :], psw[0:D, 0:D]))
                    nc.vector.tensor_copy(wb[D:P, 0, :], psw[D:P, 0:D]).then_inc(wb_ok, 1)
                    v.wait_ge(s_h, 16 * B)
                    ch.step(nc.vector.tensor_copy(uc[:], hl[:]))
                    norm_rows(nc, v, ch, pv, pr, 1, ul[:], uc[:], z[:], stat, NG)
                    ch.wait()
                    for a in range(NA):
                        v.wait_ge(fdone, a + 1)
                        nc.vector.tensor_tensor(z[:, 8 * a:8 * a + 8, :], psf[:, a % 3, :].rearrange("p (g d) -> p g d", d=D), bmid(bfc[:], 8), ALU.add).then_inc(zadd, 1)
                    v.wait_ge(zg, NA)
                    ch.step(nc.vector.tensor_tensor(z[:], z[:], ul[:], ALU.add))
                    norm_rows(nc, v, ch, pv, pr, 2, uc[:], z[:], ul[:], stat, NG)
                    ch.wait()
                    ch.step(nc.vector.tensor_tensor(uc[:], uc[:], bmid(lng[:], NG), ALU.mult))
                    ch.step(nc.vector.tensor_tensor(uc[:], uc[:], bmid(lnb[:], NG), ALU.add))
                    nc.vector.tensor_tensor(z[:], hl[:], uc[:], ALU.add).then_inc(h_ok, 1)


NH, NE, HD = 4, 4, 16
HE = NH * NE
FEPS = 1e-8
TERMS_Q = (0, 1, 0, 2, 0, 1)
TERMS_K = (0, 0, 1, 0, 2, 1)
KT = HD * len(TERMS_Q)
KM = KT + 3
VW = 32
QT = 512
UB = 3
LAST = L - (NA - 1) * P
FB = 384


def score_units(per_unit, whole_tiles=False):
    banks, units = [], []
    for tile in range(2):
        if whole_tiles:
            units, banks = units + [banks[i:i + per_unit] for i in range(0, len(banks), per_unit)], []
        for j in range(4 * tile):
            banks += [[(0, j, e, QT * tile, QT)] for e in range(NE)]
        d = lambda i, e, c: (c, 4 * tile + i, e, QT * tile + P * i, QT - P * i)
        banks += [[d(0, e, 0)] for e in range(NE)]
        banks += [[d(1, e, 0), d(3, e, 384)] for e in range(NE)]
        banks += [[d(2, e, 0), d(2, e + 1, 256)] for e in (0, 2)]
    if whole_tiles:
        units, banks = units + [banks[i:i + per_unit] for i in range(0, len(banks), per_unit)], []
    for j in range(NA):
        banks.append([(0, j, None, 2 * QT, LAST)])
    return units + [banks[i:i + per_unit] for i in range(0, len(banks), per_unit)]


def norm_groups(nc, v, ch, pool_var, pool_r, which, out, src, tmp, stat, n, d, eps):
    ch.step(nc.vector.tensor_reduce(stat[:, 0, 0:n], src, AX.X, ALU.add))
    ch.step(nc.vector.tensor_scalar(stat[:, 1, 0:n], stat[:, 0, 0:n], -1.0 / d, None, ALU.mult))
    ch.step(nc.vector.tensor_tensor(src, src, bcast(stat[:, 1, 0:n], d), ALU.add))
    ch.step(nc.vector.tensor_tensor(tmp, src, src, ALU.mult))
    ch.step(nc.vector.tensor_reduce(stat[:, 0, 0:n], tmp, AX.X, ALU.add))
    nc.vector.tensor_scalar(stat[:, 2, 0:n], stat[:, 0, 0:n], 1.0 / d, eps, ALU.mult, ALU.add).then_inc(pool_var, 1)
    v.wait_ge(pool_r, which)
    ch.step(nc.vector.tensor_tensor(out, src, bcast(stat[:, 3, 0:n], d), ALU.mult))


def stage_ffn_exact(nc, t, h2d, out, flag_d):
    units = score_units(UB)
    NU = len(units)
    NDVE = 141
    qk_d = nc.dram_tensor("qk_parts", (3, 2 * P + D, LP), BF16).ap()
    xsrc = lambda b: h2d[b].rearrange("(a p) d -> p a d", p=P)
    with ExitStack() as ctx:
        sb = lambda n, s, d=F32: ctx.enter_context(nc.sbuf_tensor(n, s, d))
        ps = lambda n, s, d=F32: ctx.enter_context(nc.psum_tensor(n, s, d))
        sem = lambda n: ctx.enter_context(nc.semaphore(n))
        ident = sb("a_ident", [P, P])
        identb = sb("a_identb", [P, P], BF16)
        maskb = sb("maskb", [P, P], BF16)
        maskf = sb("maskf", [P, P])
        wha = sb("wha", [NH * HD, D + 1])
        wbd = sb("wbd", [NH * HD, 448])
        wall = sb("wall", [D + 1, 448])
        fcw = sb("fcw", [D + 1, 2, D])
        gw = sb("gw", [P, HE * 64])
        gb = sb("gb", [P, HE])
        fgw = sb("fgw", [P, NH, D])
        vec = sb("vec", [P, 4, HD])
        resid = sb("resid", [P, NA, D])
        h4 = sb("h4", [P, 4 * NA, D])
        hb = sb("hb", [P, NA, D])
        xn = sb("xn", [P, NA, D])
        tmp = sb("a_tmp", [P, 4 * NA, D])
        stat = sb("a_stat", [P, 4, 4 * NA])
        mh = sb("a_mh", [P, 4 * NA])
        xt = sb("xt", [D + 1, LP])
        qs = sb("qs", [P, 3, 2, LP], BF16)
        ks = sb("ks", [D, 3, LP], BF16)
        rq = sb("rq", [P, 3, FB])
        qop = sb("qop", [KM, NH, NE, LP], BF16)
        kop = sb("kop", [KM, NH, LP], BF16)
        vop = sb("vop", [P, NA, NH, VW])
        msk = sb("msk", [P, NA, D])
        mpart = sb("mpart", [P, NE, NA])
        mtok = sb("mtok", [P, NA, HE])
        mtp = sb("mtp", [P, NA, 3, HE], BF16)
        mres = sb("mres", [P, NA, HE])
        mt = sb("mt", [3 * HE, LP], BF16)
        pb = sb("pb", [P, 3, UB, QT])
        ofm = sb("ofm", [P, 2, QT])
        ot = sb("ot", [P, NA * NH, NE, VW])
        on = sb("on", [P, NA * NH, NE * HD])
        rec = sb("rec", [P, NA * NH, NE])
        lg = sb("lg", [P, NA * NH, NE])
        mx = sb("mx", [P, NA * NH])
        gs = sb("gs", [P, NA * NH, NE])
        mix = sb("mix", [P, NA * NH, HD])
        fx = sb("fx", [P, NA * NH, HD])
        fxt = sb("fxt", [D + 1, LP])
        hx1 = sb("hx1", [D + 1, LP])
        pm = sb("pm", [D, LP])
        fo = sb("fo", [P, NA * NH, HD])
        pss = ps("pss", [P, 2, UB, QT])
        pso = ps("a_pso", [P, QT])
        psm = ps("psm", [P, QT])
        psmb = psm[:].bitcast(BF16)

        res = sb("res", [P, NA, D])
        names = ("weights_loaded", "wbd_zeroed", "resid_loaded", "h_loaded", "bank_full", "bank_free", "vector_steps",
                 "variance", "rstd", "rest_ready", "rest_free", "parts_ready", "part1", "placed", "parts_used", "max_split", "max_placed",
                 "scored", "exped", "masked", "summed", "sums_copied", "logits", "logits_exped", "gate_exped", "result", "stored", "spilled", "passed", "tile_done", "pool_passed",
                 "mh_ready", "xn_ready", "fx_ready", "hx_ready", "swept", "swept_max", "ident_ready", "const_ready")
        (weights, wbd_zero, r_load, h_load, full, free, dve, var, rstd, rest, rest_free, parts, part1, placed, used, max_split, max_placed,
         scored, exped, masked, summed, acc_free, logit, logit_exp, gate_exp, result, stored, spilled, passed, tile_done, pool_passed,
         mh_ok, xn_ok, fx_ok, hx_ok, swept, swept_max, ident_ok, const_ok) = (sem("a_" + n) for n in names)
        chunks = [(0, 4), (4, 8), (8, 9)]

        PRO = [("turn", c) for c in chunks] + [("tok", c) for c in chunks] + [("feat", (g, k)) for g in range(3) for k in range(3)]
        MXJ = [("mrow", (0, 8)), ("mrow", (8, 9))]
        EPI = [("fturn", c) for c in chunks] + [("fc1", k) for k in range(3)] + [("fc2", k) for k in range(3)] + [("back", c) for c in chunks]
        OUTJ = [("oturn", (n, x)) for n in range(NH) for x in range(3)]
        J = len(PRO) + len(MXJ) + len(OUTJ) + len(EPI)
        JS = 1 + 4 * 6
        SWEEP = NH * NA * (NA + 1) // 2
        NUB = NH * NU
        dj = [[(c, b) for b, bank in enumerate(u) for (c, j, e, q0, w) in bank if (q0 == P * j if e is not None else j == NA - 1)] for u in units]
        NM = NH * sum(bool(d) for d in dj)
        assert NUB % 6 == 0 and SWEEP % 6 == 0
        order_m = {}
        for u, d in enumerate(dj):
            order_m[u] = sum(bool(x) for x in dj[:u + 1])
        tile_of = lambda q0: q0 // QT
        last_unit = {x: max(u for u, un in enumerate(units) for bank in un for p in bank if tile_of(p[3]) == x) for x in range(3)}
        last_bank = max(b for b, bank in enumerate(units[last_unit[0]]) if tile_of(bank[0][3]) == 0)
        assert last_bank < UB - 1 and all(tile_of(units[last_unit[x]][-1][0][3]) == x for x in (1, 2))

        with nc.Block() as block:
            @block.sync
            def _(sp):
                with sp.If(sp.value_load(flag_d, min_val=0, max_val=1) > 0):
                    for s_, c in ((exped, 2), (summed, 3), (free, 1), (acc_free, 1), (parts, 3), (stored, 16), (swept_max, 6), (used, 1)):
                        sp.sem_inc(s_, c)
                    sp.dma_start(ident[:], t["c_ident"]).then_inc(ident_ok, 16)
                    sp.dma_start(wha[:, 0:D], t["L0_ffn_hl_w"].rearrange("n d h -> (n d) h")).then_inc(weights, 16)
                    sp.dma_start(wha[:, D:D + 1], t["L0_ffn_hl_b"].rearrange("n (d o) -> (n d) o", o=1), allow_slow_non_contiguous=True).then_inc(weights, 16)
                    sp.dma_start(gw[:], rows(t["L0_ffn_gate_w"].rearrange("n e f -> (n e f)"), P)).then_inc(weights, 16)
                    sp.dma_start(gb[:], rows(t["L0_ffn_gate_b"].rearrange("n e -> (n e)"), P)).then_inc(weights, 16)
                    sp.dma_start(fgw[:].rearrange("p n d -> p (n d)"), rows(t["L0_ffn_fgate_w"].rearrange("n d -> (n d)"), P)).then_inc(weights, 16)
                    for i, n in enumerate(("ln_g", "ln_b", "fnorm_g", "fnorm_b")):
                        sp.dma_start(vec[:, i, :], rows(t["L0_ffn_" + n], P)).then_inc(weights, 16)
                    for n in range(4):
                        sp.dma_start(h4[:, NA * n:NA * (n + 1), :], xsrc(n)).then_inc(r_load, 16)
                    sp.wait_ge(wbd_zero, 2)
                    sp.dma_start(wbd[:, 384:448], t["c_ident"][0:D, 0:D]).then_inc(weights, 16)
                    for n in range(NH):
                        r = slice(HD * n, HD * n + HD)
                        o = HD * n
                        sp.dma_start(wbd[r, D * n:D * n + D], t["L0_ffn_wq"][n].rearrange("e o d -> d (e o)"), allow_slow_non_contiguous=True).then_inc(weights, 16)
                        sp.dma_start(wbd[r, 256 + o:272 + o], t["L0_ffn_wk"][n].rearrange("o d -> d o"), allow_slow_non_contiguous=True).then_inc(weights, 16)
                        sp.dma_start(wbd[r, 320 + o:336 + o], t["L0_ffn_wv"][n].rearrange("o d -> d o"), allow_slow_non_contiguous=True).then_inc(weights, 16)
                        for i in range(2):
                            w_, b_ = t[f"L0_ffn_fc{i + 1}_w"], t[f"L0_ffn_fc{i + 1}_b"]
                            sp.dma_start(fcw[r, i, o:o + HD], w_.rearrange("o d -> d o"), allow_slow_non_contiguous=True).then_inc(weights, 16)
                            sp.dma_start(fcw[D:D + 1, i, o:o + HD], rows(b_, 1)).then_inc(weights, 16)
                    with sp.Fori(0, B) as it:
                        src = xsrc(it)
                        sp.wait_ge(stored, it * 32 + 16)
                        sp.dma_start(hb[:], src).then_inc(h_load, 16)
                        for g in range(2):
                            sp.wait_ge(parts, it * 9 + 3 * g + 6)
                            sp.dma_start(qk_d[:, P * g:P * g + P, :].rearrange("t r q -> r t q"), qs[:, :, g, :]).then_inc(spilled, 16)
                        sp.wait_ge(parts, it * 9 + 12)
                        sp.dma_start(qk_d[:, 2 * P:2 * P + D, :].rearrange("t r q -> r t q"), ks[:]).then_inc(spilled, 16)
                        sp.wait_ge(spilled, it * 48 + 48)
                        for i, (qp, kp) in enumerate(zip(TERMS_Q, TERMS_K)):
                            r = slice(HD * i, HD * i + HD)
                            sp.dma_start(qop[r].rearrange("o n e q -> o (n e) q"), qk_d[qp, 0:2 * P].rearrange("(m o) q -> o m q", o=HD)).then_inc(placed, 16)
                            sp.dma_start(kop[r], qk_d[kp, 2 * P:2 * P + D].rearrange("(n o) q -> o n q", o=HD)).then_inc(placed, 16)
                        sp.wait_ge(max_split, it + 1)
                        for i in range(3):
                            sp.dma_start(qop[KT + i:KT + i + 1].rearrange("k n e q -> k (n e) q"), mt[HE * i:HE * i + HE, :]).then_inc(max_placed, 16)
                        ores = out[it]
                        sp.wait_ge(result, it + 1)
                        sp.dma_start(ores[0:(NA - 1) * P].rearrange("(a p) d -> p a d", p=P), res[:, 0:NA - 1]).then_inc(stored, 16)
                        sp.dma_start(ores[(NA - 1) * P:L], res[0:LAST, NA - 1]).then_inc(stored, 16)
                    sp.wait_ge(stored, 32 * B + 16)

            @block.tensor
            def _(pe):
                with pe.If(pe.value_load(flag_d, min_val=0, max_val=1) > 0):
                    k = [0]

                    def job(base, ins):
                        ins().then_inc(full, 1)
                        k[0] += 1

                    def gate(base):
                        pe.wait_ge(free, base + k[0] + 1)

                    def turn_rows(src, c, base, rows_=D):
                        gate(base)
                        pe.sem_inc(passed, 1)
                        for a in range(*c):
                            mm = pe.transpose(psm[0:D, (a - c[0]) * P:(a - c[0] + 1) * P], src[:, a, :], ident[:])
                        job(base, lambda: mm)

                    pe.wait_ge(weights, 16 * 38)
                    pe.wait_ge(ident_ok, 16)
                    gate(0)
                    job(0, lambda: pe.matmul(psm[0:D + 1, 0:448], wha[:], wbd[:], start=True, stop=True))
                    pe.wait_ge(xn_ok, 1)
                    for n in range(4):
                        for c in chunks:
                            turn_rows(h4[:, NA * n:NA * (n + 1)], c, 0)
                        for c in chunks:
                            gate(0)
                            for a in range(*c):
                                mm = pe.matmul(psm[:, (a - c[0]) * HD:(a - c[0] + 1) * HD], xt[:, a * P:(a + 1) * P], wall[:, 384 + HD * n:400 + HD * n], start=True, stop=True)
                            job(0, lambda: mm)
                    assert k[0] == JS
                    pe.wait_ge(const_ok, 3)
                    with pe.Fori(0, B) as it:
                        k[0] = 0
                        base = it * J + JS
                        g0 = it * NUB
                        pe.wait_ge(xn_ok, it + 2)
                        for kind, c in PRO:
                            if kind == "turn":
                                turn_rows(xn, c, base)
                            elif kind == "tok":
                                gate(base)
                                for a in range(*c):
                                    mm = pe.matmul(psm[:, (a - c[0]) * P:(a - c[0] + 1) * P], xt[:, a * P:(a + 1) * P], wall[:, 320:448], start=True, stop=True)
                                job(base, lambda: mm)
                            else:
                                g, x = c
                                gate(base)
                                m = P if g < 2 else D
                                job(base, lambda: pe.matmul(psm[0:m, 0:FB], wall[:, g * P:g * P + m], xt[:, x * FB:(x + 1) * FB], start=True, stop=True))
                        pe.wait_ge(placed, it * 192 + 192)
                        sw = 0
                        for n in range(NH):
                            for i in range(NA):
                                for j in range(i + 1):
                                    pe.wait_ge(swept_max, it * SWEEP + sw + 1)
                                    bank = pss[:, sw // 3 % 2, sw % 3, :]
                                    for e in range(NE):
                                        mm = pe.matmul(bank[:, e * P:(e + 1) * P], qop[0:KT, n, e, i * P:(i + 1) * P], kop[0:KT, n, j * P:(j + 1) * P],
                                                       start=(e == 0 or i != j), stop=(i != j), skip_group_check=True)
                                    if i == j:
                                        mm = pe.matmul(bank, identb[:], bmid(maskb[:], NE), start=False, stop=True, skip_group_check=True)
                                    mm.then_inc(swept, 1)
                                    sw += 1
                        for kind, c in MXJ:
                            gate(base)
                            pe.wait_ge(used, it + 2)
                            pe.sem_inc(passed, 1)
                            for a in range(*c):
                                mm = pe.transpose(psmb[0:3 * HE, (a - c[0]) * P:(a - c[0] + 1) * P], mtp[:, a], identb[:])
                            job(base, lambda: mm)
                        pe.wait_ge(max_placed, it * 48 + 48)
                        pe.wait_ge(swept_max, it * SWEEP + SWEEP + 6)

                        def scores(u):
                            n, un = divmod(u, NU)
                            pe.wait_ge(exped, g0 + u + 1)
                            for b, bank in enumerate(units[un]):
                                for col, j, e, q0, w in bank:
                                    lhs = kop[:, n, j * P:(j + 1) * P]
                                    if e is None:
                                        mm = pe.matmul(pss[:, u % 2, b, 0:NE * w], lhs, qop[:, n, :, q0:q0 + w], start=True, stop=True, skip_group_check=True)
                                    else:
                                        mm = pe.matmul(pss[:, u % 2, b, col:col + w], lhs, qop[:, n, e, q0:q0 + w], start=True, stop=True, skip_group_check=True)
                            mm.then_inc(scored, 1)

                        def sums(u):
                            n, un = divmod(u, NU)
                            pe.wait_ge(exped, g0 + u + 3)
                            if dj[un]:
                                pe.wait_ge(masked, it * NM + (NM // NH) * n + order_m[un])
                            for b, bank in enumerate(units[un]):
                                for col, j, e, q0, w in bank:
                                    x = tile_of(q0)
                                    if j == 0 and e in (0, None):
                                        pe.wait_ge(acc_free, it * 3 * NH + 3 * n + x + 1)
                                    r = P if j < NA - 1 else LAST
                                    for ee in range(NE) if e is None else (e,):
                                        cc = col + (w * ee if e is None else 0)
                                        mm = pe.matmul(pso[VW * ee:VW * (ee + 1), q0 - QT * x:q0 - QT * x + w], vop[0:r, j, n, :], pb[0:r, u % 3, b, cc:cc + w],
                                                       start=(j == 0), stop=(q0 == P * j if e is not None else j == NA - 1), skip_group_check=True)
                                if un == last_unit[0] and b == last_bank:
                                    mm.then_inc(tile_done, 1)
                            mm.then_inc(summed, 1)

                        for u in range(NUB + 1):
                            if u < NUB:
                                scores(u)
                            if u >= 1:
                                sums(u - 1)
                                n = (u - 1) // NU
                                for x in (x for x in range(3) if last_unit[x] == (u - 1) % NU):
                                    c = (4 * x, min(4 * x + 4, NA))
                                    gate(base)
                                    pe.wait_ge(acc_free, it * 3 * NH + 3 * n + x + 2)
                                    for a in range(*c):
                                        wd = P if a < NA - 1 else LAST
                                        mm = pe.transpose(psm[0:wd, (a - c[0]) * P:(a - c[0] + 1) * P], ofm[:, (3 * n + x) % 2, (a - c[0]) * P:(a - c[0]) * P + wd], ident[:])
                                    job(base, lambda: mm)
                        pe.wait_ge(fx_ok, it + 1)
                        for kind, c in EPI:
                            if kind == "fturn":
                                turn_rows(fx[:].rearrange("p (a n) d -> p a (n d)", n=NH), c, base)
                            elif kind in ("fc1", "fc2"):
                                gate(base)
                                i = kind == "fc2"
                                job(base, lambda: pe.matmul(psm[0:D, 0:FB], fcw[:, int(i), :], (hx1 if i else fxt)[:, c * FB:(c + 1) * FB], start=True, stop=True))
                            else:
                                gate(base)
                                pe.sem_inc(passed, 1)
                                for a in range(*c):
                                    mm = pe.transpose(psm[:, (a - c[0]) * D:(a - c[0] + 1) * D], pm[:, a * P:(a + 1) * P], ident[0:D, 0:D])
                                job(base, lambda: mm)
                        assert k[0] == J

            @block.scalar
            def _(act):
                with act.If(act.value_load(flag_d, min_val=0, max_val=1) > 0):
                    with act.Fori(0, B) as it:
                        g0 = it * NUB
                        for u in range(NUB):
                            un = u % NU
                            act.wait_ge(scored, g0 + u + 1)
                            act.wait_ge(summed, g0 + u + 1)
                            w = QT if units[un][0][0][2] is not None else NE * LAST
                            nc.scalar.activation(pb[:, u % 3, :, 0:w], pss[:, u % 2, :, 0:w], ACT.Exp, scale=float(HD) ** 0.5).then_inc(exped, 1)
                        for i, (src, s_) in enumerate(((lg[:], logit_exp), (gs[:, 0:NA, :], gate_exp))):
                            act.wait_ge(logit, it * 2 + i + 1)
                            nc.scalar.activation(src, src, ACT.Exp).then_inc(s_, 1)

            @block.gpsimd
            def _(pool):
                with pool.If(pool.value_load(flag_d, min_val=0, max_val=1) > 0):
                    pool.memset(mh[:], -0.5).then_inc(mh_ok, 1)
                    pool.wait_ge(mh_ok, 1)
                    pool.memset(maskf[:], 0.0).then_inc(mh_ok, 1)
                    pool.wait_ge(mh_ok, 2)
                    pool.affine_select(out=maskf[:], in_=maskf[:], compare_op=ALU.is_ge, fill=-1e30, base=0, pattern=[[-1, P]], channel_multiplier=1).then_inc(mh_ok, 1)
                    pool.wait_ge(mh_ok, 3)
                    pool.wait_ge(var, 1)
                    pool.tensor_tensor(stat[:, 3], stat[:, 2], mh[:], ALU.pow).then_inc(rstd, 1)

                    def root(i, it, n):
                        pool.wait_ge(var, it * 3 + i + 2)
                        pool.tensor_tensor(stat[:, 3, 0:n], stat[:, 2, 0:n], mh[:, 0:n], ALU.pow).then_inc(rstd, 1)

                    with pool.Fori(0, B) as it:
                        root(0, it, NA)
                        for i in range(9):
                            g, x = divmod(i, 3)
                            m = P if g < 2 else D
                            dst = (lambda p_: qs[:, p_, g, x * FB:(x + 1) * FB]) if g < 2 else (lambda p_: ks[:, p_, x * FB:(x + 1) * FB])
                            pool.wait_ge(free, it * J + JS + 6 + i + 2)
                            pool.sem_inc(pool_passed, 1)
                            pool.tensor_copy(dst(1), rq[0:m, i % 3, :]).then_inc(part1, 1)
                            pool.wait_ge(part1, it * 9 + i + 1)
                            pool.tensor_tensor(dst(2), rq[0:m, i % 3, :], dst(1), ALU.subtract).then_inc(parts, 1)
                            pool.wait_ge(parts, it * 9 + i + 4)
                        for u in range(NUB):
                            un = u % NU
                            if not dj[un]:
                                continue
                            pool.wait_ge(exped, it * NUB + u + 3)
                            pool.sem_inc(pool_passed, 1)
                            cols = {}
                            for c, b in dj[un]:
                                cols.setdefault(c, []).append(b)
                            n_ = 0
                            for c, bs in sorted(cols.items()):
                                if units[un][bs[0]][0][2] is None:
                                    v_ = pb[0:LAST, u % 3, bs[0], 0:NE * LAST].rearrange("p (e q) -> p e q", e=NE)
                                    pat = [[0, NE], [1, LAST]]
                                else:
                                    v_ = pb[:, u % 3, bs[0]:bs[-1] + 1, c:c + P]
                                    pat = [[0, len(bs)], [1, P]]
                                ins = pool.affine_select(out=v_, in_=v_, compare_op=ALU.is_ge, fill=0.0, base=0, pattern=pat, channel_multiplier=-1)
                            ins.then_inc(masked, 1)
                        root(1, it, NA * NH)
                        root(2, it, NA * NH)

            @block.vector
            def _(v):
                with v.If(v.value_load(flag_d, min_val=0, max_val=1) > 0):
                    tt, ts, stt, cp = nc.vector.tensor_tensor, nc.vector.tensor_scalar, nc.vector.scalar_tensor_tensor, nc.vector.tensor_copy
                    red = nc.vector.tensor_reduce
                    k = [0]
                    nc.vector.memset(wbd[:], 0.0).then_inc(wbd_zero, 1)
                    nc.vector.memset(fcw[:], 0.0).then_inc(wbd_zero, 1)
                    ch = Chain(v, dve)
                    ch.step(nc.vector.memset(xt[D:D + 1], 1.0))
                    ch.step(nc.vector.memset(fxt[D:D + 1], 1.0))
                    ch.step(nc.vector.memset(hx1[D:D + 1], 1.0))
                    ch.step(nc.vector.memset(vop[:], 0.0))
                    ch.step(nc.vector.memset(vop[:, :, :, HD:HD + 1], 1.0))
                    ch.step(nc.vector.memset(ot[:], 1.0))
                    nc.vector.memset(kop[KT:KM], -1.0).then_inc(const_ok, 1)
                    v.wait_ge(ident_ok, 16)
                    cp(identb[:], ident[:]).then_inc(const_ok, 1)
                    v.wait_ge(mh_ok, 3)
                    cp(maskb[:], maskf[:]).then_inc(const_ok, 1)

                    def take(base):
                        v.wait_ge(full, base + k[0] + 1)

                    def give(ins):
                        ins.then_inc(free, 1)
                        k[0] += 1

                    take(0)
                    give(cp(wall[:], psm[0:D + 1, 0:448]))
                    v.wait_ge(r_load, 64)
                    norm_groups(nc, v, ch, var, rstd, 1, h4[:], h4[:], tmp[:], stat, 4 * NA, D, EPS)
                    ch.wait()
                    cp(stat[:, 0, 0:1], stat[:, 1, 0:1]).then_inc(xn_ok, 1)
                    for n in range(4):
                        for c in chunks:
                            take(0)
                            give(cp(xt[0:D, c[0] * P:c[1] * P], psm[0:D, 0:(c[1] - c[0]) * P]))
                        for c in chunks:
                            take(0)
                            give(cp(resid[:, c[0]:c[1], HD * n:HD * n + HD], psm[:, 0:(c[1] - c[0]) * HD].rearrange("p (a d) -> p a d", d=HD)))
                    assert k[0] == JS
                    n_setup = ch.n
                    v.wait_ge(free, JS + 1)
                    with v.Fori(0, B) as it:
                        k[0] = 0
                        base = it * J + JS
                        ch = Chain(v, dve, it * NDVE + n_setup)
                        v.wait_ge(h_load, it * 16 + 16)
                        ch.step(cp(tmp[:, NA:2 * NA, :], hb[:]))
                        norm_groups(nc, v, ch, var, rstd, it * 3 + 2, xn[:], tmp[:, NA:2 * NA, :], tmp[:, 0:NA, :], stat, NA, D, EPS)
                        cp(stat[:, 0, 0:1], stat[:, 1, 0:1]).then_inc(xn_ok, 1)
                        for kind, c in PRO:
                            take(base)
                            if kind == "turn":
                                give(cp(xt[0:D, c[0] * P:c[1] * P], psm[0:D, 0:(c[1] - c[0]) * P]))
                            elif kind == "tok":
                                pv = psm[:].rearrange("p (a s x) -> p a s x", s=2, x=D)[:, 0:c[1] - c[0]]
                                ch.done(cp(vop[:, c[0]:c[1], :, 0:HD], pv[:, :, 0, :].rearrange("p a (n d) -> p a n d", d=HD)))
                                give(ts(msk[:, c[0]:c[1], :], pv[:, :, 1, :], 0.0, None, ALU.not_equal))
                            else:
                                g, x = c
                                i = 3 * g + x
                                m = P if g < 2 else D
                                p0 = qs[:, 0, g, x * FB:(x + 1) * FB] if g < 2 else ks[:, 0, x * FB:(x + 1) * FB]
                                ch.step(cp(p0, psm[0:m, 0:FB]))
                                v.wait_ge(parts, it * 9 + i + 1)
                                give(tt(rq[0:m, i % 3, :], psm[0:m, 0:FB], p0, ALU.subtract))
                        sw = 0
                        for n in range(NH):
                            for i in range(NA):
                                for j in range(i + 1):
                                    v.wait_ge(swept, it * SWEEP + sw + 1)
                                    red(mpart[:, :, j:j + 1], pss[:, sw // 3 % 2, sw % 3, :].rearrange("p (e t) -> p e t", e=NE), AX.X, ALU.max).then_inc(swept_max, 1)
                                    sw += 1
                                v.wait_ge(swept_max, it * SWEEP + sw + 6)
                                ch.step(red(mtok[:, i, NE * n:NE * n + NE], mpart[:, :, 0:i + 1], AX.X, ALU.max))
                        ch.step(cp(mtp[:, :, 0, :], mtok[:]))
                        ch.step(tt(mres[:], mtok[:], mtp[:, :, 0, :], ALU.subtract))
                        ch.step(cp(mtp[:, :, 1, :], mres[:]))
                        tt(mtp[:, :, 2, :], mres[:], mtp[:, :, 1, :], ALU.subtract).then_inc(used, 1)
                        for kind, c in MXJ:
                            take(base)
                            if c[0] == 0:
                                give(cp(mt[:, 0:8 * P], psmb[0:3 * HE, 0:8 * P]))
                            else:
                                give(cp(mt[:, 8 * P:], psmb[0:3 * HE, 0:P]))
                                v.wait_ge(free, base + k[0] + 1)
                                cp(stat[0:1, 1, 0:1], stat[0:1, 0, 0:1]).then_inc(max_split, 1)
                        for n in range(NH):
                            for x in range(3):
                                w = QT if x < 2 else LAST
                                if x == 0:
                                    v.wait_ge(tile_done, it * NH + n + 1)
                                else:
                                    v.wait_ge(summed, it * NUB + n * NU + last_unit[x] + 4)
                                cp(ofm[:, (3 * n + x) % 2, 0:w], pso[:, 0:w]).then_inc(acc_free, 1)
                                take(base)
                                c = (4 * x, min(4 * x + 4, NA))
                                dst = ot[:].rearrange("p (a n) e w -> p a n (e w)", n=NH)
                                if x < 2:
                                    give(cp(dst[:, c[0]:c[1], n, :], psm[:].rearrange("p (a w) -> p a w", w=P)))
                                else:
                                    give(cp(dst[0:LAST, NA - 1, n, :], psm[0:LAST, 0:P]))
                        v.wait_ge(free, base + k[0] + 1)
                        G = NA * NH
                        ch.step(nc.vector.reciprocal(rec[:], ot[:, :, :, HD]))
                        onv = on[:].rearrange("p g (e d) -> p g e d", d=HD)
                        ch.step(tt(onv, ot[:, :, :, 0:HD], bcast(rec[:], HD), ALU.mult))
                        ch.step(tt(onv, onv, bmid(msk[:].rearrange("p a (n d) -> p (a n) d", d=HD), NE), ALU.mult))
                        on4 = on[:].rearrange("p (a n) f -> p a n f", n=NH)
                        tm4 = tmp[:].rearrange("p (a n) f -> p a n f", n=NH)
                        gwv = gw[:].rearrange("p (n e f) -> p e n f", n=NH, f=64)
                        for e in range(NE):
                            for a in range(NA):
                                ch.done(tt(tm4[:, a], on4[:, a], gwv[:, e], ALU.mult))
                            ch.wait()
                            ch.step(red(lg[:, :, e:e + 1], tmp[:], AX.X, ALU.add))
                        ch.step(tt(lg[:].rearrange("p (a n) e -> p a (n e)", n=NH), lg[:].rearrange("p (a n) e -> p a (n e)", n=NH), bmid(gb[:], NA), ALU.add))
                        ch.step(red(mx[:], lg[:], AX.X, ALU.max))
                        tt(lg[:], lg[:], bcast(mx[:], NE), ALU.subtract).then_inc(logit, 1)
                        v.wait_ge(logit_exp, it + 1)
                        ch.step(red(mx[:], lg[:], AX.X, ALU.add))
                        ch.step(nc.vector.reciprocal(mx[:], mx[:]))
                        ch.step(tt(lg[:], lg[:], bcast(mx[:], NE), ALU.mult))
                        ch.step(tt(tmp[:].rearrange("p g (e d) -> p g e d", d=HD), onv, bcast(lg[:], HD), ALU.mult))
                        ch.step(red(mix[:], tmp[:].rearrange("p g (e d) -> p g d e", d=HD), AX.X, ALU.add))
                        ch.step(tt(mix[:], mix[:], resid[:].rearrange("p a (n d) -> p (a n) d", d=HD), ALU.add))
                        t16 = tmp[:, :, 0:HD]
                        norm_groups(nc, v, ch, var, rstd, it * 3 + 3, fx[:], mix[:], t16, stat, G, HD, FEPS)
                        ch.step(tt(fx[:], fx[:], bmid(vec[:, 0, :], G), ALU.mult))
                        tt(fx[:], fx[:], bmid(vec[:, 1, :], G), ALU.add).then_inc(fx_ok, 1)
                        for kind, c in EPI:
                            take(base)
                            if kind == "fturn":
                                give(cp(fxt[0:D, c[0] * P:c[1] * P], psm[0:D, 0:(c[1] - c[0]) * P]))
                            elif kind == "fc1":
                                s_ = slice(c * FB, (c + 1) * FB)
                                if c == 0:
                                    v.wait_ge(free, base + k[0] + 1)
                                    ch.step(ts(pm[:], fxt[0:D], 0.0, None, ALU.not_equal))
                                give(stt(hx1[0:D, s_], psm[0:D, 0:FB], 0.0, pm[:, s_], ALU.max, ALU.mult))
                            elif kind == "fc2":
                                s_ = slice(c * FB, (c + 1) * FB)
                                ch.step(tt(pm[:, s_], psm[0:D, 0:FB], pm[:, s_], ALU.mult))
                                give(tt(pm[:, s_], pm[:, s_], fxt[0:D, s_], ALU.add))
                            else:
                                give(cp(fo[:].rearrange("p (a n) d -> p a (n d)", n=NH)[:, c[0]:c[1], :], psm[:, 0:(c[1] - c[0]) * D].rearrange("p (a d) -> p a d", d=D)))
                        assert k[0] == J
                        v.wait_ge(free, base + k[0] + 1)
                        norm_groups(nc, v, ch, var, rstd, it * 3 + 4, fx[:], fo[:], t16, stat, G, HD, FEPS)
                        ch.step(tt(fx[:], fx[:], bmid(vec[:, 2, :], G), ALU.mult))
                        ch.step(tt(fx[:], fx[:], bmid(vec[:, 3, :], G), ALU.add))
                        fa = fx[:].rearrange("p (a n) d -> p a (n d)", n=NH)
                        for n in range(NH):
                            ch.step(tt(tmp[:, 0:NA, :], fa, bmid(fgw[:, n, :], NA), ALU.mult))
                            ch.step(red(gs[:, 0:NA, n:n + 1], tmp[:, 0:NA, :], AX.X, ALU.add))
                        gg = gs[:, 0:NA, :]
                        ch.step(red(mx[:, 0:NA], gg, AX.X, ALU.max))
                        tt(gg, gg, bcast(mx[:, 0:NA], NH), ALU.subtract).then_inc(logit, 1)
                        v.wait_ge(gate_exp, it + 1)
                        ch.step(red(mx[:, 0:NA], gg, AX.X, ALU.add))
                        ch.step(nc.vector.reciprocal(mx[:, 0:NA], mx[:, 0:NA]))
                        ch.step(tt(gg, gg, bcast(mx[:, 0:NA], NH), ALU.mult))
                        ch.step(tt(fx[:].rearrange("p (a n) d -> p a n d", n=NH), fx[:].rearrange("p (a n) d -> p a n d", n=NH), bcast(gg, HD), ALU.mult))
                        v.wait_ge(stored, it * 32 + 16)
                        tt(res[:], hb[:], fa, ALU.add).then_inc(result, 1)
                        assert ch.n == NDVE, ch.n


SHIFT = 56.0
SUM_MIN = 1e-27
VALUE_MAX = 1e10
ROUNDING = 1.0 + 2.0 ** -5


def stage_ffn_bounded(nc, t, h2d, out, flag_d):
    UB, PB, LAG = 2, 4, 3
    units = score_units(UB, whole_tiles=True)
    NU = len(units)
    qk_d = nc.dram_tensor("qk_parts_b", (B, 3, 2 * P + D, LP), BF16).ap()
    mt_d = nc.dram_tensor("bound_parts", (B, HE, 3, LP), BF16).ap()
    xsrc = lambda b: h2d[b].rearrange("(a p) d -> p a d", p=P)
    with ExitStack() as ctx:
        sb = lambda n, s, d=F32: ctx.enter_context(nc.sbuf_tensor(n, s, d))
        ps = lambda n, s, d=F32: ctx.enter_context(nc.psum_tensor(n, s, d))
        sem = lambda n: ctx.enter_context(nc.semaphore(n))
        ident = sb("b_ident", [P, P])
        blkq = sb("b_blkq", [P, 2, HE])
        blkk = sb("b_blkk", [D, HE])
        wha = sb("b_wha", [NH * HD, D + 1])
        wbd = sb("b_wbd", [NH * HD, 448])
        wall = sb("b_wall", [D + 1, 448])
        fcw = sb("b_fcw", [D + 1, 2, D])
        gw = sb("b_gw", [P, HE * 64])
        gb = sb("b_gb", [P, HE])
        fgw = sb("b_fgw", [P, NH, D])
        vec = sb("b_vec", [P, 4, HD])
        resid = sb("b_resid", [P, NA, D])
        h4 = sb("b_h4", [P, 4 * NA, D])
        hb = sb("b_hb", [P, NA, D])
        xn = sb("b_xn", [P, NA, D])
        tmp = sb("b_tmp", [P, 4 * NA, D])
        stat = sb("b_stat", [P, 4, 4 * NA])
        statx = sb("b_statx", [P, 4, NA])
        mh = sb("b_mh", [P, 4 * NA])
        xt = sb("b_xt", [D + 1, LP])
        qs = sb("b_qs", [P, 3, 2, LP], BF16)
        ks = sb("b_ks", [D, 3, LP], BF16)
        rq = sb("b_rq", [P, 3, FB])
        qop = sb("b_qop", [KM, NH, NE, LP], BF16)
        kop = sb("b_kop", [KM, NH, LP], BF16)
        vop = sb("b_vop", [P, NA, NH, VW])
        msk = sb("b_msk", [P, NA, D])
        kmax = sb("b_kmax", [HE, 4])
        bound = sb("b_bound", [HE, LP])
        mt = sb("b_mt", [HE, 3, LP], BF16)
        good = sb("b_good", [P, 3])
        bad = sb("b_bad", [P, 2])
        flag = sb("b_flag", [P, 1], I32)
        pb = sb("b_pb", [P, PB, UB, QT])
        ofm = sb("b_ofm", [P, 2, QT])
        ot = sb("b_ot", [P, 2, NA, NE, VW])
        on = sb("b_on", [P, NA, NE * HD])
        rec = sb("b_rec", [P, NA, NE])
        lg = sb("b_lg", [P, NA, NE])
        mxh = sb("b_mxh", [P, NA])
        vnext = sb("b_vnext", [P, NA, NH, HD])
        mnext = sb("b_mnext", [P, NA, D])
        hr = sb("b_hr", [P, NA, D])
        mx = sb("b_mx", [P, NA * NH])
        gs = sb("b_gs", [P, NA, NE])
        mix = sb("b_mix", [P, NA * NH, HD])
        fx = sb("b_fx", [P, NA * NH, HD])
        fxt = sb("b_fxt", [D + 1, LP])
        hx1 = sb("b_hx1", [D + 1, LP])
        pm = sb("b_pm", [D, LP])
        fo = sb("b_fo", [P, NA * NH, HD])
        pss = ps("b_pss", [P, 2, UB, QT])
        pso = ps("b_pso", [P, 2, QT])
        psm = ps("b_psm", [P, 2, QT])

        res = sb("b_res", [P, NA, D])
        names = ("weights_loaded", "wbd_zeroed", "resid_loaded", "h_loaded", "h_again", "bank_full", "bank_free", "vector_steps",
                 "variance", "rstd", "parts_ready", "part1", "bound_split", "values_put", "scored", "exped", "masked", "summed",
                 "sums_copied", "logits", "logits_exped", "gate_logits", "gate_exped", "result", "stored", "spilled", "passed",
                 "pool_passed", "sp_passed", "mh_ready", "xn_ready", "fx_ready", "squared_bound", "rooted",
                 "flag_ready", "bad_ready", "flag_done", "const_ready")
        (weights, wbd_zero, r_load, h_load, hr_load, full, free, dve, var, rstd, parts, part1, bound_split, vput, scored, exped, masked,
         summed, acc_free, logit, logit_exp, glogit, gate_exp, result, stored, spilled, passed, pool_passed, sp_passed,
         mh_ok, xn_ok, fx_ok, squared_bound, rooted, flag_ready, bad_ready, flag_ok, const_ok) = (sem("b_" + n) for n in names)
        placed = [sem(f"b_head{n}_placed") for n in range(NH)]
        chunks = [(0, 4), (4, 8), (8, 9)]

        tile_of = lambda q0: q0 // QT
        last_unit = {x: max(u for u, un in enumerate(units) for bank in un for p in bank if tile_of(p[3]) == x) for x in range(3)}
        SPAN = NH * NU
        toks = [(0, 3), (3, 6), (6, 8), (8, 9)]
        PRO = [(25 + i, "turn", c) for i, c in enumerate(chunks)] + [(28 + i, "tok", c) for i, c in enumerate(toks)]
        PRO += [(33 + 3 * x, "feat", (2, x)) for x in range(3)] + [(40 + x, "knorm", x) for x in range(3)]
        for x in range(3):
            PRO += [(43 + 10 * x, "feat", (0, x)), (47 + 10 * x, "feat", (1, x)), (51 + 10 * x, "qnorm", x)]
        EPI = [(s_, "fturn", c) for s_, c in zip((32, 34, 35), chunks)] + [(37 + i, "fc1", i) for i in range(3)]
        EPI += [(s_, "fc2", i) for i, s_ in enumerate((45, 46, 48))] + [(s_, "back", c) for s_, c in zip((50, 52, 54), chunks)]
        done_at = lambda n, x: NU * n + last_unit[x] + LAG
        late = lambda n, x: done_at(n, x) + 1 >= SPAN
        EPI = [(done_at(n, x) + 1 - SPAN, "oturn", (n, x)) for n in range(NH) for x in range(3) if late(n, x)] + EPI
        ATT = [(done_at(n, x) + 1, "oturn", (n, x)) for n in range(NH) for x in range(3) if not late(n, x)]
        FEATS = [c for _, kind, c in PRO if kind == "feat"]
        squares = h4[:].rearrange("p a d -> p (a d)").rearrange("p (s f) -> p s f", f=FB)
        slot = {c: i % 6 for i, c in enumerate(FEATS)}
        GATE, RESCALE = 27, 35
        PUT = (40, 60, 83, 5)
        CHECK, MASK, SPLIT, SQUARED, ROOT = 44, 12, 74, 71, 73
        FXNORM, XNORM, LASTNORM = (13, 18, 23), (15, 19, 22), (56, 64, 67)
        LASTGATE, GATEEXP, FINISH = 69, 74, 79

        def jobs(att, pro, prev):
            at = {}
            for s_, kind, c in sorted(att * ATT + pro * PRO + prev * EPI, key=lambda j: j[0]):
                at.setdefault(s_, []).append((kind, c))
            return at

        J = len(ATT) + len(PRO) + len(EPI)
        JS = 1 + 4 * 6

        def jobs_before(p):
            if isinstance(p, int) and p <= 0:
                return JS + (p + 1) * len(PRO)
            n = JS + 2 * len(PRO) + len(ATT) + (p - 1) * J
            return n - len(PRO) if isinstance(p, int) and p == B else n

        def parity(p):
            return jobs_before(p if isinstance(p, int) else 1) % 2

        def norms_before(p):
            if isinstance(p, int) and p <= 0:
                return 2 + p
            return p * 3 - 1 if isinstance(p, int) and p == B else p * 3

        def periods(eng, run):
            run(-1, False, True, False)
            run(0, True, True, False)
            with eng.Fori(0, B - 2) as it:
                run(it + 1, True, True, True)
            run(B - 1, True, False, True)
            run(B, False, False, True)

        NUB = NH * NU
        dj = [[(c, b) for b, bank in enumerate(u) for (c, j, e, q0, w) in bank if (q0 == P * j if e is not None else j == NA - 1)] for u in units]
        NM = NH * sum(bool(d) for d in dj)
        assert NUB % (2 * PB) in (0, PB) and NUB % 2 == 0 and J % 2 == 0
        order_m = {}
        for u, d in enumerate(dj):
            order_m[u] = sum(bool(x) for x in dj[:u + 1])
        with nc.Block() as block:
            @block.sync
            def _(sp):
                for s_, c in ((exped, 2), (summed, PB), (free, 2), (acc_free, 2), (parts, 3), (stored, 16), (spilled, 16), (result, 1)):
                    sp.sem_inc(s_, c)
                sp.dma_start(ident[:], t["c_ident"]).then_inc(weights, 16)
                sp.dma_start(blkq[:], t["c_blkq"]).then_inc(weights, 16)
                sp.dma_start(blkk[:], t["c_blkk"]).then_inc(weights, 16)
                sp.dma_start(wha[:, 0:D], t["L0_ffn_hl_w"].rearrange("n d h -> (n d) h")).then_inc(weights, 16)
                sp.dma_start(wha[:, D:D + 1], t["L0_ffn_hl_b"].rearrange("n (d o) -> (n d) o", o=1), allow_slow_non_contiguous=True).then_inc(weights, 16)
                sp.dma_start(gw[:], rows(t["L0_ffn_gate_w"].rearrange("n e f -> (n e f)"), P)).then_inc(weights, 16)
                sp.dma_start(gb[:], rows(t["L0_ffn_gate_b"].rearrange("n e -> (n e)"), P)).then_inc(weights, 16)
                sp.dma_start(fgw[:].rearrange("p n d -> p (n d)"), rows(t["L0_ffn_fgate_w"].rearrange("n d -> (n d)"), P)).then_inc(weights, 16)
                for i, n in enumerate(("ln_g", "ln_b", "fnorm_g", "fnorm_b")):
                    sp.dma_start(vec[:, i, :], rows(t["L0_ffn_" + n], P)).then_inc(weights, 16)
                for n in range(4):
                    sp.dma_start(h4[:, NA * n:NA * (n + 1), :], xsrc(n)).then_inc(r_load, 16)
                sp.wait_ge(wbd_zero, 2)
                sp.dma_start(wbd[:, 384:448], t["c_ident"][0:D, 0:D]).then_inc(weights, 16)
                for n in range(NH):
                    r = slice(HD * n, HD * n + HD)
                    o = HD * n
                    sp.dma_start(wbd[r, D * n:D * n + D], t["L0_ffn_wq"][n].rearrange("e o d -> d (e o)"), allow_slow_non_contiguous=True).then_inc(weights, 16)
                    sp.dma_start(wbd[r, 256 + o:272 + o], t["L0_ffn_wk"][n].rearrange("o d -> d o"), allow_slow_non_contiguous=True).then_inc(weights, 16)
                    sp.dma_start(wbd[r, 320 + o:336 + o], t["L0_ffn_wv"][n].rearrange("o d -> d o"), allow_slow_non_contiguous=True).then_inc(weights, 16)
                    for i in range(2):
                        w_, b_ = t[f"L0_ffn_fc{i + 1}_w"], t[f"L0_ffn_fc{i + 1}_b"]
                        sp.dma_start(fcw[r, i, o:o + HD], w_.rearrange("o d -> d o"), allow_slow_non_contiguous=True).then_inc(weights, 16)
                        sp.dma_start(fcw[D:D + 1, i, o:o + HD], rows(b_, 1)).then_inc(weights, 16)

                def run(p, att, pro, prev):
                    c, d = p + 1, p - 1
                    if pro:
                        src = xsrc(c)
                        sp.wait_ge(xn_ok, c + 1)
                        sp.dma_start(hb[:], src).then_inc(h_load, 16)
                    if prev:
                        src = xsrc(d)
                        sp.wait_ge(result, d + 1)
                        sp.dma_start(hr[:], src).then_inc(hr_load, 16)
                    if pro:
                        qk, mt_ = qk_d[c], mt_d[c]
                        sp.wait_ge(parts, c * 9 + 6)
                        sp.sem_inc(sp_passed, 1)
                        sp.dma_start(qk[:, 2 * P:2 * P + D, :].rearrange("t r q -> r t q"), ks[:]).then_inc(spilled, 16)
                        sp.wait_ge(parts, c * 9 + 12)
                        sp.sem_inc(sp_passed, 1)
                        for g in range(2):
                            sp.dma_start(qk[:, P * g:P * g + P, :].rearrange("t r q -> r t q"), qs[:, :, g, :]).then_inc(spilled, 16)
                        sp.wait_ge(bound_split, c + 1)
                        sp.sem_inc(sp_passed, 1)
                        sp.dma_start(mt_, mt[:]).then_inc(spilled, 16)
                        sp.wait_ge(spilled, c * 64 + 80)
                        sp.sem_inc(sp_passed, 1)
                        for n in range(NH):
                            if att:
                                sp.wait_ge(scored, p * NUB + (n + 1) * NU)
                                sp.sem_inc(sp_passed, 1)
                            for i, (qp, kp) in enumerate(zip(TERMS_Q, TERMS_K)):
                                r = slice(HD * i, HD * i + HD)
                                sp.dma_start(qop[r, n], qk[qp, D * n:D * n + D].rearrange("(e o) q -> o e q", o=HD)).then_inc(placed[n], 16)
                                sp.dma_start(kop[r, n], qk[kp, 2 * P + HD * n:2 * P + HD * n + HD]).then_inc(placed[n], 16)
                            sp.dma_start(qop[KT:KM, n], mt_[NE * n:NE * n + NE].rearrange("e i q -> i e q")).then_inc(placed[n], 16)
                    if prev:
                        ores = out[d]
                        sp.wait_ge(result, d + 2)
                        sp.sem_inc(sp_passed, 1)
                        sp.dma_start(ores[0:(NA - 1) * P].rearrange("(a p) d -> p a d", p=P), res[:, 0:NA - 1]).then_inc(stored, 16)
                        sp.dma_start(ores[(NA - 1) * P:L], res[0:LAST, NA - 1]).then_inc(stored, 16)

                periods(sp, run)
                sp.wait_ge(flag_ok, 1)
                sp.dma_start(flag_d, flag[0:1, 0:1]).then_inc(stored, 16)
                sp.wait_ge(stored, 32 * B + 32)

            @block.tensor
            def _(pe):
                k, first = [0], [0]
                bank = lambda: psm[:, (first[0] + k[0]) % 2, :]

                def job(base, ins):
                    ins().then_inc(full, 1)
                    k[0] += 1

                def gate(base, all_out=False):
                    pe.wait_ge(free, base + k[0] + (2 if all_out else 1))

                def turn_rows(src, c, base, rows_=D):
                    gate(base)
                    pe.sem_inc(passed, 1)
                    for a in range(*c):
                        mm = pe.transpose(bank()[0:D, (a - c[0]) * P:(a - c[0] + 1) * P], src[:, a, :], ident[:])
                    job(base, lambda: mm)

                pe.wait_ge(weights, 16 * 41)
                gate(0)
                job(0, lambda: pe.matmul(bank()[0:D + 1, 0:448], wha[:], wbd[:], start=True, stop=True))
                pe.wait_ge(xn_ok, 1)
                for n in range(4):
                    for c in chunks:
                        turn_rows(h4[:, NA * n:NA * (n + 1)], c, 0)
                    for c in chunks:
                        gate(0, c[0] == 0)
                        for a in range(*c):
                            mm = pe.matmul(bank()[:, (a - c[0]) * HD:(a - c[0] + 1) * HD], xt[:, a * P:(a + 1) * P], wall[:, 384 + HD * n:400 + HD * n], start=True, stop=True)
                        job(0, lambda: mm)
                assert k[0] == JS
                pe.wait_ge(const_ok, 2)

                def scores(p, u):
                    n, un = divmod(u, NU)
                    if un == 0:
                        pe.wait_ge(placed[n], (p + 1) * (13 * 16))
                    pe.wait_ge(exped, p * NUB + u + 1)
                    for b, bank in enumerate(units[un]):
                        for col, j, e, q0, w in bank:
                            lhs = kop[:, n, j * P:(j + 1) * P]
                            if e is None:
                                mm = pe.matmul(pss[:, u % 2, b, 0:NE * w], lhs, qop[:, n, :, q0:q0 + w], start=True, stop=True, skip_group_check=True)
                            else:
                                mm = pe.matmul(pss[:, u % 2, b, col:col + w], lhs, qop[:, n, e, q0:q0 + w], start=True, stop=True, skip_group_check=True)
                    mm.then_inc(scored, 1)

                def sums(p, u):
                    n, un = divmod(u, NU)
                    if un == 0:
                        pe.wait_ge(vput, p * NH + n + 1)
                    pe.wait_ge(exped, p * NUB + u + 3)
                    if dj[un]:
                        pe.wait_ge(masked, p * NM + (NM // NH) * n + order_m[un])
                    for b, bank in enumerate(units[un]):
                        for col, j, e, q0, w in bank:
                            x = tile_of(q0)
                            if j == 0 and e in (0, None):
                                pe.wait_ge(acc_free, p * 3 * NH + 3 * n + x + 1)
                            r = P if j < NA - 1 else LAST
                            for ee in range(NE) if e is None else (e,):
                                cc = col + (w * ee if e is None else 0)
                                mm = pe.matmul(pso[VW * ee:VW * (ee + 1), (3 * n + x) % 2, q0 - QT * x:q0 - QT * x + w], vop[0:r, j, n, :], pb[0:r, u % PB, b, cc:cc + w],
                                               start=(j == 0), stop=(q0 == P * j if e is not None else j == NA - 1), skip_group_check=True)
                    mm.then_inc(summed, 1)

                def fill(base, p, kind, c):
                    if kind == "turn":
                        pe.wait_ge(xn_ok, p + 3)
                        turn_rows(xn, c, base)
                        return
                    if kind == "fturn":
                        pe.wait_ge(fx_ok, p)
                        turn_rows(fx[:].rearrange("p (a n) d -> p a (n d)", n=NH), c, base)
                        return
                    if kind == "oturn":
                        n, x = c
                        q = p - late(n, x)
                        pe.wait_ge(acc_free, q * 3 * NH + 3 * n + x + 3)
                        gate(base)
                        c = (4 * x, min(4 * x + 4, NA))
                        for a in range(*c):
                            wd = P if a < NA - 1 else LAST
                            mm = pe.transpose(bank()[0:wd, (a - c[0]) * P:(a - c[0] + 1) * P], ofm[:, (3 * n + x) % 2, (a - c[0]) * P:(a - c[0]) * P + wd], ident[:])
                    elif kind == "tok":
                        gate(base, c[0] == 0)
                        for a in range(*c):
                            mm = pe.matmul(bank()[:, (a - c[0]) * P:(a - c[0] + 1) * P], xt[:, a * P:(a + 1) * P], wall[:, 320:448], start=True, stop=True)
                    elif kind == "feat":
                        g, x = c
                        m = P if g < 2 else D
                        gate(base)
                        mm = pe.matmul(bank()[0:m, 0:FB], wall[:, g * P:g * P + m], xt[:, x * FB:(x + 1) * FB], start=True, stop=True)
                    elif kind == "knorm":
                        gate(base, True)
                        pe.sem_inc(passed, 1)
                        mm = pe.matmul(bank()[0:HE, 0:FB], blkk[:], squares[0:D, slot[2, c], :], start=True, stop=True)
                    elif kind == "qnorm":
                        gate(base, True)
                        pe.matmul(bank()[0:HE, 0:FB], blkq[:, 0, :], squares[:, slot[0, c], :], start=True, stop=False)
                        mm = pe.matmul(bank()[0:HE, 0:FB], blkq[:, 1, :], squares[:, slot[1, c], :], start=False, stop=True)
                    elif kind in ("fc1", "fc2"):
                        gate(base, True)
                        i = int(kind == "fc2")
                        mm = pe.matmul(bank()[0:D, 0:FB], fcw[:, i, :], (hx1 if i else fxt)[:, c * FB:(c + 1) * FB], start=True, stop=True)
                    else:
                        gate(base, True)
                        pe.sem_inc(passed, 1)
                        for a in range(*c):
                            mm = pe.transpose(bank()[:, (a - c[0]) * D:(a - c[0] + 1) * D], pm[:, a * P:(a + 1) * P], ident[0:D, 0:D])
                    job(base, lambda: mm)

                def run(p, att, pro, prev):
                    k[0], first[0] = 0, parity(p)
                    at = jobs(att, pro, prev)
                    for s in range(SPAN):
                        if att:
                            scores(p, s)
                        if s < LAG and prev:
                            sums(p - 1, SPAN - LAG + s)
                        elif s >= LAG and att:
                            sums(p, s - LAG)
                        for kind, c in at.get(s, ()):
                            fill(jobs_before(p), p, kind, c)

                periods(pe, run)

            @block.scalar
            def _(act):
                def run(p, att, pro, prev):
                    for s in range(SPAN):
                        if att:
                            act.wait_ge(scored, p * NUB + s + 1)
                            act.wait_ge(summed, p * NUB + s + 1)
                            un = s % NU
                            w = QT if units[un][0][0][2] is not None else NE * LAST
                            nb = len(units[un])
                            nc.scalar.activation(pb[:, s % PB, 0:nb, 0:w], pss[:, s % 2, 0:nb, 0:w], ACT.Exp, scale=float(HD) ** 0.5).then_inc(exped, 1)
                        if pro and s == ROOT:
                            act.wait_ge(squared_bound, p + 2)
                            nc.scalar.activation(bound[:], bound[:], ACT.Sqrt).then_inc(rooted, 1)
                        h = s - RESCALE + 1
                        if h % NU == 0 and (att if h >= 0 else prev):
                            act.wait_ge(logit, p * NH + h // NU + 1)
                            nc.scalar.activation(lg[:], lg[:], ACT.Exp).then_inc(logit_exp, 1)
                        if prev and s == GATEEXP:
                            act.wait_ge(glogit, p)
                            nc.scalar.activation(gs[:], gs[:], ACT.Exp).then_inc(gate_exp, 1)

                periods(act, run)

            @block.gpsimd
            def _(pool):
                pool.memset(mh[:], -0.5).then_inc(mh_ok, 1)
                pool.wait_ge(mh_ok, 1)
                pool.wait_ge(var, 1)
                pool.tensor_tensor(stat[:, 3], stat[:, 2], mh[:], ALU.pow).then_inc(rstd, 1)

                def root(c, st, n):
                    pool.wait_ge(var, c)
                    pool.tensor_tensor(st[:, 3, 0:n], st[:, 2, 0:n], mh[:, 0:n], ALU.pow).then_inc(rstd, 1)

                def split(p, i, g, x):
                    m = P if g < 2 else D
                    dst = (lambda p_: qs[:, p_, g, x * FB:(x + 1) * FB]) if g < 2 else (lambda p_: ks[:, p_, x * FB:(x + 1) * FB])
                    pool.tensor_copy(dst(1), rq[0:m, i % 3, :]).then_inc(part1, 1)
                    pool.wait_ge(part1, (p + 1) * 9 + i + 1)
                    pool.tensor_tensor(dst(2), rq[0:m, i % 3, :], dst(1), ALU.subtract).then_inc(parts, 1)
                    pool.wait_ge(parts, (p + 1) * 9 + i + 4)
                    pool.sem_inc(pool_passed, 1)

                def mask(p, u):
                    un = u % NU
                    if not dj[un]:
                        return
                    pool.wait_ge(exped, p * NUB + u + 3)
                    pool.sem_inc(pool_passed, 1)
                    cols = {}
                    for c, b in dj[un]:
                        cols.setdefault(c, []).append(b)
                    for c, bs in sorted(cols.items()):
                        if units[un][bs[0]][0][2] is None:
                            v_ = pb[0:LAST, u % PB, bs[0], 0:NE * LAST].rearrange("p (e q) -> p e q", e=NE)
                            pat = [[0, NE], [1, LAST]]
                        else:
                            v_ = pb[:, u % PB, bs[0]:bs[-1] + 1, c:c + P]
                            pat = [[0, len(bs)], [1, P]]
                        ins = pool.affine_select(out=v_, in_=v_, compare_op=ALU.is_ge, fill=0.0, base=0, pattern=pat, channel_multiplier=-1)
                    ins.then_inc(masked, 1)

                def run(p, att, pro, prev):
                    at, k, roots, i = jobs(att, pro, prev), 0, 0, 0
                    for s in range(SPAN):
                        if att:
                            mask(p, s)
                        for when, st, n, on_ in ((FXNORM, stat, NA * NH, prev), (XNORM, statx, NA, pro), (LASTNORM, stat, NA * NH, prev)):
                            if s == when[1] and on_:
                                roots += 1
                                root(norms_before(p) + roots, st, n)
                        for kind, c in at.get(s, ()):
                            k += 1
                            if kind == "feat":
                                pool.wait_ge(free, jobs_before(p) + k + 2)
                                pool.sem_inc(pool_passed, 1)
                                split(p, i, *c)
                                i += 1

                periods(pool, run)
                pool.wait_ge(flag_ready, 1)
                pool.partition_all_reduce(bad[:, 1:2], bad[:, 0:1], channels=P, reduce_op=RMAX).then_inc(bad_ready, 1)

            @block.vector
            def _(v):
                tt, ts, stt, cp = nc.vector.tensor_tensor, nc.vector.tensor_scalar, nc.vector.scalar_tensor_tensor, nc.vector.tensor_copy
                red = nc.vector.tensor_reduce
                k, first = [0], [0]
                bank = lambda: psm[:, (first[0] + k[0]) % 2, :]
                nc.vector.memset(wbd[:], 0.0).then_inc(wbd_zero, 1)
                nc.vector.memset(fcw[:], 0.0).then_inc(wbd_zero, 1)
                ch = Chain(v, dve)
                ch.step(nc.vector.memset(xt[D:D + 1], 1.0))
                ch.step(nc.vector.memset(fxt[D:D + 1], 1.0))
                ch.step(nc.vector.memset(hx1[D:D + 1], 1.0))
                ch.step(nc.vector.memset(vop[:], 0.0))
                ch.step(nc.vector.memset(vop[:, :, :, HD:HD + 1], 1.0))
                ch.step(nc.vector.memset(ot[:], 1.0))
                nc.vector.memset(kop[KT:KM], -1.0).then_inc(const_ok, 1)
                nc.vector.memset(good[:], 1.0).then_inc(const_ok, 1)

                def take(base):
                    v.wait_ge(full, base + k[0] + 1)

                def give(ins):
                    ins.then_inc(free, 1)
                    k[0] += 1

                take(0)
                give(cp(wall[:], bank()[0:D + 1, 0:448]))
                v.wait_ge(r_load, 64)
                norm_groups(nc, v, ch, var, rstd, 1, h4[:], h4[:], tmp[:], stat, 4 * NA, D, EPS)
                ch.wait()
                cp(stat[:, 0, 0:1], stat[:, 1, 0:1]).then_inc(xn_ok, 1)
                for n in range(4):
                    for c in chunks:
                        take(0)
                        give(cp(xt[0:D, c[0] * P:c[1] * P], bank()[0:D, 0:(c[1] - c[0]) * P]))
                    for c in chunks:
                        take(0)
                        give(cp(resid[:, c[0]:c[1], HD * n:HD * n + HD], bank()[:, 0:(c[1] - c[0]) * HD].rearrange("p (a d) -> p a d", d=HD)))
                assert k[0] == JS
                v.wait_ge(free, JS + 2)
                FULL_STEPS = 157

                def wellformed(src):
                    ch.step(red(good[:, 1:2], src, AX.X, ALU.min))
                    ch.step(tt(good[:, 0:1], good[:, 0:1], good[:, 1:2], ALU.min))

                def empty(p, base, kind, c):
                    if kind == "oturn":
                        n, x = c
                        w = QT if x < 2 else LAST
                        take(base)
                        a = (4 * x, min(4 * x + 4, NA))
                        dst = ot[:, n % 2].rearrange("p a e w -> p a (e w)")
                        if x < 2:
                            give(cp(dst[:, a[0]:a[1], :], bank().rearrange("p (a w) -> p a w", w=P)))
                        else:
                            give(cp(dst[0:LAST, NA - 1, :], bank()[0:LAST, 0:P]))
                        return
                    take(base)
                    if kind == "turn":
                        give(cp(xt[0:D, c[0] * P:c[1] * P], bank()[0:D, 0:(c[1] - c[0]) * P]))
                    elif kind == "tok":
                        pv = bank().rearrange("p (a s x) -> p a s x", s=2, x=D)[:, 0:c[1] - c[0]]
                        ch.done(cp(vnext[:, c[0]:c[1]], pv[:, :, 0, :].rearrange("p a (n d) -> p a n d", d=HD)))
                        give(ts(mnext[:, c[0]:c[1], :], pv[:, :, 1, :], 0.0, None, ALU.not_equal))
                    elif kind == "knorm":
                        give(red(kmax[:, c:c + 1], bank()[0:HE, 0:FB], AX.X, ALU.max))
                        if c == 2:
                            v.wait_ge(free, base + k[0] + 2)
                            ch.step(red(kmax[:, 3:4], kmax[:, 0:3], AX.X, ALU.max))
                    elif kind == "qnorm":
                        give(ts(bound[:, c * FB:(c + 1) * FB], bank()[0:HE, 0:FB], kmax[:, 3:4], ROUNDING, ALU.mult, ALU.mult))
                    elif kind == "feat":
                        g, x = c
                        i = FEATS.index(c)
                        m = P if g < 2 else D
                        p0 = qs[:, 0, g, x * FB:(x + 1) * FB] if g < 2 else ks[:, 0, x * FB:(x + 1) * FB]
                        if i == 0:
                            v.wait_ge(spilled, (p + 1) * 64 + 16)
                        ch.step(cp(p0, bank()[0:m, 0:FB]))
                        ch.step(tt(squares[0:m, slot[c], :], p0, p0, ALU.mult))
                        v.wait_ge(parts, (p + 1) * 9 + i + 1)
                        give(tt(rq[0:m, i % 3, :], bank()[0:m, 0:FB], p0, ALU.subtract))
                    elif kind == "fturn":
                        give(cp(fxt[0:D, c[0] * P:c[1] * P], bank()[0:D, 0:(c[1] - c[0]) * P]))
                    elif kind == "fc1":
                        s_ = slice(c * FB, (c + 1) * FB)
                        if c == 0:
                            v.wait_ge(free, base + k[0] + 2)
                            ch.step(ts(pm[:], fxt[0:D], 0.0, None, ALU.not_equal))
                        give(stt(hx1[0:D, s_], bank()[0:D, 0:FB], 0.0, pm[:, s_], ALU.max, ALU.mult))
                    elif kind == "fc2":
                        s_ = slice(c * FB, (c + 1) * FB)
                        ch.step(tt(pm[:, s_], bank()[0:D, 0:FB], pm[:, s_], ALU.mult))
                        give(tt(pm[:, s_], pm[:, s_], fxt[0:D, s_], ALU.add))
                    else:
                        give(cp(fo[:].rearrange("p (a n) d -> p a (n d)", n=NH)[:, c[0]:c[1], :], bank()[:, 0:(c[1] - c[0]) * D].rearrange("p (a d) -> p a d", d=D)))

                onv = on[:].rearrange("p a (e d) -> p a e d", d=HD)
                th = tmp[:, 0:NA, :]
                mixh = mix[:].rearrange("p (a n) d -> p a n d", n=NH)

                def head_outputs(n):
                    o = ot[:, n % 2]
                    ch.step(ts(lg[:], o[:, :, :, HD], SUM_MIN, None, ALU.is_ge))
                    wellformed(lg[:].rearrange("p a e -> p (a e)"))
                    ch.step(nc.vector.reciprocal(rec[:], o[:, :, :, HD]))
                    ch.step(tt(onv, o[:, :, :, 0:HD], bcast(rec[:], HD), ALU.mult))
                    ch.step(tt(onv, onv, bmid(msk[:, :, HD * n:HD * n + HD], NE), ALU.mult))

                def head_logits(n, e):
                    g0 = (n * NE + e) * D
                    ch.step(tt(th, on[:], bmid(gw[:, g0:g0 + D], NA), ALU.mult))
                    ch.step(red(lg[:, :, e:e + 1], th, AX.X, ALU.add))
                    if e == NE - 1:
                        ch.step(tt(lg[:], lg[:], bmid(gb[:, NE * n:NE * n + NE], NA), ALU.add))
                        ch.step(red(mxh[:], lg[:], AX.X, ALU.max))
                        tt(lg[:], lg[:], bcast(mxh[:], NE), ALU.subtract).then_inc(logit, 1)

                def head_mix(p, n):
                    v.wait_ge(logit_exp, p * NH + n + 1)
                    ch.step(red(mxh[:], lg[:], AX.X, ALU.add))
                    ch.step(nc.vector.reciprocal(mxh[:], mxh[:]))
                    ch.step(tt(lg[:], lg[:], bcast(mxh[:], NE), ALU.mult))
                    ch.step(tt(th.rearrange("p a (e d) -> p a e d", d=HD), onv, bcast(lg[:], HD), ALU.mult))
                    ch.step(red(rec4, th.rearrange("p a (e d) -> p a d e", d=HD), AX.X, ALU.add))
                    ch.step(tt(mixh[:, :, n, :], rec4, resid[:, :, HD * n:HD * n + HD], ALU.add))

                rec4 = tmp[:, 2 * NA:3 * NA, 0:HD]
                t16 = tmp[:, :, 0:HD]
                fa = fx[:].rearrange("p (a n) d -> p a (n d)", n=NH)
                G = NA * NH

                def variance(src, sq, st, n, d, eps):
                    ch.step(red(st[:, 0, 0:n], src, AX.X, ALU.add))
                    ch.step(ts(st[:, 1, 0:n], st[:, 0, 0:n], -1.0 / d, None, ALU.mult))
                    ch.step(tt(src, src, bcast(st[:, 1, 0:n], d), ALU.add))
                    ch.step(tt(sq, src, src, ALU.mult))
                    ch.step(red(st[:, 0, 0:n], sq, AX.X, ALU.add))
                    ts(st[:, 2, 0:n], st[:, 0, 0:n], 1.0 / d, eps, ALU.mult, ALU.add).then_inc(var, 1)

                def put_values(n):
                    cp(vop[:, :, n, 0:HD], vnext[:, :, n, :]).then_inc(vput, 1)

                def run(p, att, pro, prev):
                    k[0], first[0] = 0, parity(p)
                    base = jobs_before(p)
                    roots0 = norms_before(p)
                    at = jobs(att, pro, prev)
                    for s in range(SPAN):
                        for n in range(NH):
                            for x in range(3):
                                over = done_at(n, x) >= SPAN
                                if s == done_at(n, x) % SPAN and (prev if over else att):
                                    w = QT if x < 2 else LAST
                                    v.wait_ge(summed, (p - over) * NUB + n * NU + last_unit[x] + 1 + PB)
                                    cp(ofm[:, (3 * n + x) % 2, 0:w], pso[:, (3 * n + x) % 2, 0:w]).then_inc(acc_free, 1)
                        for kind, c in at.get(s, ()):
                            empty(p, base, kind, c)
                        for n in range(NH):
                            over = NU * n + GATE >= SPAN
                            if prev if over else att:
                                e = s - (NU * n + GATE) % SPAN
                                if e == 0:
                                    v.wait_ge(free, base + k[0] + 2)
                                    head_outputs(n)
                                if 0 < e <= NE:
                                    head_logits(n, e - 1)
                                if s == (NU * n + RESCALE) % SPAN:
                                    head_mix(p - over, n)
                        if att and s == MASK:
                            ch.step(cp(msk[:], mnext[:]))
                        if prev and s == FXNORM[0]:
                            variance(mix[:], t16, stat, G, HD, FEPS)
                        if prev and s == FXNORM[2]:
                            v.wait_ge(rstd, roots0 + 1)
                            ch.step(tt(fx[:], mix[:], bcast(stat[:, 3], HD), ALU.mult))
                            ch.step(tt(fx[:], fx[:], bmid(vec[:, 0, :], G), ALU.mult))
                            tt(fx[:], fx[:], bmid(vec[:, 1, :], G), ALU.add).then_inc(fx_ok, 1)
                        if s == PUT[NH - 1] and prev and att:
                            put_values(NH - 1)
                        if pro and s == XNORM[0]:
                            v.wait_ge(h_load, (p + 2) * 16)
                            variance(hb[:], tmp[:, 3 * NA:, :], statx, NA, D, EPS)
                        if pro and s == XNORM[2]:
                            v.wait_ge(rstd, roots0 + 1 + prev)
                            tt(xn[:], hb[:], bcast(statx[:, 3], D), ALU.mult).then_inc(xn_ok, 1)
                        if pro:
                            if s in PUT[:NH - 1]:
                                put_values(PUT.index(s))
                            if s == PUT[NH - 2] + 1 and not att:
                                put_values(NH - 1)
                            if s == CHECK:
                                vals = tmp[:, 0:NA, :]
                                ch.step(tt(vals, vnext[:].rearrange("p a n d -> p a (n d)"), vnext[:].rearrange("p a n d -> p a (n d)"), ALU.mult))
                                ch.step(ts(vals, vals, VALUE_MAX ** 2, None, ALU.is_le))
                                wellformed(vals.rearrange("p a d -> p (a d)"))
                            if s == SQUARED:
                                v.wait_ge(free, base + k[0] + 2)
                                tt(bound[0:1, 0:1], bound[0:1, 0:1], bound[0:1, 0:1], ALU.max).then_inc(squared_bound, 1)
                            if s == SPLIT:
                                v.wait_ge(rooted, p + 2)
                                ch.step(ts(bound[:], bound[:], -SHIFT / float(HD) ** 0.5, None, ALU.add))
                            if s == SPLIT + 1:
                                ch.step(cp(mt[:, 0, :], bound[:]))
                                ch.step(tt(bound[:], bound[:], mt[:, 0, :], ALU.subtract))
                            if s == SPLIT + 2:
                                ch.step(cp(mt[:, 1, :], bound[:]))
                                tt(mt[:, 2, :], bound[:], mt[:, 1, :], ALU.subtract).then_inc(bound_split, 1)
                        if not prev:
                            continue
                        if s == LASTNORM[0]:
                            v.wait_ge(free, base + k[0] + 2)
                            variance(fo[:], t16, stat, G, HD, FEPS)
                        if s == LASTNORM[2]:
                            v.wait_ge(rstd, roots0 + 2 + pro)
                            ch.step(tt(fx[:], fo[:], bcast(stat[:, 3], HD), ALU.mult))
                        if s == LASTNORM[2] + 1:
                            ch.step(tt(fx[:], fx[:], bmid(vec[:, 2, :], G), ALU.mult))
                            ch.step(tt(fx[:], fx[:], bmid(vec[:, 3, :], G), ALU.add))
                        if LASTGATE <= s < LASTGATE + NH:
                            n = s - LASTGATE
                            ch.step(tt(tmp[:, 0:NA, :], fa, bmid(fgw[:, n, :], NA), ALU.mult))
                            ch.step(red(gs[:, :, n:n + 1], tmp[:, 0:NA, :], AX.X, ALU.add))
                        if s == LASTGATE + NH - 1:
                            ch.step(red(mx[:, 0:NA], gs[:], AX.X, ALU.max))
                            tt(gs[:], gs[:], bcast(mx[:, 0:NA], NH), ALU.subtract).then_inc(glogit, 1)
                        if s == FINISH:
                            v.wait_ge(gate_exp, p)
                            ch.step(red(mx[:, 0:NA], gs[:], AX.X, ALU.add))
                            ch.step(nc.vector.reciprocal(mx[:, 0:NA], mx[:, 0:NA]))
                            ch.step(tt(gs[:], gs[:], bcast(mx[:, 0:NA], NH), ALU.mult))
                            ch.step(tt(fx[:].rearrange("p (a n) d -> p a n d", n=NH), fx[:].rearrange("p (a n) d -> p a n d", n=NH), bcast(gs[:], HD), ALU.mult))
                            v.wait_ge(hr_load, p * 16)
                            v.wait_ge(stored, (p - 1) * 32 + 16)
                            tt(res[:], hr[:], fa, ALU.add).then_inc(result, 1)

                run(-1, False, True, False)
                run(0, True, True, False)
                before = ch.n
                with v.Fori(0, B - 2) as it:
                    ch = Chain(v, dve, it * FULL_STEPS + before)
                    run(it + 1, True, True, True)
                    assert ch.n == FULL_STEPS, ch.n
                ch = Chain(v, dve, before + (B - 2) * FULL_STEPS)
                run(B - 1, True, False, True)
                run(B, False, False, True)
                ts(bad[:, 0:1], good[:, 0:1], -1.0, 1.0, ALU.mult, ALU.add).then_inc(flag_ready, 1)
                v.wait_ge(bad_ready, 1)
                cp(flag[:], bad[:, 1:2]).then_inc(flag_ok, 1)


def consts():
    t = np.arange(PATCH)[None, :]
    f = np.arange(F)[:, None]
    w = 2 * np.pi * f * t / PATCH
    k = np.arange(KC * P) * (np.arange(KC * P) < KH)
    tan = np.tan(np.pi * k / L)
    both = np.concatenate([tan, -tan])
    m = (np.arange(KH)[:, None] * (L - 1 - np.arange(L))[None, :]) % L
    wt = np.where(np.arange(KH) == 0, 0.5, 1.0)[:, None] / L
    half = np.repeat([[1.0, 0.0, -1.0, 0.0], [-1.0, -1.0, 0.0, 0.0]], D, 0)
    heads = np.arange(P) // (P // 8)
    c = {
        "c_blkq": (heads[:, None, None] + 8 * np.arange(2)[None, :, None]) == np.arange(16),
        "c_blkk": (np.arange(D) // 16)[:, None] == np.arange(16) // 4,
        "c_dft": np.concatenate([np.cos(w), -np.sin(w)], 0) / np.sqrt(PATCH),
        "c_ident": np.eye(P),
        "c_fold": np.concatenate([np.eye(D), np.eye(D)], 0),
        "c_tanrow": both,
        "c_tancol": both.reshape(2 * KC, P).T,
        "c_halves": half,
        "c_cos": wt * np.cos(2 * np.pi * m / L),
        "c_sin": -wt * np.sin(2 * np.pi * m / L),
    }
    return {k: np.ascontiguousarray(v.astype(np.float32)) for k, v in c.items()}


def kernel(**inputs):
    import numpy as _np
    import concourse.bacc as _bacc
    from concourse import mybir as _mybir
    from concourse.bass_utils import run_bass_kernel_spmd as _run

    nc = _bacc.Bacc("TRN2", target_bir_lowering=False, num_devices=1)
    arrays, aps = {}, {}
    for name, a in {**inputs, **consts()}.items():
        a = _np.ascontiguousarray(a)
        arrays["in_" + name] = a
        aps[name] = nc.dram_tensor("in_" + name, a.shape, _mybir.dt.from_np(a.dtype), kind="ExternalInput").ap()
    out = nc.dram_tensor("out", (B, L, D), F32, kind="ExternalOutput").ap()
    h1 = nc.dram_tensor("h1", (B, LP, D), F32).ap()
    taps = nc.dram_tensor("taps", (D, KREV), F32).ap()
    h2 = nc.dram_tensor("h2", (B, LP, D), F32).ap()
    stage_embed(nc, aps, h1)
    stage_taps(nc, aps, taps)
    stage_ssm(nc, aps, h1, taps, h2)
    retry = nc.dram_tensor("retry", (1, 1), I32).ap()
    stage_ffn_bounded(nc, aps, h2, out, retry)
    stage_ffn_exact(nc, aps, h2, out, retry)
    r = _run(nc, [arrays], core_ids=[0])
    return r.results[0]["out"]
```
